# Optimizing a Trainium2 kernel written in Bass

```python
import numpy as np
import jax
import jax.numpy as jnp

def _softmax(x, axis=-1):
    return jax.nn.softmax(x, axis=axis)

def _gelu(x):
    return jax.nn.gelu(x, approximate=True)

def _silu(x):
    return jax.nn.silu(x)

def _sigmoid(x):
    return jax.nn.sigmoid(x)

def _layernorm(x, axis=-1, eps=1e-05):
    m = jnp.mean(x, axis=axis, keepdims=True)
    v = jnp.var(x, axis=axis, keepdims=True)
    return (x - m) / jnp.sqrt(v + eps)

def _scatter_add(tgt, idx, src, axis=0):
    return tgt.at[idx].add(src)

def _segment_sum(src, seg, n):
    return jax.ops.segment_sum(src, seg, n)
kernel_name = 'mk_flamingo_gated_d2_seqx_r4_235144'

def setup_inputs(seed: int=0):
    np.random.seed(seed)
    _w = jnp.asarray

    def _rec_inputs():
        import jax
        import jax.numpy as jnp
        _rk = jax.random.key(seed)
        x = -0.0002928 + 1 * jax.random.normal(jax.random.fold_in(_rk, 1), (2, 1024, 256), jnp.float32)
        _lenS = 1024 - jax.random.randint(jax.random.fold_in(_rk, 7), (2,), 0, max(1, 1024 // 4) + 1, jnp.int32)
        _lenS2 = 64 - jax.random.randint(jax.random.fold_in(_rk, 8), (2,), 0, max(1, 64 // 4) + 1, jnp.int32)
        _ctx_512P = jax.random.normal(jax.random.fold_in(_rk, 11), (2, 16, 128), jnp.float32)
        _ctx_512c = jax.random.dirichlet(jax.random.fold_in(_rk, 511), 0.3 * jnp.ones((16,), jnp.float32), (2, 64))
        _ctx_512t = jnp.einsum('bsk,bkd->bsd', _ctx_512c, _ctx_512P)
        _ctx_512t = _ctx_512t * jax.lax.rsqrt(jnp.mean(jnp.square(_ctx_512t)) + 1e-12) * 0.953939
        ctx_512 = 0.00222621 + 0.99962 * (_ctx_512t + 0.3 * jax.random.normal(jax.random.fold_in(_rk, 611), (2, 64, 128), jnp.float32))
        _g = jax.random.normal(jax.random.fold_in(_rk, 9001), (2, 2), jnp.float32)
        _g = jnp.sign(_g) * jnp.maximum(jnp.abs(_g), 1.0) + (_g == 0) * 1.0
        g_xattn = _g[0]
        g_ffn = _g[1]
        return (x, ctx_512, g_xattn, g_ffn)
    x, ctx_512, g_xattn, g_ffn = _rec_inputs()

    def _L0_xattn_setup():
        import jax, jax.numpy as jnp
        import numpy as np
        H, D, C1, C2, S, M, B, W = (16, 32, 256, 128, 512, 128, 2, 4)

        def _ln(x, g, b):
            m = jnp.mean(x, -1, keepdims=True)
            v = jnp.var(x, -1, keepdims=True)
            return (x - m) * jax.lax.rsqrt(v + 1e-05) * g + b

        def _mha(x, y, wq, wk, wv, li1_w, li1_b, lnx_g, lnx_b, lny_g, lny_b, ln3_g, ln3_b, li2_w, li2_b, li3_w, li3_b, causal):
            xn = _ln(x, lnx_g, lnx_b)
            yn = _ln(y, lny_g, lny_b)
            q = jnp.einsum('bsc,hcd->bhsd', xn, wq)
            k = jnp.einsum('btc,hcd->bhtd', yn, wk)
            v = jnp.einsum('btc,hcd->bhtd', yn, wv)
            a = jax.nn.softmax(jnp.einsum('bhsd,bhtd->bhst', q, k) * D ** (-0.5), axis=-1)
            if causal:
                s, t = (a.shape[-2], a.shape[-1])
                mask = (jnp.arange(t)[None, :] > jnp.arange(s)[:, None]).astype(a.dtype)
                a = a * mask
            o = jnp.einsum('bhst,bhtd->bhsd', a, v)
            o = o.transpose(0, 2, 1, 3).reshape(x.shape[0], x.shape[1], H * D)
            x_out = x + o @ li1_w + li1_b
            h = jax.nn.gelu(_ln(x_out, ln3_g, ln3_b) @ li2_w + li2_b, approximate=False)
            return x_out + h @ li3_w + li3_b
        key = jax.random.key(seed)
        ks = iter(jax.random.split(key, 64))

        def w(shape, scale=0.02):
            return jax.random.normal(next(ks), shape, jnp.float32) * scale
        inp = {'xx': jax.random.normal(next(ks), (B, S, C1), jnp.float32), 'ee': jax.random.normal(next(ks), (B, M, C2), jnp.float32), 'ln1_g': jnp.ones(C1, jnp.float32), 'ln1_b': jnp.zeros(C1, jnp.float32), 'ln2_g': jnp.ones(C1, jnp.float32), 'ln2_b': jnp.zeros(C1, jnp.float32)}
        for pfx, cy in (('a1', C1), ('a2', C2)):
            inp[pfx + '_wq'] = w((H, C1, D))
            inp[pfx + '_wk'] = w((H, cy, D))
            inp[pfx + '_wv'] = w((H, cy, D))
            inp[pfx + '_li1_w'] = w((H * D, C1))
            inp[pfx + '_li1_b'] = jnp.zeros(C1, jnp.float32)
            inp[pfx + '_lnx_g'] = jnp.ones(C1, jnp.float32)
            inp[pfx + '_lnx_b'] = jnp.zeros(C1, jnp.float32)
            inp[pfx + '_lny_g'] = jnp.ones(cy, jnp.float32)
            inp[pfx + '_lny_b'] = jnp.zeros(cy, jnp.float32)
            inp[pfx + '_ln3_g'] = jnp.ones(C1, jnp.float32)
            inp[pfx + '_ln3_b'] = jnp.zeros(C1, jnp.float32)
            inp[pfx + '_li2_w'] = w((C1, C1 * W))
            inp[pfx + '_li2_b'] = jnp.zeros(C1 * W, jnp.float32)
            inp[pfx + '_li3_w'] = w((C1 * W, C1))
            inp[pfx + '_li3_b'] = jnp.zeros(C1, jnp.float32)
        inp['training'] = 0
        return inp
    _L0_xattn_all = _L0_xattn_setup()
    _L0_xattn_in = {k: v for k, v in _L0_xattn_all.items() if k in ('ln1_g', 'ln1_b', 'ln2_g', 'ln2_b', 'a1_wq', 'a1_wk', 'a1_wv', 'a1_li1_w', 'a1_li1_b', 'a1_lnx_g', 'a1_lnx_b', 'a1_lny_g', 'a1_lny_b', 'a1_ln3_g', 'a1_ln3_b', 'a1_li2_w', 'a1_li2_b', 'a1_li3_w', 'a1_li3_b', 'a2_wq', 'a2_wk', 'a2_wv', 'a2_li1_w', 'a2_li1_b', 'a2_lnx_g', 'a2_lnx_b', 'a2_lny_g', 'a2_lny_b', 'a2_ln3_g', 'a2_ln3_b', 'a2_li2_w', 'a2_li2_b', 'a2_li3_w', 'a2_li3_b')}
    del _L0_xattn_all

    def _L0_ffn_setup():
        import jax, jax.numpy as jnp
        import numpy as np
        DIM = 256
        DEPTH = 2
        HEADS = 8
        DIM_HEAD = 64
        WINDOW = 128
        INNER = HEADS * DIM_HEAD
        HID = int(DIM * 4 * 2 / 3)
        B, N = (2, 2048)
        QK_SCALE = 8.0

        def shift_token(t):
            t1, t2 = jnp.split(t, 2, axis=-1)
            t2 = jnp.pad(t2, ((0, 0), (1, 0), (0, 0)))[:, :-1]
            return jnp.concatenate([t1, t2], axis=-1)

        def l2norm(t):
            return t / jnp.clip(jnp.linalg.norm(t, axis=-1, keepdims=True), 1e-12)

        def rotate_half(x):
            x1, x2 = jnp.split(x, 2, axis=-1)
            return jnp.concatenate([-x2, x1], axis=-1)

        def rotary_xpos(q, k):
            n = q.shape[-2]
            half_idx = jnp.arange(0, DIM_HEAD, 2, dtype=jnp.float32)
            inv_freq = 1.0 / 10000.0 ** (half_idx / DIM_HEAD)
            t = jnp.arange(n, dtype=jnp.float32)
            freqs = t[:, None] * inv_freq[None, :]
            freqs = jnp.concatenate([freqs, freqs], axis=-1)
            base = (half_idx + 0.4 * DIM_HEAD) / (1.4 * DIM_HEAD)
            power = (t - n // 2) / float(WINDOW // 2)
            scale = base[None, :] ** power[:, None]
            scale = jnp.concatenate([scale, scale], axis=-1)
            cos, sin = (jnp.cos(freqs), jnp.sin(freqs))
            q = q * cos * scale + rotate_half(q) * sin * scale
            k = k * cos / scale + rotate_half(k) * sin / scale
            return (q, k)

        def local_attention(q, k, v):
            b, h, n, d = q.shape
            w = n // WINDOW
            bq = q.reshape(b, h, w, WINDOW, d) * QK_SCALE
            bk = k.reshape(b, h, w, WINDOW, d)
            bv = v.reshape(b, h, w, WINDOW, d)

            def look_around(t):
                p = jnp.pad(t, ((0, 0), (0, 0), (1, 0), (0, 0), (0, 0)))
                return jnp.concatenate([p[:, :, :w], p[:, :, 1:]], axis=3)
            bk, bv = (look_around(bk), look_around(bv))
            bt = jnp.arange(n).reshape(w, WINDOW)
            btp = jnp.pad(bt, ((1, 0), (0, 0)), constant_values=-1)
            btk = jnp.concatenate([btp[:w], btp[1:]], axis=1)
            sim = jnp.einsum('bhwid,bhwjd->bhwij', bq, bk)
            i = bt[:, :, None]
            j = btk[:, None, :]
            mask = (i < j) | (i > j + WINDOW) | (j == -1)
            sim = jnp.where(mask, -jnp.finfo(sim.dtype).max, sim)
            attn = jax.nn.softmax(sim, axis=-1)
            out = jnp.einsum('bhwij,bhwjd->bhwid', attn, bv)
            return out.reshape(b, h, n, d)

        def _layer(x, wqkv, qs, ksc, wo, lg, lb, w1, b1, w2, b2):
            b, n, _ = x.shape
            h = shift_token(x)
            qkv = h @ wqkv
            q, k, v = jnp.split(qkv, 3, axis=-1)
            to_heads = lambda t: t.reshape(b, n, HEADS, DIM_HEAD).transpose(0, 2, 1, 3)
            q, k, v = (to_heads(q), to_heads(k), to_heads(v))
            q = l2norm(q) * qs
            k = l2norm(k) * ksc
            q, k = rotary_xpos(q, k)
            o = local_attention(q, k, v)
            o = o.transpose(0, 2, 1, 3).reshape(b, n, INNER)
            x = x + o @ wo
            h = shift_token(x)
            mu = h.mean(-1, keepdims=True)
            var = h.var(-1, keepdims=True)
            h = (h - mu) / jnp.sqrt(var + 1e-05) * lg + lb
            h = h @ w1 + b1
            a, g = jnp.split(h, 2, axis=-1)
            h = a * jax.nn.gelu(g, approximate=False)
            x = x + h @ w2 + b2
            return x
        key = jax.random.key(seed)
        ks = jax.random.split(key, 6)
        return {'x': jax.random.normal(ks[0], (B, N, DIM), jnp.float32), 'wqkv': jax.random.normal(ks[1], (DEPTH, DIM, 3 * INNER), jnp.float32) * 0.02, 'q_scale': jnp.ones((DEPTH, DIM_HEAD), jnp.float32), 'k_scale': jnp.ones((DEPTH, DIM_HEAD), jnp.float32), 'wo': jax.random.normal(ks[2], (DEPTH, INNER, DIM), jnp.float32) * 0.02, 'ln_g': jnp.ones((DEPTH, DIM), jnp.float32), 'ln_b': jnp.zeros((DEPTH, DIM), jnp.float32), 'w1': jax.random.normal(ks[3], (DEPTH, DIM, 2 * HID), jnp.float32) * 0.02, 'b1': jnp.zeros((DEPTH, 2 * HID), jnp.float32), 'w2': jax.random.normal(ks[4], (DEPTH, HID, DIM), jnp.float32) * 0.02, 'b2': jnp.zeros((DEPTH, DIM), jnp.float32)}
    _L0_ffn_all = _L0_ffn_setup()
    _L0_ffn_in = {k: v for k, v in _L0_ffn_all.items() if k in ('wqkv', 'q_scale', 'k_scale', 'wo', 'ln_g', 'ln_b', 'w1', 'b1', 'w2', 'b2')}
    del _L0_ffn_all

    def _L1_xattn_setup():
        import jax, jax.numpy as jnp
        import numpy as np
        HEADS = 16
        D_MODEL = 256
        IMG_MODEL = 128
        D_K = D_MODEL // HEADS
        key = jax.random.key(seed)
        ks = jax.random.split(key, 12)
        B, LQ, LKV = (8, 512, 256)
        s_dm = 1.0 / np.sqrt(D_MODEL)
        s_im = 1.0 / np.sqrt(IMG_MODEL)
        return {'q': jax.random.normal(ks[0], (B, LQ, D_MODEL), jnp.float32), 'k': jax.random.normal(ks[1], (B, LKV, IMG_MODEL), jnp.float32), 'v': jax.random.normal(ks[2], (B, LKV, IMG_MODEL), jnp.float32), 'Wq': jax.random.normal(ks[3], (D_MODEL, D_MODEL), jnp.float32) * s_dm, 'bq': jnp.zeros((D_MODEL,), jnp.float32), 'Wk': jax.random.normal(ks[4], (IMG_MODEL, D_MODEL), jnp.float32) * s_im, 'bk': jnp.zeros((D_MODEL,), jnp.float32), 'Wv': jax.random.normal(ks[5], (IMG_MODEL, D_MODEL), jnp.float32) * s_im, 'bv': jnp.zeros((D_MODEL,), jnp.float32), 'Wo': jax.random.normal(ks[6], (D_MODEL, D_MODEL), jnp.float32) * s_dm, 'bo': jnp.zeros((D_MODEL,), jnp.float32)}
    _L1_xattn_all = _L1_xattn_setup()
    _L1_xattn_in = {k: v for k, v in _L1_xattn_all.items() if k in ('Wq', 'bq', 'Wk', 'bk', 'Wv', 'bv', 'Wo', 'bo')}
    del _L1_xattn_all

    def _L1_ffn_setup():
        import jax, jax.numpy as jnp
        import numpy as np
        import math
        B, L, D = (4, 1024, 256)
        F = 1024
        E = 16
        CAP_FACTOR = 1.0
        EPS = 1e-05
        key = jax.random.key(seed)
        ks = jax.random.split(key, 8)
        std = 0.02
        return {'x': jax.random.normal(ks[0], (B, L, D), dtype=jnp.float32), 'norm_weight': jnp.ones((D,), dtype=jnp.float32), 'router_weight': jax.random.normal(ks[1], (E, D), dtype=jnp.float32) * std, 'router_bias': jnp.zeros((E,), dtype=jnp.float32), 'fc1_weight': jax.random.normal(ks[2], (E, F, D), dtype=jnp.float32) * std, 'fc1_bias': jnp.zeros((E, F), dtype=jnp.float32), 'fc2_weight': jax.random.normal(ks[3], (E, D, F), dtype=jnp.float32) * std, 'fc2_bias': jnp.zeros((E, D), dtype=jnp.float32)}
    _L1_ffn_all = _L1_ffn_setup()
    _L1_ffn_in = {k: v for k, v in _L1_ffn_all.items() if k in ('norm_weight', 'router_weight', 'router_bias', 'fc1_weight', 'fc1_bias', 'fc2_weight', 'fc2_bias')}
    del _L1_ffn_all
    return {'x': x, 'ctx_512': ctx_512, 'g_xattn': g_xattn, 'g_ffn': g_ffn, 'L0_xattn_ln1_g': _L0_xattn_in['ln1_g'], 'L0_xattn_ln1_b': _L0_xattn_in['ln1_b'], 'L0_xattn_ln2_g': _L0_xattn_in['ln2_g'], 'L0_xattn_ln2_b': _L0_xattn_in['ln2_b'], 'L0_xattn_a1_wq': _L0_xattn_in['a1_wq'], 'L0_xattn_a1_wk': _L0_xattn_in['a1_wk'], 'L0_xattn_a1_wv': _L0_xattn_in['a1_wv'], 'L0_xattn_a1_li1_w': _L0_xattn_in['a1_li1_w'], 'L0_xattn_a1_li1_b': _L0_xattn_in['a1_li1_b'], 'L0_xattn_a1_lnx_g': _L0_xattn_in['a1_lnx_g'], 'L0_xattn_a1_lnx_b': _L0_xattn_in['a1_lnx_b'], 'L0_xattn_a1_lny_g': _L0_xattn_in['a1_lny_g'], 'L0_xattn_a1_lny_b': _L0_xattn_in['a1_lny_b'], 'L0_xattn_a1_ln3_g': _L0_xattn_in['a1_ln3_g'], 'L0_xattn_a1_ln3_b': _L0_xattn_in['a1_ln3_b'], 'L0_xattn_a1_li2_w': _L0_xattn_in['a1_li2_w'], 'L0_xattn_a1_li2_b': _L0_xattn_in['a1_li2_b'], 'L0_xattn_a1_li3_w': _L0_xattn_in['a1_li3_w'], 'L0_xattn_a1_li3_b': _L0_xattn_in['a1_li3_b'], 'L0_xattn_a2_wq': _L0_xattn_in['a2_wq'], 'L0_xattn_a2_wk': _L0_xattn_in['a2_wk'], 'L0_xattn_a2_wv': _L0_xattn_in['a2_wv'], 'L0_xattn_a2_li1_w': _L0_xattn_in['a2_li1_w'], 'L0_xattn_a2_li1_b': _L0_xattn_in['a2_li1_b'], 'L0_xattn_a2_lnx_g': _L0_xattn_in['a2_lnx_g'], 'L0_xattn_a2_lnx_b': _L0_xattn_in['a2_lnx_b'], 'L0_xattn_a2_lny_g': _L0_xattn_in['a2_lny_g'], 'L0_xattn_a2_lny_b': _L0_xattn_in['a2_lny_b'], 'L0_xattn_a2_ln3_g': _L0_xattn_in['a2_ln3_g'], 'L0_xattn_a2_ln3_b': _L0_xattn_in['a2_ln3_b'], 'L0_xattn_a2_li2_w': _L0_xattn_in['a2_li2_w'], 'L0_xattn_a2_li2_b': _L0_xattn_in['a2_li2_b'], 'L0_xattn_a2_li3_w': _L0_xattn_in['a2_li3_w'], 'L0_xattn_a2_li3_b': _L0_xattn_in['a2_li3_b'], 'L0_ffn_wqkv': _L0_ffn_in['wqkv'], 'L0_ffn_q_scale': _L0_ffn_in['q_scale'], 'L0_ffn_k_scale': _L0_ffn_in['k_scale'], 'L0_ffn_wo': _L0_ffn_in['wo'], 'L0_ffn_ln_g': _L0_ffn_in['ln_g'], 'L0_ffn_ln_b': _L0_ffn_in['ln_b'], 'L0_ffn_w1': _L0_ffn_in['w1'], 'L0_ffn_b1': _L0_ffn_in['b1'], 'L0_ffn_w2': _L0_ffn_in['w2'], 'L0_ffn_b2': _L0_ffn_in['b2'], 'L1_xattn_Wq': _L1_xattn_in['Wq'], 'L1_xattn_bq': _L1_xattn_in['bq'], 'L1_xattn_Wk': _L1_xattn_in['Wk'], 'L1_xattn_bk': _L1_xattn_in['bk'], 'L1_xattn_Wv': _L1_xattn_in['Wv'], 'L1_xattn_bv': _L1_xattn_in['bv'], 'L1_xattn_Wo': _L1_xattn_in['Wo'], 'L1_xattn_bo': _L1_xattn_in['bo'], 'L1_ffn_norm_weight': _L1_ffn_in['norm_weight'], 'L1_ffn_router_weight': _L1_ffn_in['router_weight'], 'L1_ffn_router_bias': _L1_ffn_in['router_bias'], 'L1_ffn_fc1_weight': _L1_ffn_in['fc1_weight'], 'L1_ffn_fc1_bias': _L1_ffn_in['fc1_bias'], 'L1_ffn_fc2_weight': _L1_ffn_in['fc2_weight'], 'L1_ffn_fc2_bias': _L1_ffn_in['fc2_bias']}

def reference(x, ctx_512, g_xattn, g_ffn, L0_xattn_ln1_g, L0_xattn_ln1_b, L0_xattn_ln2_g, L0_xattn_ln2_b, L0_xattn_a1_wq, L0_xattn_a1_wk, L0_xattn_a1_wv, L0_xattn_a1_li1_w, L0_xattn_a1_li1_b, L0_xattn_a1_lnx_g, L0_xattn_a1_lnx_b, L0_xattn_a1_lny_g, L0_xattn_a1_lny_b, L0_xattn_a1_ln3_g, L0_xattn_a1_ln3_b, L0_xattn_a1_li2_w, L0_xattn_a1_li2_b, L0_xattn_a1_li3_w, L0_xattn_a1_li3_b, L0_xattn_a2_wq, L0_xattn_a2_wk, L0_xattn_a2_wv, L0_xattn_a2_li1_w, L0_xattn_a2_li1_b, L0_xattn_a2_lnx_g, L0_xattn_a2_lnx_b, L0_xattn_a2_lny_g, L0_xattn_a2_lny_b, L0_xattn_a2_ln3_g, L0_xattn_a2_ln3_b, L0_xattn_a2_li2_w, L0_xattn_a2_li2_b, L0_xattn_a2_li3_w, L0_xattn_a2_li3_b, L0_ffn_wqkv, L0_ffn_q_scale, L0_ffn_k_scale, L0_ffn_wo, L0_ffn_ln_g, L0_ffn_ln_b, L0_ffn_w1, L0_ffn_b1, L0_ffn_w2, L0_ffn_b2, L1_xattn_Wq, L1_xattn_bq, L1_xattn_Wk, L1_xattn_bk, L1_xattn_Wv, L1_xattn_bv, L1_xattn_Wo, L1_xattn_bo, L1_ffn_norm_weight, L1_ffn_router_weight, L1_ffn_router_bias, L1_ffn_fc1_weight, L1_ffn_fc1_bias, L1_ffn_fc2_weight, L1_ffn_fc2_bias):
    import jax
    import jax.numpy as jnp

    def _L0_xattn_ref(xx, ee, ln1_g, ln1_b, ln2_g, ln2_b, a1_wq, a1_wk, a1_wv, a1_li1_w, a1_li1_b, a1_lnx_g, a1_lnx_b, a1_lny_g, a1_lny_b, a1_ln3_g, a1_ln3_b, a1_li2_w, a1_li2_b, a1_li3_w, a1_li3_b, a2_wq, a2_wk, a2_wv, a2_li1_w, a2_li1_b, a2_lnx_g, a2_lnx_b, a2_lny_g, a2_lny_b, a2_ln3_g, a2_ln3_b, a2_li2_w, a2_li2_b, a2_li3_w, a2_li3_b, training):
        import jax, jax.numpy as jnp
        import numpy as np
        H, D, C1, C2, S, M, B, W = (16, 32, 256, 128, 512, 128, 2, 4)

        def _ln(x, g, b):
            m = jnp.mean(x, -1, keepdims=True)
            v = jnp.var(x, -1, keepdims=True)
            return (x - m) * jax.lax.rsqrt(v + 1e-05) * g + b

        def _mha(x, y, wq, wk, wv, li1_w, li1_b, lnx_g, lnx_b, lny_g, lny_b, ln3_g, ln3_b, li2_w, li2_b, li3_w, li3_b, causal):
            xn = _ln(x, lnx_g, lnx_b)
            yn = _ln(y, lny_g, lny_b)
            q = jnp.einsum('bsc,hcd->bhsd', xn, wq)
            k = jnp.einsum('btc,hcd->bhtd', yn, wk)
            v = jnp.einsum('btc,hcd->bhtd', yn, wv)
            a = jax.nn.softmax(jnp.einsum('bhsd,bhtd->bhst', q, k) * D ** (-0.5), axis=-1)
            if causal:
                s, t = (a.shape[-2], a.shape[-1])
                mask = (jnp.arange(t)[None, :] > jnp.arange(s)[:, None]).astype(a.dtype)
                a = a * mask
            o = jnp.einsum('bhst,bhtd->bhsd', a, v)
            o = o.transpose(0, 2, 1, 3).reshape(x.shape[0], x.shape[1], H * D)
            x_out = x + o @ li1_w + li1_b
            h = jax.nn.gelu(_ln(x_out, ln3_g, ln3_b) @ li2_w + li2_b, approximate=False)
            return x_out + h @ li3_w + li3_b
        x = _ln(xx, ln1_g, ln1_b)
        x = x + _mha(x, x, a1_wq, a1_wk, a1_wv, a1_li1_w, a1_li1_b, a1_lnx_g, a1_lnx_b, a1_lny_g, a1_lny_b, a1_ln3_g, a1_ln3_b, a1_li2_w, a1_li2_b, a1_li3_w, a1_li3_b, causal=True)
        x = _ln(x, ln2_g, ln2_b)
        return x + _mha(x, ee, a2_wq, a2_wk, a2_wv, a2_li1_w, a2_li1_b, a2_lnx_g, a2_lnx_b, a2_lny_g, a2_lny_b, a2_ln3_g, a2_ln3_b, a2_li2_w, a2_li2_b, a2_li3_w, a2_li3_b, causal=False)

    def _L0_ffn_ref(x, wqkv, q_scale, k_scale, wo, ln_g, ln_b, w1, b1, w2, b2):
        import jax, jax.numpy as jnp
        import numpy as np
        DIM = 256
        DEPTH = 2
        HEADS = 8
        DIM_HEAD = 64
        WINDOW = 128
        INNER = HEADS * DIM_HEAD
        HID = int(DIM * 4 * 2 / 3)
        B, N = (2, 2048)
        QK_SCALE = 8.0

        def shift_token(t):
            t1, t2 = jnp.split(t, 2, axis=-1)
            t2 = jnp.pad(t2, ((0, 0), (1, 0), (0, 0)))[:, :-1]
            return jnp.concatenate([t1, t2], axis=-1)

        def l2norm(t):
            return t / jnp.clip(jnp.linalg.norm(t, axis=-1, keepdims=True), 1e-12)

        def rotate_half(x):
            x1, x2 = jnp.split(x, 2, axis=-1)
            return jnp.concatenate([-x2, x1], axis=-1)

        def rotary_xpos(q, k):
            n = q.shape[-2]
            half_idx = jnp.arange(0, DIM_HEAD, 2, dtype=jnp.float32)
            inv_freq = 1.0 / 10000.0 ** (half_idx / DIM_HEAD)
            t = jnp.arange(n, dtype=jnp.float32)
            freqs = t[:, None] * inv_freq[None, :]
            freqs = jnp.concatenate([freqs, freqs], axis=-1)
            base = (half_idx + 0.4 * DIM_HEAD) / (1.4 * DIM_HEAD)
            power = (t - n // 2) / float(WINDOW // 2)
            scale = base[None, :] ** power[:, None]
            scale = jnp.concatenate([scale, scale], axis=-1)
            cos, sin = (jnp.cos(freqs), jnp.sin(freqs))
            q = q * cos * scale + rotate_half(q) * sin * scale
            k = k * cos / scale + rotate_half(k) * sin / scale
            return (q, k)

        def local_attention(q, k, v):
            b, h, n, d = q.shape
            w = n // WINDOW
            bq = q.reshape(b, h, w, WINDOW, d) * QK_SCALE
            bk = k.reshape(b, h, w, WINDOW, d)
            bv = v.reshape(b, h, w, WINDOW, d)

            def look_around(t):
                p = jnp.pad(t, ((0, 0), (0, 0), (1, 0), (0, 0), (0, 0)))
                return jnp.concatenate([p[:, :, :w], p[:, :, 1:]], axis=3)
            bk, bv = (look_around(bk), look_around(bv))
            bt = jnp.arange(n).reshape(w, WINDOW)
            btp = jnp.pad(bt, ((1, 0), (0, 0)), constant_values=-1)
            btk = jnp.concatenate([btp[:w], btp[1:]], axis=1)
            sim = jnp.einsum('bhwid,bhwjd->bhwij', bq, bk)
            i = bt[:, :, None]
            j = btk[:, None, :]
            mask = (i < j) | (i > j + WINDOW) | (j == -1)
            sim = jnp.where(mask, -jnp.finfo(sim.dtype).max, sim)
            attn = jax.nn.softmax(sim, axis=-1)
            out = jnp.einsum('bhwij,bhwjd->bhwid', attn, bv)
            return out.reshape(b, h, n, d)

        def _layer(x, wqkv, qs, ksc, wo, lg, lb, w1, b1, w2, b2):
            b, n, _ = x.shape
            h = shift_token(x)
            qkv = h @ wqkv
            q, k, v = jnp.split(qkv, 3, axis=-1)
            to_heads = lambda t: t.reshape(b, n, HEADS, DIM_HEAD).transpose(0, 2, 1, 3)
            q, k, v = (to_heads(q), to_heads(k), to_heads(v))
            q = l2norm(q) * qs
            k = l2norm(k) * ksc
            q, k = rotary_xpos(q, k)
            o = local_attention(q, k, v)
            o = o.transpose(0, 2, 1, 3).reshape(b, n, INNER)
            x = x + o @ wo
            h = shift_token(x)
            mu = h.mean(-1, keepdims=True)
            var = h.var(-1, keepdims=True)
            h = (h - mu) / jnp.sqrt(var + 1e-05) * lg + lb
            h = h @ w1 + b1
            a, g = jnp.split(h, 2, axis=-1)
            h = a * jax.nn.gelu(g, approximate=False)
            x = x + h @ w2 + b2
            return x
        for l in range(DEPTH):
            x = _layer(x, wqkv[l], q_scale[l], k_scale[l], wo[l], ln_g[l], ln_b[l], w1[l], b1[l], w2[l], b2[l])
        return x

    def _L1_xattn_ref(q, k, v, Wq, bq, Wk, bk, Wv, bv, Wo, bo):
        import jax, jax.numpy as jnp
        import numpy as np
        HEADS = 16
        D_MODEL = 256
        IMG_MODEL = 128
        D_K = D_MODEL // HEADS
        B, LQ, _ = q.shape
        LKV = k.shape[1]
        qh = (q @ Wq + bq).reshape(B, LQ, HEADS, D_K).transpose(0, 2, 1, 3)
        kh = (k @ Wk + bk).reshape(B, LKV, HEADS, D_K).transpose(0, 2, 1, 3)
        vh = (v @ Wv + bv).reshape(B, LKV, HEADS, D_K).transpose(0, 2, 1, 3)
        scale = 1.0 / np.sqrt(D_K)
        scores = jnp.einsum('bhqd,bhkd->bhqk', qh, kh) * scale
        attn = jax.nn.softmax(scores, axis=-1)
        out = jnp.einsum('bhqk,bhkd->bhqd', attn, vh)
        concat = out.transpose(0, 2, 1, 3).reshape(B, LQ, D_MODEL)
        return concat @ Wo + bo

    def _L1_ffn_ref(x, norm_weight, router_weight, router_bias, fc1_weight, fc1_bias, fc2_weight, fc2_bias):
        import jax, jax.numpy as jnp
        import numpy as np
        import math
        B, L, D = (4, 1024, 256)
        F = 1024
        E = 16
        CAP_FACTOR = 1.0
        EPS = 1e-05
        b, l, d = x.shape
        n_tokens = b * l
        n_experts = router_weight.shape[0]
        capacity = max(1, math.ceil(CAP_FACTOR * n_tokens / n_experts))
        top_k = min(capacity, n_tokens)
        xf = x.reshape(n_tokens, d)
        rms = jnp.sqrt(jnp.mean(xf * xf, axis=-1, keepdims=True) + EPS)
        xn = xf / rms * norm_weight
        logits = xn @ router_weight.T + router_bias
        probs = jax.nn.softmax(logits, axis=-1)
        _, idx = jax.lax.top_k(logits.T, top_k)
        xe = xn[idx]
        h = jnp.einsum('ecd,efd->ecf', xe, fc1_weight) + fc1_bias[:, None, :]
        h = jax.nn.gelu(h, approximate=False)
        y = jnp.einsum('ecf,edf->ecd', h, fc2_weight) + fc2_bias[:, None, :]
        gates = jnp.take_along_axis(probs.T, idx, axis=1)
        flat_idx = idx.reshape(-1)
        contrib = (y * gates[:, :, None]).reshape(-1, d)
        output = jnp.zeros((n_tokens, d), dtype=x.dtype).at[flat_idx].add(contrib)
        gate_sums = jnp.zeros((n_tokens, 1), dtype=x.dtype).at[flat_idx].add(gates.reshape(-1, 1))
        assigned = gate_sums > 0
        output = jnp.where(assigned, output / jnp.where(assigned, gate_sums, 1.0), output)
        return output.reshape(b, l, d)
    x = x + jnp.tanh(g_xattn[0]) * _L0_xattn_ref(_layernorm(x, axis=-1), ctx_512, L0_xattn_ln1_g, L0_xattn_ln1_b, L0_xattn_ln2_g, L0_xattn_ln2_b, L0_xattn_a1_wq, L0_xattn_a1_wk, L0_xattn_a1_wv, L0_xattn_a1_li1_w, L0_xattn_a1_li1_b, L0_xattn_a1_lnx_g, L0_xattn_a1_lnx_b, L0_xattn_a1_lny_g, L0_xattn_a1_lny_b, L0_xattn_a1_ln3_g, L0_xattn_a1_ln3_b, L0_xattn_a1_li2_w, L0_xattn_a1_li2_b, L0_xattn_a1_li3_w, L0_xattn_a1_li3_b, L0_xattn_a2_wq, L0_xattn_a2_wk, L0_xattn_a2_wv, L0_xattn_a2_li1_w, L0_xattn_a2_li1_b, L0_xattn_a2_lnx_g, L0_xattn_a2_lnx_b, L0_xattn_a2_lny_g, L0_xattn_a2_lny_b, L0_xattn_a2_ln3_g, L0_xattn_a2_ln3_b, L0_xattn_a2_li2_w, L0_xattn_a2_li2_b, L0_xattn_a2_li3_w, L0_xattn_a2_li3_b, 0)
    x = x + jnp.tanh(g_ffn[0]) * _L0_ffn_ref(_layernorm(x, axis=-1), L0_ffn_wqkv, L0_ffn_q_scale, L0_ffn_k_scale, L0_ffn_wo, L0_ffn_ln_g, L0_ffn_ln_b, L0_ffn_w1, L0_ffn_b1, L0_ffn_w2, L0_ffn_b2)
    x = x + jnp.tanh(g_xattn[1]) * _L1_xattn_ref(_layernorm(x, axis=-1), ctx_512, ctx_512, L1_xattn_Wq, L1_xattn_bq, L1_xattn_Wk, L1_xattn_bk, L1_xattn_Wv, L1_xattn_bv, L1_xattn_Wo, L1_xattn_bo)
    x = x + jnp.tanh(g_ffn[1]) * _L1_ffn_ref(_layernorm(x, axis=-1), L1_ffn_norm_weight, L1_ffn_router_weight, L1_ffn_router_bias, L1_ffn_fc1_weight, L1_ffn_fc1_bias, L1_ffn_fc2_weight, L1_ffn_fc2_bias)
    return x

_drawn_inputs = setup_inputs


def setup_inputs(seed=0):
    import zlib

    import numpy as np

    out = dict(_drawn_inputs(seed))
    spreads = {'g_ffn': (-1.0, 0.6),
     'L0_xattn_ln1_g': (1.0, 0.2),
     'L0_xattn_ln1_b': (0.0, 0.1),
     'L0_xattn_ln2_g': (1.0, 0.2),
     'L0_xattn_ln2_b': (0.0, 0.1),
     'L0_xattn_a1_li1_b': (0.0, 0.28),
     'L0_xattn_a1_lnx_g': (1.0, 0.6),
     'L0_xattn_a1_lnx_b': (0.0, 0.8),
     'L0_xattn_a1_lny_g': (1.0, 0.6),
     'L0_xattn_a1_lny_b': (0.0, 0.8),
     'L0_xattn_a1_ln3_g': (1.0, 0.6),
     'L0_xattn_a1_ln3_b': (0.0, 2.0),
     'L0_xattn_a1_li2_b': (0.0, 0.727),
     'L0_xattn_a1_li3_b': (0.0, 0.272),
     'L0_xattn_a2_li1_b': (0.0, 0.29),
     'L0_xattn_a2_lnx_g': (1.0, 0.6),
     'L0_xattn_a2_lnx_b': (0.0, 0.8),
     'L0_xattn_a2_lny_g': (1.0, 0.6),
     'L0_xattn_a2_lny_b': (0.0, 0.8),
     'L0_xattn_a2_ln3_g': (1.0, 0.6),
     'L0_xattn_a2_ln3_b': (0.0, 0.8),
     'L0_xattn_a2_li2_b': (0.0, 0.692),
     'L0_xattn_a2_li3_b': (0.0, 0.282),
     'L0_ffn_q_scale': (1.0, 0.6),
     'L0_ffn_k_scale': (1.0, 0.6),
     'L0_ffn_ln_g': (1.0, 0.6),
     'L0_ffn_ln_b': (0.0, 0.8),
     'L0_ffn_b1': (0.0, 0.8),
     'L0_ffn_b2': (0.0, 0.1),
     'L1_xattn_bq': (0.0, 0.58),
     'L1_xattn_bk': (0.0, 2.0),
     'L1_xattn_bv': (0.0, 0.1),
     'L1_xattn_bo': (0.0, 0.1),
     'L1_ffn_norm_weight': (1.0, 0.557),
     'L1_ffn_router_bias': (0.0, 2.0),
     'L1_ffn_fc1_bias': (0.0, 0.712),
     'L1_ffn_fc2_bias': (0.0, 0.277)}
    factors = {'L0_xattn_a1_wq': 8.0,
     'L0_xattn_a1_wk': 8.0,
     'L0_xattn_a1_wv': 8.0,
     'L0_xattn_a1_li1_w': 8.0,
     'L0_xattn_a2_wq': 8.0,
     'L0_xattn_a2_wk': 8.0,
     'L0_xattn_a2_wv': 3.159,
     'L0_xattn_a2_li1_w': 3.314,
     'L0_ffn_wqkv': 3.354,
     'L0_ffn_wo': 3.222}
    for name, (base, spread) in spreads.items():
        noise = np.random.default_rng([zlib.crc32(name.encode()), seed]).standard_normal(out[name].shape)
        drawn = base * np.exp(spread * noise) if base else spread * noise
        out[name] = jnp.asarray(drawn.astype(out[name].dtype))
    for name, factor in factors.items():
        out[name] = (out[name] * factor).astype(out[name].dtype)
    return out
```

```python
def build(nc, io, out):
    import concourse.bass as bass
    from concourse import mybir
    from collections import namedtuple
    from contextlib import ExitStack

    F32, F16, BF16, U32, I32 = mybir.dt.float32, mybir.dt.float16, mybir.dt.bfloat16, mybir.dt.uint32, mybir.dt.int32
    ALU = mybir.AluOpType
    ACT = mybir.ActivationFunctionType
    X = mybir.AxisListType.X

    P = 128
    B, N, D = io["x"].shape
    TOK = B * N
    NT = TOK // P
    TPB = N // P
    J = 4
    G = NT // J
    GW = J * P
    KD = D // P
    EPS = 1e-5

    def signals(phase, names):
        sems = []
        for n in names.split():
            sems.append(nc.alloc_semaphore(f"{phase}_{n.lstrip('@')}"))
            if not n.startswith("@"):
                nc.gpsimd.sem_inc(sems[-1], 1)
        nc.all_engine_barrier()
        return namedtuple("Signals", names.replace("@", ""))(*sems)

    def release(s):
        nc.clear_and_free_semaphores(list(s))

    stack = ExitStack()

    def sb(name, shape, dt=F32, where=None):
        return (where or stack).enter_context(nc.sbuf_tensor(name, shape, dt))

    def ps(name, shape, where, dt=F32):
        return where.enter_context(nc.psum_tensor(name, shape, dt))

    def chan(ap):
        return ap.rearrange("(k p) -> p k", p=P)

    def rows(ap):
        return ap.unsqueeze(0).to_broadcast([P, ap.shape[0]])

    with stack:
        xres = sb("xres", [P, NT, D])
        x0res = sb("x0res", [P, NT, D])
        ident = sb("ident", [P, P])
        eps = sb("eps", [P, 1])
        gate = sb("gate", [P, 4])
        stats = sb("stats", [P, J, 6])
        moments = sb("moments", [P, J, 2])
        std = sb("std", [P, J])
        rstd = sb("rstd", [P, J])

        waited = nc.alloc_semaphore("waited")

        LN = "ln_stats ln_moments ln_std ln_rstd ln_out"

        def wait_apart(e, signal, value):
            e.wait_ge(signal, value)
            e.sem_inc(waited, 1)

        def ln_vector(e, s, n, src, dst):
            for j in range(J):
                e.bn_stats(stats[:, j, :], src(j)).then_inc(s.ln_stats, 1)
            wait_apart(e, s.ln_stats, 1 + n * J + J)
            for j in range(J):
                e.bn_aggr(moments[:, j, :], stats[:, j, :]).then_inc(s.ln_moments, 1)
            e.wait_ge(s.ln_std, 1 + n + 1)
            e.reciprocal(rstd[:, :], std[:, :]).then_inc(s.ln_rstd, 1)
            e.wait_ge(s.ln_rstd, 1 + n + 1)
            e.wait_ge(s.ln_moments, 1 + n * J + J)
            for j in range(J):
                e.tensor_scalar(dst(j), src(j), moments[:, j, 0:1], rstd[:, j:j + 1],
                                ALU.subtract, ALU.mult).then_inc(s.ln_out, 1)

        def ln_scalar(a, s, n):
            a.wait_ge(s.ln_moments, 1 + n * J + J)
            a.activation(std[:, :], moments[:, :, 1], ACT.Sqrt, bias=eps[:, 0:1]).then_inc(s.ln_std, 1)

        s = signals("setup", "x_in gates_in zeroed ident_done eps_done tanh_done")
        with nc.Block() as block:
            @block.sync
            def _(sp):
                for q in range(4):
                    sp.dma_start(xres[:, q * J:(q + 1) * J, :],
                                 io["x"].rearrange("b (t p) c -> p (b t) c", p=P)[:, q * J:(q + 1) * J, :]).then_inc(s.x_in, 16)
                sp.dma_start(gate[:, 0:2], rows(io["g_xattn"])).then_inc(s.gates_in, 16)
                sp.dma_start(gate[:, 2:4], rows(io["g_ffn"])).then_inc(s.gates_in, 16)
                sp.wait_ge(s.x_in, 1 + 64)

            @block.gpsimd
            def _(pool):
                pool.memset(ident[:], 0.0).then_inc(s.zeroed, 1)
                wait_apart(pool, s.zeroed, 1 + 1)
                pool.affine_select(out=ident[:], in_=ident[:], compare_op=ALU.not_equal, fill=1.0,
                                   base=0, pattern=[[-1, P]], channel_multiplier=1).then_inc(s.ident_done, 1)
                pool.memset(eps[:], EPS).then_inc(s.eps_done, 1)

            @block.scalar
            def _(act):
                act.wait_ge(s.gates_in, 1 + 32)
                act.activation(gate[:], gate[:], ACT.Tanh).then_inc(s.tanh_done, 1)
        release(s)

        H1, _, D1 = io["L0_xattn_a1_wq"].shape
        HD = H1 * D1
        MC = HD // P
        SCALE1 = D1 ** -0.5
        q_parts = nc.dram_tensor("q_parts", (2, B * HD, N), F16).ap()
        k_parts = nc.dram_tensor("k_parts", (2, B * HD, N), F16).ap()

        attn = ExitStack()
        ores = sb("ores", [P, B * H1, TPB, D1])
        vctx = ExitStack()
        vres = sb("vres", [P, B * H1, TPB, D1], F32, vctx)

        with ExitStack() as c:
            wq = sb("a1wq", [P, KD, HD], F32, c)
            wk = sb("a1wk", [P, KD, HD], F32, c)
            wv = sb("a1wv", [P, KD, HD], F32, c)
            ln1g = sb("ln1g", [P, D], F32, c)
            ln1b = sb("ln1b", [P, D], F32, c)
            aff = sb("aff", [P, 4, KD], F32, c)
            h = sb("h", [P, J, D], F32, c)
            z = sb("z", [P, J, D], F32, c)
            xT = sb("xT", [P, KD, GW], F32, c)
            yT = sb("yT", [P, KD, GW], F32, c)
            parts = sb("parts", [P, 2, 2, MC, GW], F16, c)
            zps = [ps(f"zps{k}", [P, GW], c) for k in range(KD)]
            pps = [ps(f"pps{k}", [P, GW], c) for k in range(6)]

            s = signals("a1p", LN + " w_in aff_in scaled x0_done z_done zT_done affine_done "
                        "proj_done hi_done proj_free_dve v_done parts_out")
            with nc.Block() as block:
                @block.sync
                def _(sp):
                    with nc.allow_non_contiguous_dma(reason="small vectors by channel"):
                        for n, name in enumerate(["lnx_g", "lnx_b", "lny_g", "lny_b"]):
                            sp.dma_start(aff[:, n, :], chan(io["L0_xattn_a1_" + name])).then_inc(s.aff_in, 16)
                    sp.dma_start(ln1g[:], rows(io["L0_xattn_ln1_g"])).then_inc(s.aff_in, 16)
                    sp.dma_start(ln1b[:], rows(io["L0_xattn_ln1_b"])).then_inc(s.aff_in, 16)
                    for w, name in ((wq, "wq"), (wk, "wk"), (wv, "wv")):
                        sp.dma_start(w[:], io["a1_" + name + "_flat"].rearrange("(k p) n -> p k n", p=P)).then_inc(s.w_in, 16)
                    with sp.Fori(0, B, 1) as b:
                        for gg in range(G // B):
                            g = b * (G // B) + gg
                            sp.wait_ge(s.hi_done, 1 + g * 8 + 8)
                            sp.wait_ge(s.proj_free_dve, 1 + g * 8 + 8)
                            for t, dst in enumerate((q_parts, k_parts)):
                                for part in range(2):
                                    sp.dma_start(dst[part, bass.ts(b, HD), gg * GW:(gg + 1) * GW].rearrange("(m p) n -> p m n", p=P),
                                                 parts[:, t, part, :, :]).then_inc(s.parts_out, 16)
                    sp.wait_ge(s.parts_out, 1 + 64 * G)

                @block.vector
                def _(dve):
                    with dve.Fori(0, B, 1) as b:
                        for gg in range(G // B):
                            g = b * (G // B) + gg
                            dve.wait_ge(s.ln_out, 1 + g * 12)
                            ln_vector(dve, s, g * 3, lambda j: xres[:, g * J + j, :], lambda j: h[:, j, :])
                            dve.wait_ge(s.ln_out, 1 + g * 12 + 4)
                            dve.wait_ge(s.zT_done, 1 + g)
                            dve.wait_ge(s.x0_done, 1 + g * J)
                            ln_vector(dve, s, g * 3 + 1, lambda j: h[:, j, :], lambda j: z[:, j, :])
                            dve.wait_ge(s.x0_done, 1 + g * J + J)
                            ln_vector(dve, s, g * 3 + 2, lambda j: x0res[:, g * J + j, :], lambda j: h[:, j, :])
                            dve.wait_ge(s.parts_out, 1 + g * 64)
                            for n in range(8):
                                t, m = n // 4, n % 4
                                dve.wait_ge(s.hi_done, 1 + g * 8 + n + 1)
                                dve.scalar_tensor_tensor(out=parts[:, t, 1, m, :], in0=pps[n % 6][:],
                                                         scalar=SCALE1 if t == 0 else 1.0, in1=parts[:, t, 0, m, :],
                                                         op0=ALU.mult, op1=ALU.subtract).then_inc(s.proj_free_dve, 1)
                            for n in range(8, 12):
                                dve.wait_ge(s.proj_done, 1 + g * 12 + n + 1)
                                dve.tensor_copy(vres[:, bass.ts(b, H1), gg * J + n - 8, :],
                                                    pps[n % 6][:].rearrange("p (h d) -> p h d", h=H1)).then_inc(s.v_done, 1)

                @block.gpsimd
                def _(pool):
                    wait_apart(pool, s.aff_in, 1 + 96)
                    with pool.Fori(0, B, 1) as b:
                        for gg in range(G // B):
                            g = b * (G // B) + gg
                            for j in range(J):
                                wait_apart(pool, s.ln_out, 1 + g * 12 + 5 + j)
                                pool.tensor_tensor(z[:, j, :], z[:, j, :], ln1g[:], ALU.mult).then_inc(s.scaled, 1)
                                wait_apart(pool, s.scaled, 1 + g * J + j + 1)
                                pool.tensor_tensor(x0res[:, g * J + j, :], z[:, j, :], ln1b[:], ALU.add).then_inc(s.x0_done, 1)

                @block.tensor
                def _(pe):
                    pe.wait_ge(s.w_in, 1 + 48)
                    with pe.Fori(0, B, 1) as b:
                        for gg in range(G // B):
                            g = b * (G // B) + gg
                            pe.wait_ge(s.ln_out, 1 + g * 12 + 12)
                            pe.wait_ge(s.affine_done, 1 + g * 4)
                            for k in range(KD):
                                for j in range(J):
                                    mm = pe.transpose(zps[k][:, j * P:(j + 1) * P], h[:, j, k * P:(k + 1) * P], ident[:])
                            mm.then_inc(s.zT_done, 1)
                            pe.wait_ge(s.affine_done, 1 + g * 4 + 4)
                            for n in range(12):
                                if n < 4:
                                    pe.wait_ge(s.proj_free_dve if n < 2 else s.v_done, 1 + g * (8 if n < 2 else 4))
                                elif n < 6:
                                    pe.wait_ge(s.v_done, 1 + g * 4)
                                else:
                                    pe.wait_ge(s.proj_free_dve, 1 + g * 8 + n - 5)
                                for k in range(KD):
                                    if n < 4:
                                        mm = pe.matmul(pps[n % 6][:], wq[:, k, n * P:(n + 1) * P], xT[:, k, :],
                                                       start=(k == 0), stop=(k == KD - 1))
                                    elif n < 8:
                                        mm = pe.matmul(pps[n % 6][:], wk[:, k, (n - 4) * P:(n - 3) * P], yT[:, k, :],
                                                       start=(k == 0), stop=(k == KD - 1))
                                    else:
                                        mm = pe.matmul(pps[n % 6][:], yT[:, k, (n - 8) * P:(n - 7) * P], wv[:, k, :],
                                                       start=(k == 0), stop=(k == KD - 1))
                                mm.then_inc(s.proj_done, 1)

                @block.scalar
                def _(act):
                    act.wait_ge(s.aff_in, 1 + 96)
                    with act.Fori(0, B, 1) as b:
                        for gg in range(G // B):
                            g = b * (G // B) + gg
                            for n in range(3):
                                ln_scalar(act, s, g * 3 + n)
                            act.wait_ge(s.zT_done, 1 + g + 1)
                            act.wait_ge(s.proj_done, 1 + g * 12)
                            for k in range(KD):
                                act.activation(xT[:, k, :], zps[k][:], ACT.Identity, bias=aff[:, 1, k:k + 1],
                                               scale=aff[:, 0, k:k + 1]).then_inc(s.affine_done, 1)
                                act.activation(yT[:, k, :], zps[k][:], ACT.Identity, bias=aff[:, 3, k:k + 1],
                                               scale=aff[:, 2, k:k + 1]).then_inc(s.affine_done, 1)
                            act.wait_ge(s.parts_out, 1 + g * 64)
                            for n in range(8):
                                t, m = n // 4, n % 4
                                act.wait_ge(s.proj_done, 1 + g * 12 + n + 1)
                                act.activation(parts[:, t, 0, m, :], pps[n % 6][:], ACT.Copy,
                                               scale=SCALE1 if t == 0 else 1.0).then_inc(s.hi_done, 1)
            release(s)

        with ExitStack() as c:
            qs = sb("qs", [P, 2, N], F16, c)
            ks = sb("ks", [P, 2, N], F16, c)
            prob = sb("prob", [P, 4, N], F32, c)
            probT = sb("probT", [P, 3, GW], F32, c)
            after = sb("after", [P, P], F32, c)
            negmax = sb("negmax", [P, 2, TPB], F32, c)
            rowsum = sb("rowsum", [P, 2, TPB], F32, c)
            rinv = sb("rinv", [P, 2, TPB], F32, c)
            sps = [ps(f"sps{i}", [P, N], c) for i in range(2)]
            tps = [ps(f"tps{i}", [P, GW], c) for i in range(2)]
            opsum = [ps(f"ops{i}", [P, 512], c) for i in range(2)]

            one_head = [(i, t0, min(4, TPB - t0), "act" if t0 > i or i == 3 else "dve")
                        for i in range(TPB) for t0 in range(i, TPB, 4)]
            groups = [(u * TPB + i, t0, cnt, who) for u in range(2) for (i, t0, cnt, who) in one_head]
            NG = len(groups)
            TILES = 2 * TPB
            LEAD = 3
            PAIRS = B * H1 // 2

            def evacuated(who, k):
                return sum(g[3] == who for g in groups[:k])

            def turned_before(n):
                return sum(g[0] < n for g in groups)

            ALL_ACT, ALL_DVE = evacuated("act", NG), evacuated("dve", NG)
            s = signals("a1a", "in_even in_odd cleared after_ready scores max_done exp_done masked "
                        "turned evac_act evac_dve used rinv_done out_done")
            landed = (s.in_even, s.in_odd)
            with nc.Block() as block:
                @block.sync
                def _(sp):
                    def load(hh, u):
                        for r in range(4):
                            sp.dma_start(qs[32 * r:32 * r + 32, u, :],
                                         q_parts[r // 2, bass.ds(hh * D1, D1), :]).then_inc(landed[u], 16)
                            sp.dma_start(ks[32 * r:32 * r + 32, u, :],
                                         k_parts[r % 2, bass.ds(hh * D1, D1), :]).then_inc(landed[u], 16)

                    load(0, 0)
                    load(1, 1)
                    with sp.Fori(1, PAIRS, 1) as it:
                        for u in range(2):
                            sp.wait_ge(s.scores, 1 + it * TILES - TILES + TPB * (u + 1))
                            load(it * 2 + u, u)

                @block.tensor
                def _(pe):
                    def tile_scores(it, n):
                        u, i = (n // TPB) % 2, n % TPB
                        if i == 0:
                            pe.wait_ge(landed[u], 1 + it * 128 + 128 * (n // TILES + 1))
                        if n >= 2:
                            pe.wait_ge(s.exp_done, 1 + it * TILES + n - 1)
                        for half in range(2):
                            mm = pe.matmul(sps[n % 2][:, half * 512:(half + 1) * 512], qs[:, u, i * P:(i + 1) * P],
                                           ks[:, u, half * 512:(half + 1) * 512], start=True, stop=True)
                        mm.then_inc(s.scores, 1)

                    def turn(it, k):
                        n, t0, cnt, who = groups[k]
                        pe.wait_ge(s.masked, 1 + it * TILES + n + 1)
                        pe.wait_ge(s.evac_act, 1 + it * ALL_ACT + evacuated("act", max(k - 1, 0)))
                        pe.wait_ge(s.evac_dve, 1 + it * ALL_DVE + evacuated("dve", max(k - 1, 0)))
                        for w in range(cnt):
                            mm = pe.transpose(tps[k % 2][:, w * P:(w + 1) * P],
                                              prob[:, n % 4, (t0 + w) * P:(t0 + w + 1) * P], ident[:])
                        mm.then_inc(s.turned, 1)

                    def weigh(it, k):
                        n, t0, cnt, who = groups[k]
                        u, i = n // TPB, n % TPB
                        pe.wait_ge(s.evac_act, 1 + it * ALL_ACT + evacuated("act", k + 1))
                        pe.wait_ge(s.evac_dve, 1 + it * ALL_DVE + evacuated("dve", k + 1))
                        if i == 0 and t0 == 0:
                            pe.wait_ge(s.out_done, 1 + it * 2)
                        for w in range(cnt):
                            mm = pe.matmul(opsum[u][:, i * D1:(i + 1) * D1], probT[:, k % 3, w * P:(w + 1) * P],
                                           vres[:, it * 2 + u, t0 + w, :],
                                           start=(t0 == i and w == 0), stop=(t0 + w == TPB - 1))
                        mm.then_inc(s.used, 1)

                    def pair(it, last):
                        for k in range(NG):
                            n = groups[k][0]
                            if (k == 0 or groups[k - 1][0] != n) and not (last and n + LEAD >= TILES):
                                tile_scores(it, n + LEAD)
                            turn(it, k)
                            if k > 1:
                                weigh(it, k - 2)
                        weigh(it, NG - 2)
                        weigh(it, NG - 1)

                    for n in range(LEAD):
                        tile_scores(0, n)
                    with pe.Fori(0, PAIRS - 1, 1) as it:
                        pair(it, False)
                    pair(PAIRS - 1, True)

                @block.vector
                def _(dve):
                    def row_max(it, n):
                        u, i = (n // TPB) % 2, n % TPB
                        dve.wait_ge(s.scores, 1 + it * TILES + n + 1)
                        dve.tensor_reduce(negmax[:, u, i:i + 1], sps[n % 2][:], X, ALU.max, negate=True).then_inc(s.max_done, 1)

                    def pair(it, last):
                        k = 0
                        for n in range(TILES):
                            u = n // TPB
                            while k < NG and groups[k][0] == n:
                                if groups[k][3] == "dve":
                                    w = groups[k][2] * P
                                    dve.wait_ge(s.turned, 1 + it * NG + k + 1)
                                    dve.wait_ge(s.used, 1 + it * NG + max(k - 2, 0))
                                    dve.tensor_copy(probT[:, k % 3, 0:w], tps[k % 2][:, 0:w]).then_inc(s.evac_dve, 1)
                                k += 1
                            if not (last and n + LEAD >= TILES):
                                row_max(it, n + LEAD)
                            if n % TPB == TPB - 1:
                                dve.wait_ge(s.exp_done, 1 + it * TILES + n + 1)
                                dve.reciprocal(rinv[:, u, :], rowsum[:, u, :]).then_inc(s.rinv_done, 1)
                            if n in (TPB, TILES - 1):
                                u = n // TPB - 1 if n == TPB else 1
                                dve.wait_ge(s.rinv_done, 1 + it * 2 + u + 1)
                                dve.wait_ge(s.used, 1 + it * NG + NG // 2 * (u + 1))
                                dve.tensor_tensor(ores[:, it * 2 + u, :, :],
                                                  opsum[u][:, 0:TPB * D1].rearrange("p (i d) -> p i d", i=TPB),
                                                  rinv[:, u, :].unsqueeze(2).to_broadcast([P, TPB, D1]),
                                                  ALU.mult).then_inc(s.out_done, 1)

                    for n in range(LEAD):
                        row_max(0, n)
                    with dve.Fori(0, PAIRS - 1, 1) as it:
                        pair(it, False)
                    pair(PAIRS - 1, True)

                @block.scalar
                def _(act):
                    def exponent(it, n):
                        u, i = (n // TPB) % 2, n % TPB
                        act.wait_ge(s.max_done, 1 + it * TILES + n + 1)
                        if n >= LEAD:
                            act.wait_ge(s.turned, 1 + it * NG + turned_before(n - 3))
                        if i == 0 and n > 0:
                            act.wait_ge(s.rinv_done, 1 + it * 2 + n // TILES)
                        act.activation(prob[:, n % 4, :], sps[n % 2][:], ACT.Exp, bias=negmax[:, u, i:i + 1],
                                       accum_out=rowsum[:, u, i:i + 1]).then_inc(s.exp_done, 1)

                    def pair(it, last):
                        k = 0
                        for n in range(TILES):
                            while k < NG and groups[k][0] == n:
                                if groups[k][3] == "act":
                                    w = groups[k][2] * P
                                    act.wait_ge(s.turned, 1 + it * NG + k + 1)
                                    act.wait_ge(s.used, 1 + it * NG + max(k - 2, 0))
                                    act.copy(probT[:, k % 3, 0:w], tps[k % 2][:, 0:w]).then_inc(s.evac_act, 1)
                                k += 1
                            if not (last and n + LEAD >= TILES):
                                exponent(it, n + LEAD)

                    for n in range(LEAD):
                        exponent(0, n)
                    with act.Fori(0, PAIRS - 1, 1) as it:
                        pair(it, False)
                    pair(PAIRS - 1, True)

                @block.gpsimd
                def _(pool):
                    pool.memset(after[:], 0.0).then_inc(s.cleared, 1)
                    pool.wait_ge(s.cleared, 1 + 1)
                    pool.affine_select(out=after[:], in_=after[:], compare_op=ALU.is_ge, fill=1.0,
                                       base=0, pattern=[[-1, P]], channel_multiplier=1).then_inc(s.after_ready, 1)
                    wait_apart(pool, s.after_ready, 1 + 1)
                    with pool.Fori(0, PAIRS, 1) as it:
                        for n in range(TILES):
                            i = n % TPB
                            wait_apart(pool, s.exp_done, 1 + it * TILES + n + 1)
                            blk = prob[:, n % 4, i * P:(i + 1) * P]
                            pool.tensor_tensor(blk, blk, after[:], ALU.mult).then_inc(s.masked, 1)
            release(s)
        vctx.close()

        def attention_tail(phase, name, out_tile, finish):
            F = io[name + "li2_w"].shape[1]
            FC = F // P
            OC = HD // P
            with ExitStack() as c:
                w1 = sb(phase + "w1", [P, OC, D], F32, c)
                w2 = sb(phase + "w2", [P, KD, F], F32, c)
                w3 = sb(phase + "w3", [P, FC, D], F32, c)
                b1 = sb(phase + "b1", [P, D], F32, c)
                b3 = sb(phase + "b3", [P, D], F32, c)
                ng = sb(phase + "ng", [P, D], F32, c)
                nb = sb(phase + "nb", [P, D], F32, c)
                b2 = sb(phase + "b2", [P, FC], F32, c)
                aff = sb(phase + "aff", [P, 2, KD], F32, c)
                ost = sb(phase + "ost", [P, J, HD], F32, c)
                oT = sb(phase + "oT", [P, OC, GW], F32, c)
                xb = sb(phase + "xb", [P, J, D], F32, c)
                x1 = sb(phase + "x1", [P, J, D], F32, c)
                x1c = sb(phase + "x1c", [P, J, D], F32, c)
                z = sb(phase + "z", [P, J, D], F32, c)
                zT = sb(phase + "zT", [P, KD, GW], F32, c)
                hT = sb(phase + "hT", [P, FC, GW], F32, c)
                y = sb(phase + "y", [P, J, D], F32, c)
                tps = [ps(f"{phase}tps{i}", [P, GW], c) for i in range(4)]
                p1 = [ps(f"{phase}p1{i}", [P, 2, D], c) for i in range(2)]
                p3 = [ps(f"{phase}p3{i}", [P, 2, D], c) for i in range(2)]
                NLN = 2 if finish == "norm" else 1

                s = signals(phase, LN + " w_in v_in staged base_done oT_dve oT_act oT_turned p1_done x1_done "
                            "zT_turned zT_done h_done gelu_done sum1 sum2 p3_done y_done scaled x_out")
                with nc.Block() as block:
                    @block.sync
                    def _(sp):
                        sp.dma_start(w1[:], io[name + "li1_w"].rearrange("(k p) n -> p k n", p=P)).then_inc(s.w_in, 16)
                        sp.dma_start(w2[:], io[name + "li2_w"].rearrange("(k p) n -> p k n", p=P)).then_inc(s.w_in, 16)
                        sp.dma_start(w3[:], io[name + "li3_w"].rearrange("(k p) n -> p k n", p=P)).then_inc(s.w_in, 16)
                        sp.dma_start(b1[:], rows(io[name + "li1_b"])).then_inc(s.v_in, 16)
                        sp.dma_start(b3[:], rows(io[name + "li3_b"])).then_inc(s.v_in, 16)
                        sp.dma_start(ng[:], rows(io["L0_xattn_ln2_g"])).then_inc(s.v_in, 16)
                        sp.dma_start(nb[:], rows(io["L0_xattn_ln2_b"])).then_inc(s.v_in, 16)
                        with nc.allow_non_contiguous_dma(reason="small vectors by channel"):
                            sp.dma_start(b2[:], chan(io[name + "li2_b"])).then_inc(s.v_in, 16)
                            sp.dma_start(aff[:, 0, :], chan(io[name + "ln3_g"])).then_inc(s.v_in, 16)
                            sp.dma_start(aff[:, 1, :], chan(io[name + "ln3_b"])).then_inc(s.v_in, 16)

                    @block.gpsimd
                    def _(pool):
                        wait_apart(pool, s.v_in, 1 + 112)
                        with pool.Fori(0, B, 1) as b:
                            for gg in range(G // B):
                                g = b * (G // B) + gg
                                wait_apart(pool, s.oT_turned, 1 + g * OC)
                                for j in range(J):
                                    src = out_tile(b, gg * J + j)
                                    dst = ost[:, j, :]
                                    if len(src.shape) == 3:
                                        dst = dst.rearrange("p (h d) -> p h d", h=src.shape[1])
                                    pool.tensor_copy(dst, src).then_inc(s.staged, 1)
                                wait_apart(pool, s.x1_done, 1 + g * 2)
                                for j in range(J):
                                    pool.tensor_tensor(xb[:, j, :], x0res[:, g * J + j, :], b1[:], ALU.add).then_inc(s.base_done, 1)
                                wait_apart(pool, s.x1_done, 1 + g * 2 + 2)
                                wait_apart(pool, s.y_done, 1 + g * 2)
                                for j in range(J):
                                    pool.tensor_tensor(x1c[:, j, :], x1[:, j, :], x0res[:, g * J + j, :], ALU.add).then_inc(s.sum1, 1)
                                for j in range(J):
                                    wait_apart(pool, s.sum1, 1 + g * J + j + 1)
                                    pool.tensor_tensor(x1c[:, j, :], x1c[:, j, :], b3[:], ALU.add).then_inc(s.sum2, 1)
                                if finish == "norm":
                                    for j in range(J):
                                        wait_apart(pool, s.ln_out, 1 + g * 8 + 5 + j)
                                        pool.tensor_tensor(y[:, j, :], y[:, j, :], ng[:], ALU.mult).then_inc(s.scaled, 1)
                                        wait_apart(pool, s.scaled, 1 + g * J + j + 1)
                                        pool.tensor_tensor(x0res[:, g * J + j, :], y[:, j, :], nb[:], ALU.add).then_inc(s.x_out, 1)

                    @block.vector
                    def _(dve):
                        with dve.Fori(0, G, 1) as g:
                            dve.wait_ge(s.p1_done, 1 + g * J)
                            for m in range(2):
                                dve.wait_ge(s.oT_turned, 1 + g * OC + m + 1)
                                dve.tensor_copy(oT[:, m, :], tps[m][:]).then_inc(s.oT_dve, 1)
                            dve.wait_ge(s.base_done, 1 + g * J + J)
                            dve.wait_ge(s.sum1, 1 + g * J)
                            for q in range(2):
                                dve.wait_ge(s.p1_done, 1 + g * J + 2 * q + 2)
                                dve.tensor_tensor(x1[:, 2 * q:2 * q + 2, :], p1[q][:], xb[:, 2 * q:2 * q + 2, :],
                                                  ALU.add).then_inc(s.x1_done, 1)
                            dve.wait_ge(s.x1_done, 1 + g * 2 + 2)
                            dve.wait_ge(s.zT_turned, 1 + g * KD)
                            ln_vector(dve, s, g * NLN, lambda j: x1[:, j, :], lambda j: z[:, j, :])
                            dve.wait_ge(s.sum2, 1 + g * J + J)
                            dve.wait_ge(s.x_out, 1 + g * J)
                            for q in range(2):
                                dve.wait_ge(s.p3_done, 1 + g * J + 2 * q + 2)
                                dve.tensor_tensor(y[:, 2 * q:2 * q + 2, :], p3[q][:], x1c[:, 2 * q:2 * q + 2, :],
                                                  ALU.add).then_inc(s.y_done, 1)
                            dve.wait_ge(s.y_done, 1 + g * 2 + 2)
                            if finish == "norm":
                                ln_vector(dve, s, g * 2 + 1, lambda j: y[:, j, :], lambda j: y[:, j, :])
                            else:
                                for j in range(J):
                                    dve.scalar_tensor_tensor(out=xres[:, g * J + j, :], in0=y[:, j, :], scalar=gate[:, 0:1],
                                                             in1=xres[:, g * J + j, :], op0=ALU.mult,
                                                             op1=ALU.add).then_inc(s.x_out, 1)

                    @block.scalar
                    def _(act):
                        act.wait_ge(s.v_in, 1 + 112)
                        with act.Fori(0, G, 1) as g:
                            act.wait_ge(s.p1_done, 1 + g * J)
                            for m in range(2, 4):
                                act.wait_ge(s.oT_turned, 1 + g * OC + m + 1)
                                act.copy(oT[:, m, :], tps[m][:]).then_inc(s.oT_act, 1)
                            ln_scalar(act, s, g * NLN)
                            act.wait_ge(s.h_done, 1 + g * FC)
                            for k in range(KD):
                                act.wait_ge(s.zT_turned, 1 + g * KD + k + 1)
                                act.activation(zT[:, k, :], tps[k][:], ACT.Identity, bias=aff[:, 1, k:k + 1],
                                               scale=aff[:, 0, k:k + 1]).then_inc(s.zT_done, 1)
                            act.wait_ge(s.p3_done, 1 + g * J)
                            for f in range(FC):
                                act.wait_ge(s.h_done, 1 + g * FC + f + 1)
                                act.activation(hT[:, f, :], tps[2 + f % 2][:], ACT.Gelu,
                                               bias=b2[:, f:f + 1]).then_inc(s.gelu_done, 1)
                            if finish == "norm":
                                ln_scalar(act, s, g * 2 + 1)

                    @block.tensor
                    def _(pe):
                        pe.wait_ge(s.w_in, 1 + 48)
                        with pe.Fori(0, G, 1) as g:
                            pe.wait_ge(s.staged, 1 + g * J + J)
                            pe.wait_ge(s.zT_done, 1 + g * KD)
                            pe.wait_ge(s.gelu_done, 1 + g * FC)
                            for m in range(OC):
                                for j in range(J):
                                    mm = pe.transpose(tps[m][:, j * P:(j + 1) * P], ost[:, j, m * P:(m + 1) * P], ident[:])
                                mm.then_inc(s.oT_turned, 1)
                            pe.wait_ge(s.oT_dve, 1 + g * 2 + 2)
                            pe.wait_ge(s.oT_act, 1 + g * 2 + 2)
                            pe.wait_ge(s.x1_done, 1 + g * 2)
                            for j in range(J):
                                for m in range(OC):
                                    mm = pe.matmul(p1[j // 2][:, j % 2, :], oT[:, m, j * P:(j + 1) * P], w1[:, m, :],
                                                   start=(m == 0), stop=(m == OC - 1))
                                mm.then_inc(s.p1_done, 1)
                            pe.wait_ge(s.ln_out, 1 + g * (J * NLN) + J)
                            for k in range(KD):
                                for j in range(J):
                                    mm = pe.transpose(tps[k][:, j * P:(j + 1) * P], z[:, j, k * P:(k + 1) * P], ident[:])
                                mm.then_inc(s.zT_turned, 1)
                            pe.wait_ge(s.zT_done, 1 + g * KD + KD)
                            for f in range(FC):
                                if f >= 2:
                                    pe.wait_ge(s.gelu_done, 1 + g * FC + f - 1)
                                for k in range(KD):
                                    mm = pe.matmul(tps[2 + f % 2][:], w2[:, k, f * P:(f + 1) * P], zT[:, k, :],
                                                   start=(k == 0), stop=(k == KD - 1))
                                mm.then_inc(s.h_done, 1)
                            pe.wait_ge(s.gelu_done, 1 + g * FC + FC)
                            pe.wait_ge(s.y_done, 1 + g * 2)
                            for j in range(J):
                                for f in range(FC):
                                    mm = pe.matmul(p3[j // 2][:, j % 2, :], hT[:, f, j * P:(j + 1) * P], w3[:, f, :],
                                                   start=(f == 0), stop=(f == FC - 1))
                                mm.then_inc(s.p3_done, 1)
                release(s)

        attention_tail("t1", "L0_xattn_a1_", lambda b, i: ores[:, bass.ts(b, H1), i, :], "norm")


        CT, CD = io["ctx_512"].shape[1:]
        ores_flat = ores[:].rearrange("p h i d -> p (h i d)")

        def cross_attention(phase, H, DK, src, x_affine, y_affine, wq_ap, wk_ap, wv_ap, biases, scale):
            W = H * DK
            MC = W // P
            HQ = P // DK
            NW = HQ * CT
            NP2 = H // 2
            with ExitStack() as c:
                wq = sb(phase + "wq", [P, KD, W], F32, c)
                wk = sb(phase + "wk", [P, W], F32, c)
                wv = sb(phase + "wv", [P, W], F32, c)
                aff = sb(phase + "aff", [P, 2, KD], F32, c)
                yaff = sb(phase + "yaff", [P, 2], F32, c)
                bq = sb(phase + "bq", [P, MC], F32, c)
                bk = sb(phase + "bk", [P, MC], F32, c)
                bv = sb(phase + "bv", [P, W], F32, c)
                y = sb(phase + "y", [P, CD], F32, c)
                yn = sb(phase + "yn", [P, CD], F32, c)
                yT = sb(phase + "yT", [P, P], F32, c)
                ydup = sb(phase + "ydup", [P, B, 2, CT], F32, c)
                hmask = sb(phase + "hmask", [P, HQ], F32, c)
                vmask = sb(phase + "vmask", [P, 2], F32, c)
                kT = sb(phase + "kT", [P, MC, P], F32, c)
                kblk = sb(phase + "kblk", [P, B, MC, HQ, CT], F32, c)
                v = sb(phase + "v", [P, B, W], F32, c)
                vblk = sb(phase + "vblk", [P, B, NP2, 2, DK], F32, c)
                z = sb(phase + "z", [P, J, D], F32, c)
                xT = sb(phase + "xT", [P, KD, GW], F32, c)
                qT = sb(phase + "qT", [P, MC, GW], F32, c)
                nmax = sb(phase + "nmax", [P, 2, H], F32, c)
                rsum = sb(phase + "rsum", [P, 2, H], F32, c)
                rinv = sb(phase + "rinv", [P, 2, H], F32, c)
                prob = sb(phase + "prob", [P, 2, H * CT], F32, c)
                pT = sb(phase + "pT", [P, 2, NP2 * P // 2], F32, c)
                sps = [ps(f"{phase}s{i}", [P, 1024], c) for i in range(2)]
                tps = [ps(f"{phase}t{i}", [P, GW], c) for i in range(2)]
                ops = [ps(f"{phase}o{i}", [P, GW], c) for i in range(2)]

                s = signals(phase + "c", "y_in w_in zeroed hmask_one hmask_done step")
                with nc.Block() as block:
                    @block.sync
                    def _(sp):
                        sp.dma_start(y[:], io["ctx_512"].rearrange("b t c -> (b t) c")).then_inc(s.y_in, 16)
                        sp.dma_start(wk[:], wk_ap).then_inc(s.w_in, 16)
                        sp.dma_start(wv[:], wv_ap).then_inc(s.w_in, 16)
                        sp.dma_start(wq[:], wq_ap.rearrange("(k p) n -> p k n", p=P)).then_inc(s.w_in, 16)
                        with nc.allow_non_contiguous_dma(reason="small vectors by channel"):
                            if x_affine:
                                sp.dma_start(aff[:, 0, :], chan(x_affine[0])).then_inc(s.w_in, 16)
                                sp.dma_start(aff[:, 1, :], chan(x_affine[1])).then_inc(s.w_in, 16)
                                sp.dma_start(yaff[:, 0:1], chan(y_affine[0])).then_inc(s.w_in, 16)
                                sp.dma_start(yaff[:, 1:2], chan(y_affine[1])).then_inc(s.w_in, 16)
                            if biases:
                                sp.dma_start(bq[:], chan(biases[0])).then_inc(s.w_in, 16)
                                sp.dma_start(bk[:], chan(biases[1])).then_inc(s.w_in, 16)
                        if biases:
                            sp.dma_start(bv[:], rows(biases[2])).then_inc(s.w_in, 16)
                    NW_IN = 48 + (64 if x_affine else 0) + (48 if biases else 0)

                    @block.gpsimd
                    def _(pool):
                        pool.memset(hmask[:], 1.0).then_inc(s.zeroed, 1)
                        pool.memset(vmask[:], 1.0).then_inc(s.zeroed, 1)
                        pool.wait_ge(s.zeroed, 1 + 2)
                        for mask, width, n in ((hmask, DK, HQ), (vmask, CT, 2)):
                            pool.affine_select(out=mask[:], in_=mask[:], compare_op=ALU.is_ge, fill=0.0, base=0,
                                               pattern=[[-width, n]], channel_multiplier=1).then_inc(s.hmask_one, 1)
                        pool.wait_ge(s.hmask_one, 1 + 2)
                        for mask, width, n in ((hmask, DK, HQ), (vmask, CT, 2)):
                            pool.affine_select(out=mask[:], in_=mask[:], compare_op=ALU.is_ge, fill=0.0, base=width - 1,
                                               pattern=[[width, n]], channel_multiplier=-1).then_inc(s.hmask_done, 1)

                    @block.vector
                    def _(dve):
                        dve.wait_ge(s.y_in, 1 + 16)
                        if y_affine:
                            dve.bn_stats(stats[:, 0, :], y[:]).then_inc(s.step, 1)
                            dve.wait_ge(s.step, 1 + 1)
                            dve.bn_aggr(moments[:, 0, :], stats[:, 0, :]).then_inc(s.step, 1)
                            dve.wait_ge(s.step, 1 + 3)
                            dve.reciprocal(rstd[:, 0:1], std[:, 0:1]).then_inc(s.step, 1)
                            dve.wait_ge(s.step, 1 + 4)
                            dve.tensor_scalar(yn[:], y[:], moments[:, 0, 0:1], rstd[:, 0:1],
                                              ALU.subtract, ALU.mult).then_inc(s.step, 1)
                        else:
                            dve.tensor_copy(yn[:], y[:]).then_inc(s.step, 5)
                        dve.wait_ge(s.step, 1 + 7)
                        dve.tensor_copy(ydup[:], yT[:].rearrange("p (b t) -> p b t", b=B).unsqueeze(2)
                                        .to_broadcast([P, B, 2, CT])).then_inc(s.step, 1)
                        dve.wait_ge(s.step, 1 + 9)
                        dve.wait_ge(s.w_in, 1 + NW_IN)
                        for b in range(B):
                            if biases:
                                ins = dve.tensor_tensor(v[:, b, :], ops[b][:, 0:W], bv[:], ALU.add)
                            else:
                                ins = dve.tensor_copy(v[:, b, :], ops[b][:, 0:W])
                        ins.then_inc(s.step, 1)
                        dve.wait_ge(s.step, 1 + 11)
                        dve.wait_ge(s.hmask_done, 1 + 2)
                        for b in range(B):
                            for m in range(MC):
                                dve.tensor_tensor(kblk[:, b, m, :, :],
                                                  kT[:, m, b * CT:(b + 1) * CT].unsqueeze(1).to_broadcast([P, HQ, CT]),
                                                  hmask[:].unsqueeze(2).to_broadcast([P, HQ, CT]), ALU.mult)
                            ins = dve.tensor_tensor(vblk[:, b, :, :, :],
                                                    v[:, b, :].rearrange("p (r q d) -> p r q d", r=NP2, q=2),
                                                    vmask[:].unsqueeze(1).unsqueeze(3).to_broadcast([P, NP2, 2, DK]),
                                                    ALU.mult)
                        ins.then_inc(s.step, 1)

                    @block.scalar
                    def _(act):
                        if y_affine:
                            act.wait_ge(s.step, 1 + 2)
                            act.activation(std[:, 0:1], moments[:, 0, 1:2], ACT.Sqrt, bias=eps[:, 0:1]).then_inc(s.step, 1)
                        act.wait_ge(s.step, 1 + 6)
                        act.wait_ge(s.w_in, 1 + NW_IN)
                        if y_affine:
                            act.activation(yT[:], tps[0][:, 0:P], ACT.Identity, bias=yaff[:, 1:2],
                                           scale=yaff[:, 0:1]).then_inc(s.step, 1)
                        else:
                            act.copy(yT[:], tps[0][:, 0:P]).then_inc(s.step, 1)
                        act.wait_ge(s.step, 1 + 10)
                        for m in range(MC):
                            if biases:
                                ins = act.activation(kT[:, m, :], tps[1][:, m * P:(m + 1) * P], ACT.Identity, bias=bk[:, m:m + 1])
                            else:
                                ins = act.copy(kT[:, m, :], tps[1][:, m * P:(m + 1) * P])
                        ins.then_inc(s.step, 1)

                    @block.tensor
                    def _(pe):
                        pe.wait_ge(s.step, 1 + 5)
                        pe.transpose(tps[0][:, 0:P], yn[:], ident[:]).then_inc(s.step, 1)
                        pe.wait_ge(s.step, 1 + 8)
                        pe.wait_ge(s.w_in, 1 + NW_IN)
                        for m in range(MC):
                            pe.matmul(tps[1][:, m * P:(m + 1) * P], wk[:, m * P:(m + 1) * P], yT[:], start=True, stop=True)
                        for b in range(B):
                            mm = pe.matmul(ops[b][:, 0:W], ydup[:, b, :, :].rearrange("p r t -> p (r t)"), wv[:],
                                           start=True, stop=True)
                        mm.then_inc(s.step, 1)
                release(s)

                s = signals(phase, LN + " zT_turned xT_done q_done qT_done scores max_done prob_ready exp_done "
                            "sum_done rinv_done p_turned pT_done pv_done out_done")
                with nc.Block() as block:
                    @block.vector
                    def _(dve):
                        def top(t, j):
                            dve.wait_ge(s.scores, 1 + t + 1)
                            dve.tensor_reduce(nmax[:, j % 2, :], sps[j % 2][:].rearrange("p (h t) -> p h t", h=H),
                                              X, ALU.max, negate=True).then_inc(s.max_done, 1)
                            dve.wait_ge(s.max_done, 1 + t + 1)
                            dve.wait_ge(s.p_turned, 1 + t - (1 if j >= 2 else j))
                            dve.tensor_tensor(prob[:, j % 2, :].rearrange("p (h t) -> p h t", h=H),
                                              sps[j % 2][:].rearrange("p (h t) -> p h t", h=H),
                                              nmax[:, j % 2, :].unsqueeze(2).to_broadcast([P, H, CT]),
                                              ALU.add).then_inc(s.prob_ready, 1)

                        def finish(b, t, j, tile):
                            dve.wait_ge(s.exp_done, 1 + t + 1)
                            dve.tensor_reduce(rsum[:, j % 2, :], prob[:, j % 2, :].rearrange("p (h t) -> p h t", h=H),
                                              X, ALU.add).then_inc(s.sum_done, 1)
                            dve.wait_ge(s.sum_done, 1 + t + 1)
                            dve.reciprocal(rinv[:, j % 2, :], rsum[:, j % 2, :]).then_inc(s.rinv_done, 1)
                            dve.wait_ge(s.rinv_done, 1 + t + 1)
                            dve.wait_ge(s.pv_done, 1 + t + 1)
                            dve.tensor_tensor(ores_flat[:, bass.ts(tile, W)].rearrange("p (h d) -> p h d", h=H),
                                              ops[j % 2][:, 0:W].rearrange("p (h d) -> p h d", h=H),
                                              rinv[:, j % 2, :].unsqueeze(2).to_broadcast([P, H, DK]),
                                              ALU.mult).then_inc(s.out_done, 1)

                        with dve.Fori(0, B, 1) as b:
                            for gg in range(G // B):
                                g = b * (G // B) + gg
                                dve.wait_ge(s.zT_turned, 1 + g * KD)
                                ln_vector(dve, s, g, lambda j: src(g * J + j), lambda j: z[:, j, :])
                                for j in range(J):
                                    top(g * J + j, j)
                                    if j > 0:
                                        finish(b, g * J + j - 1, j - 1, g * J + j - 1)
                                finish(b, g * J + J - 1, J - 1, g * J + J - 1)

                    @block.scalar
                    def _(act):
                        with act.Fori(0, G, 1) as g:
                            ln_scalar(act, s, g)
                            act.wait_ge(s.q_done, 1 + g * MC)
                            for k in range(KD):
                                act.wait_ge(s.zT_turned, 1 + g * KD + k + 1)
                                if x_affine:
                                    act.activation(xT[:, k, :], tps[k][:], ACT.Identity, bias=aff[:, 1, k:k + 1],
                                                   scale=aff[:, 0, k:k + 1]).then_inc(s.xT_done, 1)
                                else:
                                    act.copy(xT[:, k, :], tps[k][:]).then_inc(s.xT_done, 1)
                            act.wait_ge(s.scores, 1 + g * J)
                            for m in range(MC):
                                act.wait_ge(s.q_done, 1 + g * MC + m + 1)
                                if biases:
                                    act.activation(qT[:, m, :], sps[m // 2][:, (m % 2) * 512:(m % 2) * 512 + 512], ACT.Identity,
                                                   bias=bq[:, m:m + 1]).then_inc(s.qT_done, 1)
                                else:
                                    act.copy(qT[:, m, :], sps[m // 2][:, (m % 2) * 512:(m % 2) * 512 + 512]).then_inc(s.qT_done, 1)

                            def evacuate(j):
                                act.wait_ge(s.pv_done, 1 + g * J + j)
                                for q in range(2):
                                    act.wait_ge(s.p_turned, 1 + g * J + j + 1)
                                    act.copy(pT[:, q, :], tps[q][:]).then_inc(s.pT_done, 1)

                            for j in range(J):
                                act.wait_ge(s.prob_ready, 1 + g * J + j + 1)
                                act.activation(prob[:, j % 2, :], prob[:, j % 2, :], ACT.Exp, scale=scale).then_inc(s.exp_done, 1)
                                if j > 0:
                                    evacuate(j - 1)
                            evacuate(J - 1)

                    @block.tensor
                    def _(pe):
                        with pe.Fori(0, B, 1) as b:
                            for gg in range(G // B):
                                g = b * (G // B) + gg
                                pe.wait_ge(s.ln_out, 1 + g * J + J)
                                pe.wait_ge(s.pT_done, 1 + g * J * 2)
                                for k in range(KD):
                                    for j in range(J):
                                        mm = pe.transpose(tps[k][:, j * P:(j + 1) * P], z[:, j, k * P:(k + 1) * P], ident[:])
                                    mm.then_inc(s.zT_turned, 1)
                                pe.wait_ge(s.xT_done, 1 + g * KD + KD)
                                pe.wait_ge(s.prob_ready, 1 + g * J)
                                for m in range(MC):
                                    for k in range(KD):
                                        mm = pe.matmul(sps[m // 2][:, (m % 2) * 512:(m % 2) * 512 + 512],
                                                       wq[:, k, m * P:(m + 1) * P], xT[:, k, :], start=(k == 0), stop=(k == KD - 1))
                                    mm.then_inc(s.q_done, 1)
                                pe.wait_ge(s.qT_done, 1 + g * MC + MC)

                                def weigh(j):
                                    pe.wait_ge(s.exp_done, 1 + g * J + j + 1)
                                    pe.wait_ge(s.pT_done, 1 + (g * J + j) * 2)
                                    for r in range(NP2):
                                        mm = pe.transpose(tps[r // 4][:, (r % 4) * P:(r % 4 + 1) * P],
                                                          prob[:, j % 2, r * P:(r + 1) * P], ident[:])
                                    mm.then_inc(s.p_turned, 1)
                                    pe.wait_ge(s.pT_done, 1 + (g * J + j) * 2 + 2)
                                    pe.wait_ge(s.out_done, 1 + g * J + j - (1 if j >= 2 else j))
                                    for r in range(NP2):
                                        mm = pe.matmul(ops[j % 2][:, r * 2 * DK:(r + 1) * 2 * DK],
                                                       pT[:, r // 4, (r % 4) * P:(r % 4 + 1) * P],
                                                       vblk[:, b, r, :, :].rearrange("p q d -> p (q d)"), start=True, stop=True)
                                    mm.then_inc(s.pv_done, 1)

                                for j in range(J):
                                    if j >= 2:
                                        pe.wait_ge(s.prob_ready, 1 + g * J + j - 1)
                                    for m in range(MC):
                                        mm = pe.matmul(sps[j % 2][:, m * NW:(m + 1) * NW], qT[:, m, j * P:(j + 1) * P],
                                                       kblk[:, b, m, :, :].rearrange("p q t -> p (q t)"), start=True, stop=True)
                                    mm.then_inc(s.scores, 1)
                                    if j > 0:
                                        weigh(j - 1)
                                weigh(J - 1)
                release(s)

        cross_attention("x2", H1, D1, lambda t: x0res[:, t, :], (io["L0_xattn_a2_lnx_g"], io["L0_xattn_a2_lnx_b"]),
                        (io["L0_xattn_a2_lny_g"], io["L0_xattn_a2_lny_b"]), io["a2_wq_flat"], io["a2_wk_flat"],
                        io["a2_wv_flat"], None, SCALE1)
        attention_tail("t2", "L0_xattn_a2_", lambda b, i: ores_flat[:, bass.ts(b * TPB + i, HD)], "gate")

        attn.close()

        DEPTH, _, INNER3 = io["L0_ffn_wqkv"].shape
        HL, DL = INNER3 // 3 // io["L0_ffn_q_scale"].shape[1], io["L0_ffn_q_scale"].shape[1]
        INNER = HL * DL
        HID = io["L0_ffn_w2"].shape[1]
        FCH = [(f * P, min(P, HID - f * P)) for f in range(-(-HID // P))]
        NEG = -1e30

        s = signals("l0", LN)
        with nc.Block() as block:
            @block.vector
            def _(dve):
                with dve.Fori(0, G, 1) as g:
                    ln_vector(dve, s, g, lambda j: xres[:, g * J + j, :], lambda j: x0res[:, g * J + j, :])
                    dve.wait_ge(s.ln_out, 1 + g * J + J)

            @block.scalar
            def _(act):
                with act.Fori(0, G, 1) as g:
                    ln_scalar(act, s, g)
        release(s)

        def local_attention(l):
            U = 4
            ph = f"la{l}"
            with ExitStack() as c:
                wqkv = sb(ph + "w", [P, KD, 3, INNER], F32, c)
                wo = sb(ph + "wo", [P, INNER // P, D], F32, c)
                scl = sb(ph + "scl", [P, 2, DL], F32, c)
                cosr = sb(ph + "cos", [P, NT, 2, DL], F32, c)
                sinr = sb(ph + "sin", [P, NT, 2, DL], F32, c)
                maskf = sb(ph + "mf", [P, 2, 2, P], F32, c)
                masks = sb(ph + "mb", [P, U, 2, 2 * P], BF16, c)
                masko = sb(ph + "mo", [P, 2, 2 * P], BF16, c)
                identb = sb(ph + "ib", [P, P], BF16, c)
                goes_on = sb(ph + "go", [P, U], F32, c)
                xst = sb(ph + "xst", [P, 2, D], F32, c)
                hx = sb(ph + "hx", [P, 2, 2 * P + 1], F32, c)
                sq = sb(ph + "sq", [P, 2 * INNER], F32, c)
                ssum = sb(ph + "ss", [P, 2 * HL], F32, c)
                norm = sb(ph + "nm", [P, 2 * HL], F32, c)
                rnorm = sb(ph + "rn", [P, 2 * HL], F32, c)
                qn = sb(ph + "qn", [P, 2 * HL, DL], F32, c)
                qc = sb(ph + "qc", [P, 2 * HL, DL], F32, c)
                qs = sb(ph + "qs", [P, 2 * HL, DL], F32, c)
                qr = sb(ph + "qr", [P, 2 * HL, DL], F32, c)
                qT = sb(ph + "qT", [P, 2, HL // 2, P], F32, c)
                kT = sb(ph + "kT", [P, U, HL // 2, P], F32, c)
                v = sb(ph + "v", [P, U, INNER], F32, c)
                nmax = sb(ph + "nx", [P, HL], F32, c)
                rsum = sb(ph + "rs", [P, HL], F32, c)
                rinv = sb(ph + "ri", [P, HL], F32, c)
                prob = sb(ph + "pr", [P, HL, 2 * P], F32, c)
                pT = sb(ph + "pT", [P, HL, 2 * P], F32, c)
                o = sb(ph + "o", [P, INNER], F32, c)
                oT = sb(ph + "oT", [P, INNER], F32, c)
                bz = ps(ph + "bz", [P, 512], c)
                bqk = ps(ph + "bqk", [P, 2 * INNER], c)
                bv = ps(ph + "bv", [P, INNER], c)
                bs = ps(ph + "bs", [P, 2048], c)
                order = [4 * (r // 2) + 2 * x + r % 2 for r in range(4) for x in range(2)]

                s = signals(ph, "w_in tab_in built1 built2 built3 tab1 staged x_turned h_copied carried qk_done "
                            "v_ready squared v_done ssum_done norm_done clipped rnorm_done normed cos_done sin_done "
                            "rotated qk_turned qT_done kT_done scores max_done exp_done rinv_done p_turned pT_act pT_dve "
                            "pv_done o_done o_turned oT_done wo_done x_done")

                def steps(e, begin, step):
                    begin()
                    with e.Fori(0, NT // U - 1, 1) as it:
                        for u in range(U):
                            step(it * U + u, u, 2, it)
                    for u in range(U):
                        step(NT - U + u, u, min(2, U - 1 - u), NT // U - 1)

                with nc.Block() as block:
                    @block.sync
                    def _(sp):
                        sp.dma_start(wqkv[:], io["L0_ffn_wqkv"][l].rearrange("(k p) (t n) -> p k t n", p=P, t=3)).then_inc(s.w_in, 16)
                        for slot, head in enumerate(order):
                            sp.dma_start(wo[DL * (slot % 2):DL * (slot % 2) + DL, slot // 2, :],
                                         io["L0_ffn_wo"][l, head * DL:(head + 1) * DL, :]).then_inc(s.w_in, 16)
                        for n, name in enumerate(["L0_ffn_q_scale", "L0_ffn_k_scale"]):
                            sp.dma_start(scl[:, n, :], rows(io[name][l])).then_inc(s.tab_in, 16)
                        for b in range(B):
                            for tab, name in ((cosr, "rotary_cos"), (sinr, "rotary_sin")):
                                sp.dma_start(tab[:, b * TPB:(b + 1) * TPB, :, :],
                                             io[name].rearrange("(t p) q d -> p t q d", p=P)).then_inc(s.tab_in, 16)

                    @block.gpsimd
                    def _(pool):
                        pool.memset(maskf[:], 0.0).then_inc(s.built1, 1)
                        pool.memset(goes_on[:], 1.0).then_inc(s.built1, 1)
                        pool.memset(kT[:, U - 1, :, :], 0.0).then_inc(s.built1, 1)
                        pool.memset(v[:, U - 1, :], 0.0).then_inc(s.built1, 1)
                        pool.memset(hx[:, 1, :], 0.0).then_inc(s.built1, 1)
                        pool.wait_ge(s.built1, 1 + 5)
                        pool.memset(maskf[:, 0, 0, :], NEG).then_inc(s.built2, 1)
                        for q in range(0, U, 2):
                            pool.memset(goes_on[:, q:q + 1], 0.0).then_inc(s.built2, 1)
                        pool.affine_select(out=maskf[:, 1, 0, :], in_=maskf[:, 1, 0, :], compare_op=ALU.is_ge, fill=NEG,
                                           base=0, pattern=[[1, P]], channel_multiplier=-1).then_inc(s.built2, 1)
                        for w in range(2):
                            pool.affine_select(out=maskf[:, w, 1, :], in_=maskf[:, w, 1, :], compare_op=ALU.is_ge, fill=NEG,
                                               base=0, pattern=[[-1, P]], channel_multiplier=1).then_inc(s.built2, 1)
                        pool.wait_ge(s.built2, 1 + 6)
                        pool.tensor_copy(identb[:], ident[:]).then_inc(s.built3, 1)
                        for x in range(2):
                            for q in range(U):
                                pool.tensor_copy(masks[:, q, x, :], maskf[:, q % 2, :, :].rearrange("p a t -> p (a t)")).then_inc(s.built3, 1)
                            pool.tensor_copy(masko[:, x, :], maskf[:, 1, :, :].rearrange("p a t -> p (a t)")).then_inc(s.built3, 1)
                        pool.wait_ge(s.tab_in, 1 + 96)
                        for n in range(2):
                            pool.tensor_tensor(cosr[:, :, n, :], cosr[:, :, n, :],
                                               scl[:, n, :].unsqueeze(1).to_broadcast([P, NT, DL]), ALU.mult).then_inc(s.tab1, 1)
                            for a in range(2):
                                pool.tensor_tensor(sinr[:, :, n, a * 32:(a + 1) * 32], sinr[:, :, n, a * 32:(a + 1) * 32],
                                                   scl[:, n, (1 - a) * 32:(2 - a) * 32].unsqueeze(1).to_broadcast([P, NT, 32]),
                                                   ALU.mult).then_inc(s.tab1, 1)
                        pool.wait_ge(s.tab1, 1 + 6)

                        def stage(t, u):
                            if not (isinstance(t, int) and t == 0):
                                wait_apart(pool, s.x_turned, 1 + t - 1)
                            pool.tensor_copy(xst[:, u % 2, :], x0res[:, t, :]).then_inc(s.staged, 1)

                        def sines(t, u):
                            wait_apart(pool, s.normed, 1 + t + 1)
                            wait_apart(pool, s.rotated, 1 + t)
                            for q in range(2):
                                for a in range(2):
                                    pool.tensor_tensor(qs[:, q * HL:(q + 1) * HL, a * 32:(a + 1) * 32],
                                                       qn[:, q * HL:(q + 1) * HL, (1 - a) * 32:(2 - a) * 32],
                                                       sinr[:, t, q, a * 32:(a + 1) * 32].unsqueeze(1).to_broadcast([P, HL, 32]),
                                                       ALU.mult).then_inc(s.sin_done, 1)

                        def begin():
                            stage(0, 0)
                            stage(1, 1)
                            sines(0, 0)

                        def step(t, u, more, it):
                            if more == 2:
                                stage(t + 2, (u + 2) % U)
                            if more:
                                sines(t + 1, (u + 1) % U)

                        steps(pool, begin, step)

                    @block.vector
                    def _(dve):
                        dve.wait_ge(s.built3, 1 + 11)
                        dve.wait_ge(s.tab1, 1 + 6)

                        def shifted(t, u, it):
                            dve.wait_ge(s.x_turned, 1 + t + 1)
                            dve.wait_ge(s.carried, 1 + t)
                            dve.tensor_copy(hx[:, u % 2, 0:P], bz[:, 0:P]).then_inc(s.h_copied, 1)
                            dve.tensor_copy(hx[:, u % 2, P + 1:2 * P + 1], bz[:, P:2 * P]).then_inc(s.h_copied, 1)
                            if u == 0:
                                dve.tensor_scalar(hx[:, 0, P:P + 1], hx[:, 1, 2 * P:2 * P + 1], goes_on[:, bass.ds(it, 1)],
                                                  None, ALU.mult).then_inc(s.carried, 1)
                            else:
                                dve.tensor_copy(hx[:, u % 2, P:P + 1], hx[:, 1 - u % 2, 2 * P:2 * P + 1]).then_inc(s.carried, 1)

                        def squares_sum(t):
                            dve.wait_ge(s.squared, 1 + t + 1)
                            dve.tensor_reduce(ssum[:], sq[:].rearrange("p (h d) -> p h d", d=DL), X, ALU.add).then_inc(s.ssum_done, 1)

                        def rotary(t):
                            dve.wait_ge(s.norm_done, 1 + t + 1)
                            dve.tensor_scalar(rnorm[:], norm[:], 1e-12, None, ALU.max).then_inc(s.clipped, 1)
                            dve.wait_ge(s.clipped, 1 + t + 1)
                            dve.reciprocal(rnorm[:], rnorm[:]).then_inc(s.rnorm_done, 1)
                            dve.wait_ge(s.rnorm_done, 1 + t + 1)
                            dve.wait_ge(s.sin_done, 1 + t * 4)
                            dve.tensor_tensor(qn[:], bqk[:].rearrange("p (h d) -> p h d", d=DL),
                                              rnorm[:].unsqueeze(2).to_broadcast([P, 2 * HL, DL]), ALU.mult).then_inc(s.normed, 1)
                            dve.wait_ge(s.normed, 1 + t + 1)
                            dve.tensor_tensor(qc[:].rearrange("p (q h) d -> p q h d", q=2),
                                              qn[:].rearrange("p (q h) d -> p q h d", q=2),
                                              cosr[:, t, :, :].unsqueeze(2).to_broadcast([P, 2, HL, DL]),
                                              ALU.mult).then_inc(s.cos_done, 1)
                            dve.wait_ge(s.cos_done, 1 + t + 1)
                            dve.wait_ge(s.sin_done, 1 + t * 4 + 4)
                            dve.wait_ge(s.qk_turned, 1 + t)
                            dve.tensor_tensor(qr[:], qc[:], qs[:], ALU.add).then_inc(s.rotated, 1)

                        def keys(t, u):
                            dve.wait_ge(s.qk_turned, 1 + t + 1)
                            dve.tensor_copy(kT[:, u, :, :].rearrange("p m t -> p (m t)"), bqk[:, INNER:2 * INNER]).then_inc(s.kT_done, 1)

                        def row_max(t):
                            dve.wait_ge(s.scores, 1 + t + 1)
                            dve.wait_ge(s.exp_done, 1 + t * 2)
                            dve.tensor_reduce(nmax[:], bs[:].rearrange("p (s t) -> p s t", s=HL), X, ALU.max,
                                              negate=True).then_inc(s.max_done, 1)

                        def begin():
                            shifted(0, 0, 0)
                            shifted(1, 1, 0)
                            squares_sum(0)
                            rotary(0)
                            keys(0, 0)
                            row_max(0)

                        def step(t, u, more, it):
                            if more == 2:
                                shifted(t + 2, (u + 2) % U, it + 1)
                            if more:
                                squares_sum(t + 1)
                            dve.wait_ge(s.p_turned, 1 + t * 2 + 2)
                            dve.tensor_copy(pT[:, HL // 2:HL, :].rearrange("p s t -> p (s t)"), bs[:, 1024:2048]).then_inc(s.pT_dve, 1)
                            if more:
                                rotary(t + 1)
                            dve.wait_ge(s.exp_done, 1 + t * 2 + 2)
                            dve.wait_ge(s.o_done, 1 + t)
                            dve.reciprocal(rinv[:], rsum[:]).then_inc(s.rinv_done, 1)
                            dve.wait_ge(s.rinv_done, 1 + t + 1)
                            dve.wait_ge(s.pv_done, 1 + t + 1)
                            dve.tensor_tensor(o[:].rearrange("p (s d) -> p s d", s=HL), bv[:].rearrange("p (s d) -> p s d", s=HL),
                                              rinv[:].unsqueeze(2).to_broadcast([P, HL, DL]), ALU.mult).then_inc(s.o_done, 1)
                            if more:
                                keys(t + 1, (u + 1) % U)
                                row_max(t + 1)
                            dve.wait_ge(s.wo_done, 1 + t + 1)
                            dve.tensor_tensor(x0res[:, t, :], bz[:, 0:D], x0res[:, t, :], ALU.add).then_inc(s.x_done, 1)

                        steps(dve, begin, step)

                    @block.scalar
                    def _(act):
                        def squares(t, u):
                            act.wait_ge(s.qk_done, 1 + t + 1)
                            act.wait_ge(s.ssum_done, 1 + t)
                            act.activation(sq[:], bqk[:], ACT.Square).then_inc(s.squared, 1)
                            act.wait_ge(s.v_ready, 1 + t + 1)
                            act.copy(v[:, u, :], bv[:]).then_inc(s.v_done, 1)

                        def norms(t):
                            act.wait_ge(s.ssum_done, 1 + t + 1)
                            act.activation(norm[:], ssum[:], ACT.Sqrt).then_inc(s.norm_done, 1)

                        def queries(t, u):
                            act.wait_ge(s.qk_turned, 1 + t + 1)
                            act.copy(qT[:, u % 2, :, :].rearrange("p m t -> p (m t)"), bqk[:, 0:INNER]).then_inc(s.qT_done, 1)

                        def begin():
                            squares(0, 0)
                            norms(0)
                            queries(0, 0)

                        def step(t, u, more, it):
                            act.wait_ge(s.max_done, 1 + t + 1)
                            act.wait_ge(s.p_turned, 1 + t * 2)
                            act.wait_ge(s.rinv_done, 1 + t)
                            for half in range(2):
                                for h in range(half * HL // 2, (half + 1) * HL // 2):
                                    ins = act.activation(prob[:, h, :], bs[:, h * 256:(h + 1) * 256], ACT.Exp,
                                                         bias=nmax[:, h:h + 1], accum_out=rsum[:, h:h + 1])
                                ins.then_inc(s.exp_done, 1)
                            if more:
                                squares(t + 1, (u + 1) % U)
                            act.wait_ge(s.p_turned, 1 + t * 2 + 1)
                            act.copy(pT[:, 0:HL // 2, :].rearrange("p s t -> p (s t)"), bs[:, 0:1024]).then_inc(s.pT_act, 1)
                            if more:
                                norms(t + 1)
                                queries(t + 1, (u + 1) % U)
                            act.wait_ge(s.o_turned, 1 + t + 1)
                            act.copy(oT[:], bz[:]).then_inc(s.oT_done, 1)

                        steps(act, begin, step)

                    @block.tensor
                    def _(pe):
                        pe.wait_ge(s.w_in, 1 + 16 + 16 * HL)
                        pe.wait_ge(s.built3, 1 + 11)

                        def turn_x(t, u):
                            pe.wait_ge(s.staged, 1 + t + 1)
                            pe.wait_ge(s.h_copied, 1 + t * 2)
                            if not (isinstance(t, int) and t < 2):
                                pe.wait_ge(s.x_done, 1 + t - 2)
                            for k in range(KD):
                                mm = pe.transpose(bz[:, k * P:(k + 1) * P], xst[:, u % 2, k * P:(k + 1) * P], ident[:])
                            mm.then_inc(s.x_turned, 1)

                        def project(t, u):
                            pe.wait_ge(s.carried, 1 + t + 1)
                            pe.wait_ge(s.qT_done, 1 + t)
                            pe.wait_ge(s.kT_done, 1 + t)
                            for n in range(3):
                                dst = bqk[:, n * INNER:(n + 1) * INNER] if n < 2 else bv[:]
                                for k in range(KD):
                                    mm = pe.matmul(dst, hx[:, u % 2, k * P:(k + 1) * P], wqkv[:, k, n, :],
                                                   start=(k == 0), stop=(k == KD - 1))
                                if n == 1:
                                    mm.then_inc(s.qk_done, 1)
                            mm.then_inc(s.v_ready, 1)

                        def turn_qk(t, u):
                            pe.wait_ge(s.rotated, 1 + t + 1)
                            for m in range(HL):
                                mm = pe.transpose(bqk[:, m * P:(m + 1) * P],
                                                  qr[:, 2 * m:2 * m + 2, :].rearrange("p h d -> p (h d)"), ident[:])
                            mm.then_inc(s.qk_turned, 1)

                        def score(t, u, it):
                            pe.wait_ge(s.qT_done, 1 + t + 1)
                            pe.wait_ge(s.kT_done, 1 + t + 1)
                            pe.wait_ge(s.pT_act, 1 + t)
                            pe.wait_ge(s.pT_dve, 1 + t)
                            for r in range(4):
                                mask = masks[:, it, :, :] if u == 0 else masko[:]
                                pe.matmul(bs[:, r * 512:(r + 1) * 512], identb[:], mask.rearrange("p x t -> p (x t)"),
                                          start=True, stop=False, skip_group_check=True)
                                for x in range(2):
                                    e, m = r % 2, 2 * (r // 2) + x
                                    for w, ring in enumerate(((u - 1) % U, u)):
                                        mm = pe.matmul(bs[:, r * 512 + x * 256 + w * P:r * 512 + x * 256 + (w + 1) * P],
                                                       qT[DL * e:DL * e + DL, u % 2, m, :], kT[DL * e:DL * e + DL, ring, m, :],
                                                       start=False, stop=True, skip_group_check=True)
                            mm.then_inc(s.scores, 1)

                        def begin():
                            turn_x(0, 0)
                            turn_x(1, 1)
                            project(0, 0)
                            turn_qk(0, 0)
                            score(0, 0, 0)

                        def step(t, u, more, it):
                            if more:
                                project(t + 1, (u + 1) % U)
                            if more == 2:
                                turn_x(t + 2, (u + 2) % U)
                            for half in range(2):
                                pe.wait_ge(s.exp_done, 1 + t * 2 + half + 1)
                                for h in range(half * HL // 2, (half + 1) * HL // 2):
                                    for w in range(2):
                                        mm = pe.transpose(bs[:, h * 256 + w * P:h * 256 + (w + 1) * P],
                                                          prob[:, h, w * P:(w + 1) * P], ident[:])
                                mm.then_inc(s.p_turned, 1)
                            pe.wait_ge(s.v_done, 1 + t + (2 if more else 1))
                            for slot, head in enumerate(order):
                                if slot == 0:
                                    pe.wait_ge(s.pT_act, 1 + t + 1)
                                if slot == HL // 2:
                                    pe.wait_ge(s.pT_dve, 1 + t + 1)
                                for w, ring in enumerate(((u - 1) % U, u)):
                                    mm = pe.matmul(bv[:, slot * DL:(slot + 1) * DL], pT[:, slot, w * P:(w + 1) * P],
                                                   v[:, ring, head * DL:(head + 1) * DL], start=(w == 0), stop=(w == 1))
                            mm.then_inc(s.pv_done, 1)
                            if more:
                                turn_qk(t + 1, (u + 1) % U)
                            pe.wait_ge(s.o_done, 1 + t + 1)
                            pe.wait_ge(s.h_copied, 1 + 2 * (t + 3 if more == 2 else NT))
                            for m in range(INNER // P):
                                mm = pe.transpose(bz[:, m * P:(m + 1) * P], o[:, m * P:(m + 1) * P], ident[:])
                            mm.then_inc(s.o_turned, 1)
                            if more:
                                score(t + 1, (u + 1) % U, it + 1)
                            pe.wait_ge(s.oT_done, 1 + t + 1)
                            for m in range(INNER // P):
                                mm = pe.matmul(bz[:, 0:D], oT[:, m * P:(m + 1) * P], wo[:, m, :],
                                               start=(m == 0), stop=(m == INNER // P - 1))
                            mm.then_inc(s.wo_done, 1)

                        steps(pe, begin, step)
                release(s)

        def gated_ffn(l):
            ph = f"lf{l}"
            NF = len(FCH)
            HALF = D // 2
            with ExitStack() as c:
                w1 = sb(ph + "w1", [P, KD, 2 * HID], F32, c)
                w2 = sb(ph + "w2", [P, NF, D], F32, c)
                b1 = sb(ph + "b1", [P, 2, NF], F32, c)
                b2 = sb(ph + "b2", [P, D], F32, c)
                aff = sb(ph + "aff", [P, 2, KD], F32, c)
                late = sb(ph + "late", [P, NT, HALF], F32, c)
                pair = sb(ph + "pair", [P, J, 2, 6], F32, c)
                z = sb(ph + "z", [P, J, D], F32, c)
                zT = sb(ph + "zT", [P, KD, GW], F32, c)
                gl = sb(ph + "gl", [P, 2, GW], F32, c)
                hT = sb(ph + "hT", [P, NF, GW], F32, c)
                xb = sb(ph + "xb", [P, J, D], F32, c)
                tps = [ps(f"{ph}t{i}", [P, GW], c) for i in range(2)]
                pa = [ps(f"{ph}a{i}", [P, GW], c) for i in range(2)]
                pg = [ps(f"{ph}g{i}", [P, GW], c) for i in range(2)]
                p3 = [ps(f"{ph}p{i}", [P, 2, D], c) for i in range(2)]
                s = signals(ph, LN + " w_in v_in row_zero late_in zT_turned zT_done ag_done gelu_done h_done "
                            "base_done p3_done x_done gated")
                with nc.Block() as block:
                    @block.sync
                    def _(sp):
                        for lo, hi in ((0, 112), (112, 127)):
                            sp.dma_start(late[lo + 1:hi + 1, :, :], x0res[lo:hi, :, HALF:D]).then_inc(s.late_in, 16)
                        sp.wait_ge(s.row_zero, 1 + 1)
                        for b in range(B):
                            sp.dma_start(late[0:1, b * TPB + 1:(b + 1) * TPB, :],
                                         x0res[P - 1:P, b * TPB:(b + 1) * TPB - 1, HALF:D]).then_inc(s.late_in, 16)
                        sp.dma_start(w1[:], io["L0_ffn_w1"][l].rearrange("(k p) n -> p k n", p=P)).then_inc(s.w_in, 16)
                        full = (NF - 1) * P
                        sp.dma_start(w2[:, 0:NF - 1, :], io["L0_ffn_w2"][l, 0:full, :].rearrange("(k p) n -> p k n", p=P)).then_inc(s.w_in, 16)
                        sp.dma_start(w2[0:HID - full, NF - 1, :], io["L0_ffn_w2"][l, full:HID, :]).then_inc(s.w_in, 16)
                        sp.dma_start(b2[:], rows(io["L0_ffn_b2"][l])).then_inc(s.v_in, 16)
                        with nc.allow_non_contiguous_dma(reason="small vectors by channel"):
                            for n in range(2):
                                sp.dma_start(b1[:, n, 0:NF - 1], chan(io["L0_ffn_b1"][l, n * HID:n * HID + full])).then_inc(s.v_in, 16)
                                sp.dma_start(b1[0:HID - full, n, NF - 1:NF],
                                             io["L0_ffn_b1"][l, n * HID + full:(n + 1) * HID].unsqueeze(1)).then_inc(s.v_in, 16)
                            sp.dma_start(aff[:, 0, :], chan(io["L0_ffn_ln_g"][l])).then_inc(s.v_in, 16)
                            sp.dma_start(aff[:, 1, :], chan(io["L0_ffn_ln_b"][l])).then_inc(s.v_in, 16)

                    @block.gpsimd
                    def _(pool):
                        pool.memset(late[0:1, :, :], 0.0).then_inc(s.row_zero, 1)
                        pool.wait_ge(s.v_in, 1 + 112)
                        with pool.Fori(0, G, 1) as g:
                            wait_apart(pool, s.x_done, 1 + g * 2)
                            for j in range(J):
                                pool.tensor_tensor(xb[:, j, :], x0res[:, g * J + j, :], b2[:], ALU.add).then_inc(s.base_done, 1)

                    @block.vector
                    def _(dve):
                        dve.wait_ge(s.late_in, 1 + 64)
                        dve.wait_ge(s.v_in, 1 + 112)
                        with dve.Fori(0, G, 1) as g:
                            for j in range(J):
                                dve.bn_stats(pair[:, j, 0, :], x0res[:, g * J + j, 0:HALF]).then_inc(s.ln_stats, 1)
                                dve.bn_stats(pair[:, j, 1, :], late[:, g * J + j, :]).then_inc(s.ln_stats, 1)
                            wait_apart(dve, s.ln_stats, 1 + g * 2 * J + 2 * J)
                            for j in range(J):
                                dve.bn_aggr(moments[:, j, :], pair[:, j, :, :].rearrange("p a s -> p (a s)")).then_inc(s.ln_moments, 1)
                            dve.wait_ge(s.ln_std, 1 + g + 1)
                            dve.reciprocal(rstd[:, :], std[:, :]).then_inc(s.ln_rstd, 1)
                            dve.wait_ge(s.ln_rstd, 1 + g + 1)
                            dve.wait_ge(s.zT_turned, 1 + g * KD)
                            for j in range(J):
                                for a, src in ((0, x0res[:, g * J + j, 0:HALF]), (1, late[:, g * J + j, :])):
                                    ins = dve.tensor_scalar(z[:, j, a * HALF:(a + 1) * HALF], src, moments[:, j, 0:1],
                                                            rstd[:, j:j + 1], ALU.subtract, ALU.mult)
                                ins.then_inc(s.ln_out, 1)
                            dve.wait_ge(s.p3_done, 1 + g * J)
                            for f, (f0, n) in enumerate(FCH):
                                dve.wait_ge(s.gelu_done, 1 + g * NF + f + 1)
                                dve.scalar_tensor_tensor(out=hT[0:n, f, :], in0=pa[f % 2][0:n, :], scalar=b1[0:n, 0, f:f + 1],
                                                         in1=gl[0:n, f % 2, :], op0=ALU.add, op1=ALU.mult).then_inc(s.h_done, 1)
                            dve.wait_ge(s.base_done, 1 + g * J + J)
                            for q in range(2):
                                dve.wait_ge(s.p3_done, 1 + g * J + 2 * q + 2)
                                dve.tensor_tensor(x0res[:, bass.ds(g * J + 2 * q, 2), :], p3[q][:], xb[:, 2 * q:2 * q + 2, :],
                                                  ALU.add).then_inc(s.x_done, 1)
                            if l == DEPTH - 1:
                                dve.wait_ge(s.x_done, 1 + g * 2 + 2)
                                for j in range(J):
                                    dve.scalar_tensor_tensor(out=xres[:, g * J + j, :], in0=x0res[:, g * J + j, :],
                                                             scalar=gate[:, 2:3], in1=xres[:, g * J + j, :],
                                                             op0=ALU.mult, op1=ALU.add).then_inc(s.gated, 1)

                    @block.scalar
                    def _(act):
                        act.wait_ge(s.v_in, 1 + 112)
                        with act.Fori(0, G, 1) as g:
                            ln_scalar(act, s, g)
                            act.wait_ge(s.ag_done, 1 + g * NF)
                            for k in range(KD):
                                act.wait_ge(s.zT_turned, 1 + g * KD + k + 1)
                                act.activation(zT[:, k, :], tps[k][:], ACT.Identity, bias=aff[:, 1, k:k + 1],
                                               scale=aff[:, 0, k:k + 1]).then_inc(s.zT_done, 1)
                            for f, (f0, n) in enumerate(FCH):
                                act.wait_ge(s.ag_done, 1 + g * NF + f + 1)
                                act.wait_ge(s.h_done, 1 + g * NF + max(f - 1, 0))
                                act.activation(gl[0:n, f % 2, :], pg[f % 2][0:n, :], ACT.Gelu, bias=b1[0:n, 1, f:f + 1]).then_inc(s.gelu_done, 1)

                    @block.tensor
                    def _(pe):
                        pe.wait_ge(s.w_in, 1 + 48)
                        with pe.Fori(0, G, 1) as g:
                            pe.wait_ge(s.ln_out, 1 + g * J + J)
                            pe.wait_ge(s.zT_done, 1 + g * KD)
                            for k in range(KD):
                                for j in range(J):
                                    mm = pe.transpose(tps[k][:, j * P:(j + 1) * P], z[:, j, k * P:(k + 1) * P], ident[:])
                                mm.then_inc(s.zT_turned, 1)
                            pe.wait_ge(s.zT_done, 1 + g * KD + KD)
                            for f, (f0, n) in enumerate(FCH):
                                pe.wait_ge(s.h_done, 1 + g * NF + max(f - 1, 0))
                                for dst, off in ((pg[f % 2], HID), (pa[f % 2], 0)):
                                    for k in range(KD):
                                        mm = pe.matmul(dst[0:n, :], w1[:, k, off + f0:off + f0 + n], zT[:, k, :],
                                                       start=(k == 0), stop=(k == KD - 1))
                                mm.then_inc(s.ag_done, 1)
                            pe.wait_ge(s.h_done, 1 + g * NF + NF)
                            pe.wait_ge(s.x_done, 1 + g * 2)
                            for j in range(J):
                                for f, (f0, n) in enumerate(FCH):
                                    mm = pe.matmul(p3[j // 2][:, j % 2, :], hT[0:n, f, j * P:(j + 1) * P], w2[0:n, f, :],
                                                   start=(f == 0), stop=(f == NF - 1))
                                mm.then_inc(s.p3_done, 1)
                release(s)

        for l in range(DEPTH):
            local_attention(l)
            gated_ffn(l)


        H3 = 16
        D3 = D // H3
        attn = ExitStack()
        ores = sb("ores3", [P, NT * D], F32, attn)
        ores_flat = ores[:]
        cross_attention("x3", H3, D3, lambda t: xres[:, t, :], None, None, io["L1_xattn_Wq"], io["L1_xattn_Wk"],
                        io["L1_xattn_Wv"], (io["L1_xattn_bq"], io["L1_xattn_bk"], io["L1_xattn_bv"]), D3 ** -0.5)

        E = io["L1_ffn_router_bias"].shape[0]
        FE = io["L1_ffn_fc1_bias"].shape[1]
        CAP = max(1, -(-TOK // E))
        ROW = D + E
        AROW = D + 1
        assert CAP == P
        token_rows = nc.dram_tensor("token_rows", (TOK, ROW), F32).ap()
        mixed = nc.dram_tensor("mixed", (TOK, AROW), F32).ap()
        moe = ExitStack()
        logitsT = sb("logitsT", [E, TOK], F32, moe)
        idxT = sb("idxT", [P, E], U32, moe)
        RING = 4
        w1e = sb("w1e", [P, RING, KD, FE], F32, moe)
        w2e = sb("w2e", [P, RING, FE // P, D], F32, moe)

        with ExitStack() as c:
            wo = sb("r_wo", [P, KD, D], F32, c)
            bo = sb("r_bo", [P, D], F32, c)
            nw = sb("r_nw", [P, D], F32, c)
            rw = sb("r_rw", [P, KD, E], F32, c)
            rb = sb("r_rb", [P, E], F32, c)
            ost = sb("r_ost", [P, J, D], F32, c)
            oT = sb("r_oT", [P, KD, GW], F32, c)
            y = sb("r_y", [P, J, D], F32, c)
            h = sb("r_h", [P, J, D], F32, c)
            junk = sb("r_junk", [P, D], F32, c)
            ms = sb("r_ms", [P, J], F32, c)
            rms = sb("r_rms", [P, J], F32, c)
            rrms = sb("r_rr", [P, J], F32, c)
            row = sb("r_row", [P, J, ROW], F32, c)
            xT = sb("r_xT", [P, KD, GW], F32, c)
            lg = sb("r_lg", [P, J, E], F32, c)
            top = sb("r_top", [P, J], F32, c)
            ex = sb("r_ex", [P, J, E], F32, c)
            den = sb("r_den", [P, J], F32, c)
            rden = sb("r_rden", [P, J], F32, c)
            zero = sb("r_zero", [P, AROW], F32, c)
            tps = [ps(f"r_t{i}", [P, GW], c) for i in range(2)]
            p1 = [ps(f"r_p{i}", [P, 2, D], c) for i in range(2)]
            plg = ps("r_lgps", [P, J, E], c)
            plt = ps("r_ltps", [E, GW], c)
            s = signals("r", LN + " w_in zeroed mixed_zero staged oT_turned oT_done p1_done y_done x_done squared "
                        "rms_done rrms_done xn_done xn_turned xT_done lg_done lg_ready top_done shifted exp_done den_done "
                        "rden_done probs_done lgT_done lgT_out rows_out")
            with nc.Block() as block:
                @block.sync
                def _(sp):
                    sp.dma_start(wo[:], io["L1_xattn_Wo"].rearrange("(k p) n -> p k n", p=P)).then_inc(s.w_in, 16)
                    sp.dma_start(bo[:], rows(io["L1_xattn_bo"])).then_inc(s.w_in, 16)
                    sp.dma_start(nw[:], rows(io["L1_ffn_norm_weight"])).then_inc(s.w_in, 16)
                    sp.dma_start(rw[:], io["router_wT"].rearrange("(k p) n -> p k n", p=P)).then_inc(s.w_in, 16)
                    sp.dma_start(rb[:], rows(io["L1_ffn_router_bias"])).then_inc(s.w_in, 16)
                    sp.wait_ge(s.zeroed, 1 + 1)
                    sp.dma_start(mixed.rearrange("(t p) c -> p t c", p=P),
                                 zero[:].unsqueeze(1).to_broadcast([P, NT, AROW])).then_inc(s.mixed_zero, 16)
                    with sp.Fori(0, G, 1) as g:
                        sp.wait_ge(s.probs_done, 1 + g + 1)
                        sp.dma_start(token_rows.rearrange("(t p) c -> p t c", p=P)[:, bass.ts(g, J), :], row[:]).then_inc(s.rows_out, 16)
                    sp.wait_ge(s.rows_out, 1 + 16 * G)
                    sp.wait_ge(s.mixed_zero, 1 + 16)

                @block.gpsimd
                def _(pool):
                    pool.memset(zero[:], 0.0).then_inc(s.zeroed, 1)
                    with pool.Fori(0, G, 1) as g:
                        wait_apart(pool, s.oT_turned, 1 + g * KD)
                        for j in range(J):
                            pool.tensor_copy(ost[:, j, :], ores_flat[:, bass.ts(g * J + j, D)]).then_inc(s.staged, 1)

                @block.vector
                def _(dve):
                    dve.wait_ge(s.w_in, 1 + 80)
                    with dve.Fori(0, G, 1) as g:
                        for q in range(2):
                            dve.wait_ge(s.p1_done, 1 + g * J + 2 * q + 2)
                            dve.tensor_tensor(y[:, 2 * q:2 * q + 2, :], p1[q][:], bo[:].unsqueeze(1).to_broadcast([P, 2, D]),
                                              ALU.add).then_inc(s.y_done, 1)
                        dve.wait_ge(s.y_done, 1 + g * 2 + 2)
                        for j in range(J):
                            dve.scalar_tensor_tensor(out=xres[:, g * J + j, :], in0=y[:, j, :], scalar=gate[:, 1:2],
                                                     in1=xres[:, g * J + j, :], op0=ALU.mult, op1=ALU.add).then_inc(s.x_done, 1)
                        wait_apart(dve, s.x_done, 1 + g * J + J)
                        ln_vector(dve, s, g, lambda j: xres[:, g * J + j, :], lambda j: h[:, j, :])
                        dve.wait_ge(s.rms_done, 1 + g + 1)
                        dve.reciprocal(rrms[:], rms[:]).then_inc(s.rrms_done, 1)
                        dve.wait_ge(s.rrms_done, 1 + g + 1)
                        dve.wait_ge(s.rows_out, 1 + g * 16)
                        for j in range(J):
                            dve.scalar_tensor_tensor(out=row[:, j, 0:D], in0=h[:, j, :], scalar=rrms[:, j:j + 1],
                                                     in1=nw[:], op0=ALU.mult, op1=ALU.mult).then_inc(s.xn_done, 1)
                        dve.wait_ge(s.lg_done, 1 + g + 1)
                        dve.wait_ge(s.lgT_done, 1 + g)
                        dve.tensor_tensor(lg[:], plg[:], rb[:].unsqueeze(1).to_broadcast([P, J, E]), ALU.add).then_inc(s.lg_ready, 1)
                        dve.wait_ge(s.lg_ready, 1 + g + 1)
                        dve.tensor_reduce(top[:], lg[:], X, ALU.max, negate=True).then_inc(s.top_done, 1)
                        dve.wait_ge(s.top_done, 1 + g + 1)
                        dve.tensor_tensor(ex[:], lg[:], top[:].unsqueeze(2).to_broadcast([P, J, E]), ALU.add).then_inc(s.shifted, 1)
                        dve.wait_ge(s.exp_done, 1 + g + 1)
                        dve.tensor_reduce(den[:], ex[:], X, ALU.add).then_inc(s.den_done, 1)
                        dve.wait_ge(s.den_done, 1 + g + 1)
                        dve.reciprocal(rden[:], den[:]).then_inc(s.rden_done, 1)
                        dve.wait_ge(s.rden_done, 1 + g + 1)
                        dve.tensor_tensor(row[:, :, D:ROW], ex[:], rden[:].unsqueeze(2).to_broadcast([P, J, E]), ALU.mult).then_inc(s.probs_done, 1)

                @block.scalar
                def _(act):
                    with act.Fori(0, G, 1) as g:
                        act.wait_ge(s.p1_done, 1 + g * J)
                        for k in range(KD):
                            act.wait_ge(s.oT_turned, 1 + g * KD + k + 1)
                            act.copy(oT[:, k, :], tps[k][:]).then_inc(s.oT_done, 1)
                        ln_scalar(act, s, g)
                        for j in range(J):
                            act.wait_ge(s.ln_out, 1 + g * J + j + 1)
                            if j > 0:
                                act.wait_ge(s.squared, 1 + g * J + j)
                            act.activation(junk[:], h[:, j, :], ACT.Square, accum_out=ms[:, j:j + 1]).then_inc(s.squared, 1)
                        act.wait_ge(s.squared, 1 + g * J + J)
                        act.activation(rms[:], ms[:], ACT.Sqrt, bias=eps[:, 0:1], scale=1.0 / D).then_inc(s.rms_done, 1)
                        act.wait_ge(s.lg_done, 1 + g)
                        for k in range(KD):
                            act.wait_ge(s.xn_turned, 1 + g * KD + k + 1)
                            act.copy(xT[:, k, :], tps[k][:]).then_inc(s.xT_done, 1)
                        act.wait_ge(s.shifted, 1 + g + 1)
                        act.activation(ex[:], ex[:], ACT.Exp).then_inc(s.exp_done, 1)
                        act.wait_ge(s.lgT_done, 1 + g + 1)
                        act.copy(logitsT[:, bass.ts(g, GW)], plt[:]).then_inc(s.lgT_out, 1)

                @block.tensor
                def _(pe):
                    pe.wait_ge(s.w_in, 1 + 80)
                    with pe.Fori(0, G, 1) as g:
                        pe.wait_ge(s.staged, 1 + g * J + J)
                        pe.wait_ge(s.xT_done, 1 + g * KD)
                        for k in range(KD):
                            for j in range(J):
                                mm = pe.transpose(tps[k][:, j * P:(j + 1) * P], ost[:, j, k * P:(k + 1) * P], ident[:])
                            mm.then_inc(s.oT_turned, 1)
                        pe.wait_ge(s.oT_done, 1 + g * KD + KD)
                        pe.wait_ge(s.y_done, 1 + g * 2)
                        for j in range(J):
                            for k in range(KD):
                                mm = pe.matmul(p1[j // 2][:, j % 2, :], oT[:, k, j * P:(j + 1) * P], wo[:, k, :],
                                               start=(k == 0), stop=(k == KD - 1))
                            mm.then_inc(s.p1_done, 1)
                        pe.wait_ge(s.xn_done, 1 + g * J + J)
                        for k in range(KD):
                            for j in range(J):
                                mm = pe.transpose(tps[k][:, j * P:(j + 1) * P], row[:, j, k * P:(k + 1) * P], ident[:])
                            mm.then_inc(s.xn_turned, 1)
                        pe.wait_ge(s.xT_done, 1 + g * KD + KD)
                        pe.wait_ge(s.lg_ready, 1 + g)
                        for j in range(J):
                            for k in range(KD):
                                mm = pe.matmul(plg[:, j, :], xT[:, k, j * P:(j + 1) * P], rw[:, k, :],
                                               start=(k == 0), stop=(k == KD - 1))
                        mm.then_inc(s.lg_done, 1)
                        pe.wait_ge(s.lg_ready, 1 + g + 1)
                        pe.wait_ge(s.lgT_out, 1 + g)
                        for j in range(J):
                            mm = pe.transpose(plt[:, j * P:(j + 1) * P], lg[:, j, :], ident[:])
                        mm.then_inc(s.lgT_done, 1)
            release(s)

        with ExitStack() as c:
            best = sb("best", [E, 8], F32, c)
            where8 = sb("where8", [E, 8], U32, c)
            chosen = sb("chosen", [E, CAP], F32, c)
            pidx = ps("pidx", [P, E], c)
            s = signals("top", "best_done found kept removed turned idx_done")
            with nc.Block() as block:
                @block.vector
                def _(dve):
                    with dve.Fori(0, CAP // 8, 1) as r:
                        wait_apart(dve, s.removed, 1 + r)
                        dve.max(best[:], logitsT[:]).then_inc(s.best_done, 1)
                        wait_apart(dve, s.best_done, 1 + r + 1)
                        wait_apart(dve, s.kept, 1 + r)
                        dve.max_index(where8[:], best[:], logitsT[:]).then_inc(s.found, 1)
                        wait_apart(dve, s.found, 1 + r + 1)
                        dve.match_replace(logitsT[:], best[:], logitsT[:], -3.4028235e38).then_inc(s.removed, 1)
                        dve.tensor_copy(chosen[:, bass.ts(r, 8)], where8[:]).then_inc(s.kept, 1)
                    dve.wait_ge(s.turned, 1 + 1)
                    dve.tensor_copy(idxT[:], pidx[:]).then_inc(s.idx_done, 1)

                @block.tensor
                def _(pe):
                    pe.wait_ge(s.kept, 1 + CAP // 8)
                    pe.transpose(pidx[:], chosen[:], ident[0:E, 0:E]).then_inc(s.turned, 1)
            release(s)

        with ExitStack() as c:
            FC = FE // P
            b1e = sb("b1e", [P, E, FC], F32, c)
            b2e = sb("b2e", [P, E, D], F32, c)
            idx = sb("idx", [P, RING, 1], U32, c)
            xe = sb("xe", [P, RING, ROW], F32, c)
            xeT = sb("xeT", [P, 2, D], F32, c)
            hT = sb("hTe", [P, 2, FC, P], F32, c)
            gated = sb("gated", [P, 2, AROW], F32, c)
            bx = [ps(f"bx{i}", [P, D], c) for i in range(2)]
            bh = [ps(f"bh{i}", [P, FC, P], c) for i in range(2)]
            by = [ps(f"by{i}", [P, D], c) for i in range(2)]
            s = signals("e", "b_in w_in0 w_in1 w_in2 w_in3 idx_ready @x_in0 @x_in1 @x_in2 @x_in3 turned xT_done fc1_done gelu_done "
                        "fc2_done gate_done biased weighted @added")
            w_in = (s.w_in0, s.w_in1, s.w_in2, s.w_in3)
            x_in = (s.x_in0, s.x_in1, s.x_in2, s.x_in3)
            with nc.Block() as block:
                @block.sync
                def _(sp):
                    with nc.allow_non_contiguous_dma(reason="biases by channel"):
                        sp.dma_start(b1e[:], io["L1_ffn_fc1_bias"].rearrange("e (k p) -> p e k", p=P)).then_inc(s.b_in, 16)
                    sp.dma_start(b2e[:].rearrange("p e c -> p (e c)"),
                                 io["L1_ffn_fc2_bias"].rearrange("e c -> (e c)").unsqueeze(0).to_broadcast([P, E * D])).then_inc(s.b_in, 16)

                    def load(e, r):
                        sp.dma_start(w1e[:, r, :, :], io["fc1_T"].rearrange("e (k p) f -> e p k f", p=P)[e]).then_inc(w_in[r], 16)
                        sp.dma_start(w2e[:, r, :, :], io["fc2_T"].rearrange("e (k p) c -> e p k c", p=P)[e]).then_inc(w_in[r], 16)

                    for r in range(RING):
                        load(r, r)
                    with sp.Fori(1, E // RING, 1) as it:
                        for r in range(RING):
                            sp.wait_ge(s.fc2_done, 1 + it * RING - RING + r + 1)
                            load(it * RING + r, r)

                def steps(eng, step):
                    for r in range(RING):
                        step(r, r, RING)
                    with eng.Fori(1, E // RING - 1, 1) as it:
                        for r in range(RING):
                            step(it * RING + r, r, RING)
                    for r in range(RING):
                        step(E - RING + r, r, RING - 1 - r)

                @block.gpsimd
                def _(pool):
                    def fetch(e, r):
                        if not (isinstance(e, int) and e < RING):
                            wait_apart(pool, s.weighted, 1 + e - RING + 1)
                        wait_apart(pool, s.idx_ready, 1 + e + 1)
                        pool.indirect_dma_start(out=xe[:, r, :], out_offset=None, in_=token_rows,
                                                in_offset=bass.IndirectOffsetOnAxis(ap=idx[:, r, :], axis=0)).then_inc(x_in[r], 16)

                    def step(e, r, more):
                        if more >= 2:
                            fetch(e + 2, (r + 2) % RING)
                        wait_apart(pool, s.weighted, 1 + e + 1)
                        if not (isinstance(e, int) and e == 0):
                            wait_apart(pool, s.added, e * 16)
                        pool.indirect_dma_start(out=mixed, out_offset=bass.IndirectOffsetOnAxis(ap=idx[:, r, :], axis=0),
                                                in_=gated[:, r % 2, :], in_offset=None, compute_op=ALU.add).then_inc(s.added, 16)

                    fetch(0, 0)
                    fetch(1, 1)
                    steps(pool, step)
                    pool.wait_ge(s.added, 16 * E)

                @block.vector
                def _(dve):
                    dve.wait_ge(s.b_in, 1 + 32)

                    def index(e, r):
                        if not (isinstance(e, int) and e < RING):
                            dve.wait_ge(s.added, (e - RING + 1) * 16)
                        dve.tensor_copy(idx[:, r, :], idxT[:, bass.ds(e, 1)]).then_inc(s.idx_ready, 1)

                    def tokens(e, r):
                        dve.wait_ge(s.turned, 1 + e + 1)
                        if not (isinstance(e, int) and e < 2):
                            dve.wait_ge(s.fc1_done, 1 + e - 1)
                        dve.tensor_copy(xeT[:, r % 2, :], bx[r % 2][:]).then_inc(s.xT_done, 1)

                    def step(e, r, more):
                        if more >= 3:
                            index(e + 3, (r + 3) % RING)
                        if more >= 2:
                            tokens(e + 2, (r + 2) % RING)
                        if not (isinstance(e, int) and e < 2):
                            dve.wait_ge(s.added, e * 16 - 16)
                        dve.wait_ge(s.fc2_done, 1 + e + 1)
                        dve.tensor_copy(gated[:, r % 2, D:AROW], xe[:, r, bass.ds(e + D, 1)]).then_inc(s.gate_done, 1)
                        dve.tensor_tensor(gated[:, r % 2, 0:D], by[r % 2][:], b2e[:, e, :], ALU.add).then_inc(s.biased, 1)
                        dve.wait_ge(s.biased, 1 + e + 1)
                        dve.tensor_scalar(gated[:, r % 2, 0:D], gated[:, r % 2, 0:D], gated[:, r % 2, D:AROW], None,
                                          ALU.mult).then_inc(s.weighted, 1)

                    for e in range(3):
                        index(e, e)
                    tokens(0, 0)
                    tokens(1, 1)
                    steps(dve, step)

                @block.scalar
                def _(act):
                    act.wait_ge(s.b_in, 1 + 32)

                    def gelus(e, r):
                        act.wait_ge(s.fc1_done, 1 + e + 1)
                        if not (isinstance(e, int) and e < 2):
                            act.wait_ge(s.fc2_done, 1 + e - 1)
                        for f in range(FC):
                            ins = act.activation(hT[:, r % 2, f, :], bh[r % 2][:, f, :], ACT.Gelu, bias=b1e[:, e, f:f + 1])
                        ins.then_inc(s.gelu_done, 1)

                    def step(e, r, more):
                        if more >= 1:
                            gelus(e + 1, (r + 1) % RING)

                    gelus(0, 0)
                    steps(act, step)

                @block.tensor
                def _(pe):
                    def turn(e, r, it):
                        pe.wait_ge(x_in[r], it * 16 + 16)
                        if not (isinstance(e, int) and e < 2):
                            pe.wait_ge(s.xT_done, 1 + e - 1)
                        for k in range(KD):
                            mm = pe.transpose(bx[r % 2][:, k * P:(k + 1) * P], xe[:, r, k * P:(k + 1) * P], ident[:])
                        mm.then_inc(s.turned, 1)

                    def fc1(e, r, it):
                        pe.wait_ge(w_in[r], 1 + it * 32 + 32)
                        pe.wait_ge(s.xT_done, 1 + e + 1)
                        if not (isinstance(e, int) and e < 2):
                            pe.wait_ge(s.gelu_done, 1 + e - 1)
                        for f in range(FC):
                            for k in range(KD):
                                mm = pe.matmul(bh[r % 2][:, f, :], w1e[:, r, k, f * P:(f + 1) * P], xeT[:, r % 2, k * P:(k + 1) * P],
                                               start=(k == 0), stop=(k == KD - 1))
                        mm.then_inc(s.fc1_done, 1)

                    def fc2(e, r):
                        pe.wait_ge(s.gelu_done, 1 + e + 1)
                        if not (isinstance(e, int) and e < 2):
                            pe.wait_ge(s.weighted, 1 + e - 1)
                        for f in range(FC):
                            mm = pe.matmul(by[r % 2][:], hT[:, r % 2, f, :], w2e[:, r, f, :], start=(f == 0), stop=(f == FC - 1))
                        mm.then_inc(s.fc2_done, 1)

                    def step(it, r, more):
                        e = it * RING + r
                        if more >= 1:
                            fc1(e + 1, (r + 1) % RING, it + (r + 1) // RING)
                        if more >= 2:
                            turn(e + 2, (r + 2) % RING, it + (r + 2) // RING)
                        fc2(e, r)

                    turn(0, 0, 0)
                    fc1(0, 0, 0)
                    turn(1, 1, 0)
                    for r in range(RING):
                        step(0, r, RING)
                    with pe.Fori(1, E // RING - 1, 1) as it:
                        for r in range(RING):
                            step(it, r, RING)
                    for r in range(RING):
                        step(E // RING - 1, r, RING - 1 - r)
            release(s)

        with ExitStack() as c:
            acc = sb("acc", [P, NT, AROW], F32, c)
            none = sb("none", [P, NT], F32, c)
            coef = sb("coef", [P, NT], F32, c)
            fin = sb("fin", [P, NT, D], F32, c)
            s = signals("f", "in0 in1 in2 in3 none_done total_done inverse_done coef_done x_done x_out")
            got = (s.in0, s.in1, s.in2, s.in3)
            with nc.Block() as block:
                @block.sync
                def _(sp):
                    for g in range(G):
                        sp.dma_start(acc[:, g * J:(g + 1) * J, :],
                                     mixed.rearrange("(t p) c -> p t c", p=P)[:, g * J:(g + 1) * J, :]).then_inc(got[g], 16)
                    for g in range(G):
                        sp.wait_ge(s.x_done, 1 + g * J + J)
                        sp.dma_start(out.rearrange("b (t p) c -> p (b t) c", p=P)[:, g * J:(g + 1) * J, :],
                                     fin[:, g * J:(g + 1) * J, :]).then_inc(s.x_out, 16)
                    sp.wait_ge(s.x_out, 1 + 16 * G)

                @block.vector
                def _(dve):
                    for g in range(G):
                        t = slice(g * J, (g + 1) * J)
                        total = acc[:, t, D]
                        dve.wait_ge(got[g], 1 + 16)
                        dve.tensor_scalar(none[:, t], total, 0.0, None, ALU.is_le).then_inc(s.none_done, 1)
                        dve.wait_ge(s.none_done, 1 + g + 1)
                        dve.tensor_tensor(none[:, t], none[:, t], total, ALU.add).then_inc(s.total_done, 1)
                        dve.wait_ge(s.total_done, 1 + g + 1)
                        dve.reciprocal(coef[:, t], none[:, t]).then_inc(s.inverse_done, 1)
                        dve.wait_ge(s.inverse_done, 1 + g + 1)
                        dve.tensor_scalar(coef[:, t], coef[:, t], gate[:, 3:4], None, ALU.mult).then_inc(s.coef_done, 1)
                        dve.wait_ge(s.coef_done, 1 + g + 1)
                        for j in range(J):
                            dve.scalar_tensor_tensor(out=fin[:, g * J + j, :], in0=acc[:, g * J + j, 0:D],
                                                     scalar=coef[:, g * J + j:g * J + j + 1], in1=xres[:, g * J + j, :],
                                                     op0=ALU.mult, op1=ALU.add).then_inc(s.x_done, 1)
            release(s)
        moe.close()
        attn.close()


def shape_constants(tokens=1024, dim=64, window=128):
    import numpy as np

    half = np.arange(0, dim, 2, dtype=np.float32)
    inv_freq = (1.0 / np.float32(10000.0) ** (half / np.float32(dim))).astype(np.float32)
    t = np.arange(tokens, dtype=np.float32)
    freqs = t[:, None] * inv_freq[None, :]
    base = ((half + np.float32(0.4 * dim)) / np.float32(1.4 * dim)).astype(np.float32)
    power = (t - tokens // 2) / np.float32(window // 2)
    scale = (base[None, :] ** power[:, None]).astype(np.float32)
    cos, sin = np.cos(freqs), np.sin(freqs)
    qk_scale = np.float32(8.0)
    two = lambda a, b: np.concatenate([a, b], axis=-1)
    c = np.stack([two(cos * scale, cos * scale) * qk_scale, two(cos / scale, cos / scale)], axis=1)
    s = np.stack([two(-sin * scale, sin * scale) * qk_scale, two(-sin / scale, sin / scale)], axis=1)
    return {"rotary_cos": c.astype(np.float32), "rotary_sin": s.astype(np.float32)}


def kernel(**inputs):
    import numpy as np
    import concourse.bacc as bacc
    from concourse import mybir
    from concourse.bass_utils import run_bass_kernel_spmd as run

    given = {name: np.ascontiguousarray(value) for name, value in inputs.items()}
    for block in ("a1", "a2"):
        for w in ("wq", "wk", "wv"):
            a = given[f"L0_xattn_{block}_{w}"]
            given[f"{block}_{w}_flat"] = np.ascontiguousarray(a.transpose(1, 0, 2).reshape(a.shape[1], -1))
    given["router_wT"] = np.ascontiguousarray(given["L1_ffn_router_weight"].T)
    given["fc1_T"] = np.ascontiguousarray(given.pop("L1_ffn_fc1_weight").transpose(0, 2, 1))
    given["fc2_T"] = np.ascontiguousarray(given.pop("L1_ffn_fc2_weight").transpose(0, 2, 1))
    given.update(shape_constants())
    nc = bacc.Bacc("TRN2", target_bir_lowering=False, num_devices=1)
    arrays, io = {}, {}
    for name, a in given.items():
        arrays["in_" + name] = a
        io[name] = nc.dram_tensor("in_" + name, a.shape, mybir.dt.from_np(a.dtype), kind="ExternalInput").ap()
    out = nc.dram_tensor("x_out", inputs["x"].shape, mybir.dt.float32, kind="ExternalOutput").ap()
    build(nc, io, out)
    return run(nc, [arrays], core_ids=[0]).results[0]["x_out"]
```

```python
def build(nc, io, out):
    import concourse.bass as bass
    from concourse import mybir
    from collections import namedtuple
    from contextlib import ExitStack

    F32, F16, BF16, U32, I32 = mybir.dt.float32, mybir.dt.float16, mybir.dt.bfloat16, mybir.dt.uint32, mybir.dt.int32
    ALU = mybir.AluOpType
    ACT = mybir.ActivationFunctionType
    X = mybir.AxisListType.X

    P = 128
    B, N, D = io["x"].shape
    TOK = B * N
    NT = TOK // P
    TPB = N // P
    J = 4
    G = NT // J
    GW = J * P
    KD = D // P
    EPS = 1e-5

    def signals(phase, names):
        sems = []
        for n in names.split():
            sems.append(nc.alloc_semaphore(f"{phase}_{n.lstrip('@')}"))
            if not n.startswith("@"):
                nc.gpsimd.sem_inc(sems[-1], 1)
        nc.all_engine_barrier()
        return namedtuple("Signals", names.replace("@", ""))(*sems)

    def release(s):
        nc.clear_and_free_semaphores(list(s))

    stack = ExitStack()

    def sb(name, shape, dt=F32, where=None):
        return (where or stack).enter_context(nc.sbuf_tensor(name, shape, dt))

    def ps(name, shape, where, dt=F32):
        return where.enter_context(nc.psum_tensor(name, shape, dt))

    def chan(ap):
        return ap.rearrange("(k p) -> p k", p=P)

    def rows(ap):
        return ap.unsqueeze(0).to_broadcast([P, ap.shape[0]])

    with stack:
        xres = sb("xres", [P, NT, D])
        x0res = sb("x0res", [P, NT, D])
        ident = sb("ident", [P, P])
        eps = sb("eps", [P, 1])
        gate = sb("gate", [P, 4])
        stats = sb("stats", [P, J, 6])
        moments = sb("moments", [P, J, 2])
        std = sb("std", [P, J])
        rstd = sb("rstd", [P, J])

        waited = nc.alloc_semaphore("waited")

        LN = "ln_stats ln_moments ln_std ln_rstd ln_out"

        def wait_apart(e, signal, value):
            e.wait_ge(signal, value)
            e.sem_inc(waited, 1)

        def ln_vector(e, s, n, src, dst, out=None):
            for j in range(J):
                e.bn_stats(stats[:, j, :], src(j)).then_inc(s.ln_stats, 1)
            wait_apart(e, s.ln_stats, 1 + n * J + J)
            for j in range(J):
                e.bn_aggr(moments[:, j, :], stats[:, j, :]).then_inc(s.ln_moments, 1)
            e.wait_ge(s.ln_std, 1 + n + 1)
            e.reciprocal(rstd[:, :], std[:, :]).then_inc(s.ln_rstd, 1)
            e.wait_ge(s.ln_rstd, 1 + n + 1)
            e.wait_ge(s.ln_moments, 1 + n * J + J)
            for j in range(J):
                e.tensor_scalar(dst(j), src(j), moments[:, j, 0:1], rstd[:, j:j + 1],
                                ALU.subtract, ALU.mult).then_inc(out or s.ln_out, 1)

        def ln_scalar(a, s, n):
            a.wait_ge(s.ln_moments, 1 + n * J + J)
            a.activation(std[:, :], moments[:, :, 1], ACT.Sqrt, bias=eps[:, 0:1]).then_inc(s.ln_std, 1)

        s = signals("setup", "x_in gates_in zeroed ident_done eps_done tanh_done")
        with nc.Block() as block:
            @block.sync
            def _(sp):
                for q in range(4):
                    sp.dma_start(xres[:, q * J:(q + 1) * J, :],
                                 io["x"].rearrange("b (t p) c -> p (b t) c", p=P)[:, q * J:(q + 1) * J, :]).then_inc(s.x_in, 16)
                sp.dma_start(gate[:, 0:2], rows(io["g_xattn"])).then_inc(s.gates_in, 16)
                sp.dma_start(gate[:, 2:4], rows(io["g_ffn"])).then_inc(s.gates_in, 16)
                sp.wait_ge(s.x_in, 1 + 64)

            @block.gpsimd
            def _(pool):
                pool.memset(ident[:], 0.0).then_inc(s.zeroed, 1)
                wait_apart(pool, s.zeroed, 1 + 1)
                pool.affine_select(out=ident[:], in_=ident[:], compare_op=ALU.not_equal, fill=1.0,
                                   base=0, pattern=[[-1, P]], channel_multiplier=1).then_inc(s.ident_done, 1)
                pool.memset(eps[:], EPS).then_inc(s.eps_done, 1)

            @block.scalar
            def _(act):
                act.wait_ge(s.gates_in, 1 + 32)
                act.activation(gate[:], gate[:], ACT.Tanh).then_inc(s.tanh_done, 1)
        release(s)

        H1, _, D1 = io["L0_xattn_a1_wq"].shape
        HD = H1 * D1
        MC = HD // P
        SCALE1 = D1 ** -0.5
        q_parts = nc.dram_tensor("q_parts", (2, B * HD, N), F16).ap()
        k_parts = nc.dram_tensor("k_parts", (2, B * HD, N), F16).ap()

        def tail_weights(phase, name, c):
            F = io[name + "li2_w"].shape[1]
            FC = F // P
            w1 = sb(phase + "w1", [P, MC, D], F32, c)
            w2 = sb(phase + "w2", [P, KD, F], F32, c)
            w3 = sb(phase + "w3", [P, FC, D], F32, c)
            b1 = sb(phase + "b1", [P, D], F32, c)
            b3 = sb(phase + "b3", [P, D], F32, c)
            ng = sb(phase + "ng", [P, D], F32, c)
            nb = sb(phase + "nb", [P, D], F32, c)
            b2 = sb(phase + "b2", [P, FC], F32, c)
            aff = sb(phase + "aff", [P, 2, KD], F32, c)

            def ahead(sp, sem):
                sp.dma_start(w1[:], io[name + "li1_w"].rearrange("(k p) n -> p k n", p=P)).then_inc(sem, 16)
                sp.dma_start(w2[:], io[name + "li2_w"].rearrange("(k p) n -> p k n", p=P)).then_inc(sem, 16)
                sp.dma_start(w3[:], io[name + "li3_w"].rearrange("(k p) n -> p k n", p=P)).then_inc(sem, 16)
                sp.dma_start(b1[:], rows(io[name + "li1_b"])).then_inc(sem, 16)
                sp.dma_start(b3[:], rows(io[name + "li3_b"])).then_inc(sem, 16)
                sp.dma_start(ng[:], rows(io["L0_xattn_ln2_g"])).then_inc(sem, 16)
                sp.dma_start(nb[:], rows(io["L0_xattn_ln2_b"])).then_inc(sem, 16)
                with nc.allow_non_contiguous_dma(reason="small vectors by channel"):
                    sp.dma_start(b2[:], chan(io[name + "li2_b"])).then_inc(sem, 16)
                    sp.dma_start(aff[:, 0, :], chan(io[name + "ln3_g"])).then_inc(sem, 16)
                    sp.dma_start(aff[:, 1, :], chan(io[name + "ln3_b"])).then_inc(sem, 16)
                return 160

            return (w1, w2, w3, b1, b3, ng, nb, b2, aff), ahead

        attn = ExitStack()
        ores = sb("ores", [P, B * H1, TPB, D1], F32, attn)
        t1ctx = ExitStack()
        t1_weights, t1_ahead = tail_weights("t1", "L0_xattn_a1_", t1ctx)
        vctx = ExitStack()
        vres = sb("vres", [P, B * H1, TPB, D1], F32, vctx)

        with ExitStack() as c:
            wq = sb("a1wq", [P, KD, HD], F32, c)
            wk = sb("a1wk", [P, KD, HD], F32, c)
            wv = sb("a1wv", [P, KD, HD], F32, c)
            ln1g = sb("ln1g", [P, D], F32, c)
            ln1b = sb("ln1b", [P, D], F32, c)
            aff = sb("aff", [P, 4, KD], F32, c)
            h = sb("h", [P, J, D], F32, c)
            z = sb("z", [P, J, D], F32, c)
            xT = sb("xT", [P, KD, GW], F32, c)
            yT = sb("yT", [P, KD, GW], F32, c)
            parts = sb("parts", [P, 2, 2, MC, GW], F16, c)
            zps = [ps(f"zps{k}", [P, GW], c) for k in range(KD)]
            pps = [ps(f"pps{k}", [P, GW], c) for k in range(6)]

            s = signals("a1p", LN + " w_in aff_in scaled x0_done z_done zT_done affine_done "
                        "proj_done hi_done proj_free_dve v_done parts_out")

            def steps(e, first, step):
                first(0)
                with e.Fori(0, B - 1, 1) as b:
                    for gg in range(G // B):
                        step(b, gg, True)
                for gg in range(G // B):
                    step(B - 1, gg, gg + 1 < G // B)

            with nc.Block() as block:
                @block.sync
                def _(sp):
                    with nc.allow_non_contiguous_dma(reason="small vectors by channel"):
                        for n, name in enumerate(["lnx_g", "lnx_b", "lny_g", "lny_b"]):
                            sp.dma_start(aff[:, n, :], chan(io["L0_xattn_a1_" + name])).then_inc(s.aff_in, 16)
                    sp.dma_start(ln1g[:], rows(io["L0_xattn_ln1_g"])).then_inc(s.aff_in, 16)
                    sp.dma_start(ln1b[:], rows(io["L0_xattn_ln1_b"])).then_inc(s.aff_in, 16)
                    for w, name in ((wq, "wq"), (wk, "wk"), (wv, "wv")):
                        sp.dma_start(w[:], io["a1_" + name + "_flat"].rearrange("(k p) n -> p k n", p=P)).then_inc(s.w_in, 16)
                    with sp.Fori(0, B, 1) as b:
                        for gg in range(G // B):
                            g = b * (G // B) + gg
                            sp.wait_ge(s.hi_done, 1 + g * 8 + 8)
                            sp.wait_ge(s.proj_free_dve, 1 + g * 8 + 8)
                            for t, dst in enumerate((q_parts, k_parts)):
                                for part in range(2):
                                    sp.dma_start(dst[part, bass.ts(b, HD), gg * GW:(gg + 1) * GW].rearrange("(m p) n -> p m n", p=P),
                                                 parts[:, t, part, :, :]).then_inc(s.parts_out, 16)
                    sp.wait_ge(s.parts_out, 1 + 64 * G)

                @block.vector
                def _(dve):
                    def first(g):
                        dve.wait_ge(s.ln_out, 1 + g * 12)
                        dve.wait_ge(s.zT_done, 1 + g)
                        ln_vector(dve, s, g * 3, lambda j: xres[:, g * J + j, :], lambda j: h[:, j, :])
                        dve.wait_ge(s.ln_out, 1 + g * 12 + 4)
                        dve.wait_ge(s.x0_done, 1 + g * J)
                        ln_vector(dve, s, g * 3 + 1, lambda j: h[:, j, :], lambda j: z[:, j, :])

                    def step(b, gg, more):
                        g = b * (G // B) + gg
                        dve.wait_ge(s.ln_out, 1 + g * 12 + 8)
                        dve.wait_ge(s.x0_done, 1 + g * J + J)
                        ln_vector(dve, s, g * 3 + 2, lambda j: x0res[:, g * J + j, :], lambda j: h[:, j, :])
                        if more:
                            first(g + 1)
                        dve.wait_ge(s.parts_out, 1 + g * 64)
                        for n in range(8):
                            t, m = n // 4, n % 4
                            dve.wait_ge(s.hi_done, 1 + g * 8 + n + 1)
                            dve.scalar_tensor_tensor(out=parts[:, t, 1, m, :], in0=pps[n % 6][:],
                                                     scalar=SCALE1 if t == 0 else 1.0, in1=parts[:, t, 0, m, :],
                                                     op0=ALU.mult, op1=ALU.subtract).then_inc(s.proj_free_dve, 1)
                        for n in range(8, 12):
                            dve.wait_ge(s.proj_done, 1 + g * 12 + n + 1)
                            dve.tensor_copy(vres[:, bass.ts(b, H1), gg * J + n - 8, :],
                                                pps[n % 6][:].rearrange("p (h d) -> p h d", h=H1)).then_inc(s.v_done, 1)

                    steps(dve, first, step)

                @block.gpsimd
                def _(pool):
                    wait_apart(pool, s.aff_in, 1 + 96)
                    with pool.Fori(0, B, 1) as b:
                        for gg in range(G // B):
                            g = b * (G // B) + gg
                            for j in range(J):
                                wait_apart(pool, s.ln_out, 1 + g * 12 + 5 + j)
                                pool.tensor_tensor(z[:, j, :], z[:, j, :], ln1g[:], ALU.mult).then_inc(s.scaled, 1)
                                wait_apart(pool, s.scaled, 1 + g * J + j + 1)
                                pool.tensor_tensor(x0res[:, g * J + j, :], z[:, j, :], ln1b[:], ALU.add).then_inc(s.x0_done, 1)

                @block.tensor
                def _(pe):
                    pe.wait_ge(s.w_in, 1 + 48)
                    with pe.Fori(0, B, 1) as b:
                        for gg in range(G // B):
                            g = b * (G // B) + gg
                            pe.wait_ge(s.ln_out, 1 + g * 12 + 12)
                            pe.wait_ge(s.affine_done, 1 + g * 4)
                            for k in range(KD):
                                for j in range(J):
                                    mm = pe.transpose(zps[k][:, j * P:(j + 1) * P], h[:, j, k * P:(k + 1) * P], ident[:])
                            mm.then_inc(s.zT_done, 1)
                            pe.wait_ge(s.affine_done, 1 + g * 4 + 4)
                            for n in range(12):
                                if n < 4:
                                    pe.wait_ge(s.proj_free_dve if n < 2 else s.v_done, 1 + g * (8 if n < 2 else 4))
                                elif n < 6:
                                    pe.wait_ge(s.v_done, 1 + g * 4)
                                else:
                                    pe.wait_ge(s.proj_free_dve, 1 + g * 8 + n - 5)
                                for k in range(KD):
                                    if n < 4:
                                        mm = pe.matmul(pps[n % 6][:], wq[:, k, n * P:(n + 1) * P], xT[:, k, :],
                                                       start=(k == 0), stop=(k == KD - 1))
                                    elif n < 8:
                                        mm = pe.matmul(pps[n % 6][:], wk[:, k, (n - 4) * P:(n - 3) * P], yT[:, k, :],
                                                       start=(k == 0), stop=(k == KD - 1))
                                    else:
                                        mm = pe.matmul(pps[n % 6][:], yT[:, k, (n - 8) * P:(n - 7) * P], wv[:, k, :],
                                                       start=(k == 0), stop=(k == KD - 1))
                                mm.then_inc(s.proj_done, 1)

                @block.scalar
                def _(act):
                    act.wait_ge(s.aff_in, 1 + 96)
                    def first(g):
                        for n in range(2):
                            ln_scalar(act, s, g * 3 + n)

                    def step(b, gg, more):
                        g = b * (G // B) + gg
                        ln_scalar(act, s, g * 3 + 2)
                        act.wait_ge(s.zT_done, 1 + g + 1)
                        act.wait_ge(s.proj_done, 1 + g * 12)
                        for k in range(KD):
                            act.activation(xT[:, k, :], zps[k][:], ACT.Identity, bias=aff[:, 1, k:k + 1],
                                           scale=aff[:, 0, k:k + 1]).then_inc(s.affine_done, 1)
                            act.activation(yT[:, k, :], zps[k][:], ACT.Identity, bias=aff[:, 3, k:k + 1],
                                           scale=aff[:, 2, k:k + 1]).then_inc(s.affine_done, 1)
                        act.wait_ge(s.parts_out, 1 + g * 64)
                        if more:
                            first(g + 1)
                        for n in range(8):
                            t, m = n // 4, n % 4
                            act.wait_ge(s.proj_done, 1 + g * 12 + n + 1)
                            act.activation(parts[:, t, 0, m, :], pps[n % 6][:], ACT.Copy,
                                           scale=SCALE1 if t == 0 else 1.0).then_inc(s.hi_done, 1)

                    steps(act, first, step)
            release(s)

        with ExitStack() as c:
            qs = sb("qs", [P, 2, N], F16, c)
            ks = sb("ks", [P, 2, N], F16, c)
            prob = sb("prob", [P, 4, N], F32, c)
            probT = sb("probT", [P, 3, GW], F32, c)
            after = sb("after", [P, P], F32, c)
            negmax = sb("negmax", [P, 2, TPB], F32, c)
            rowsum = sb("rowsum", [P, 2, TPB], F32, c)
            rinv = sb("rinv", [P, 2, TPB], F32, c)
            sps = [ps(f"sps{i}", [P, N], c) for i in range(2)]
            tps = [ps(f"tps{i}", [P, GW], c) for i in range(2)]
            opsum = [ps(f"ops{i}", [P, 512], c) for i in range(2)]

            one_head = [(i, t0, min(4, TPB - t0), "act" if t0 > i or i == 3 else "dve")
                        for i in range(TPB) for t0 in range(i, TPB, 4)]
            groups = [(u * TPB + i, t0, cnt, who) for u in range(2) for (i, t0, cnt, who) in one_head]
            NG = len(groups)
            TILES = 2 * TPB
            LEAD = 3
            PAIRS = B * H1 // 2

            def evacuated(who, k):
                return sum(g[3] == who for g in groups[:k])

            def turned_before(n):
                return sum(g[0] < n for g in groups)

            ALL_ACT, ALL_DVE = evacuated("act", NG), evacuated("dve", NG)
            s = signals("a1a", "in_even in_odd cleared after_ready scores max_done exp_done masked "
                        "turned evac_act evac_dve used rinv_done out_done next_in")
            landed = (s.in_even, s.in_odd)
            with nc.Block() as block:
                @block.sync
                def _(sp):
                    def load(hh, u):
                        for r in range(4):
                            sp.dma_start(qs[32 * r:32 * r + 32, u, :],
                                         q_parts[r // 2, bass.ds(hh * D1, D1), :]).then_inc(landed[u], 16)
                            sp.dma_start(ks[32 * r:32 * r + 32, u, :],
                                         k_parts[r % 2, bass.ds(hh * D1, D1), :]).then_inc(landed[u], 16)

                    load(0, 0)
                    load(1, 1)
                    next_count = t1_ahead(sp, s.next_in)
                    with sp.Fori(1, PAIRS, 1) as it:
                        for u in range(2):
                            sp.wait_ge(s.scores, 1 + it * TILES - TILES + TPB * (u + 1))
                            load(it * 2 + u, u)
                    sp.wait_ge(s.next_in, 1 + next_count)

                @block.tensor
                def _(pe):
                    def tile_scores(it, n):
                        u, i = (n // TPB) % 2, n % TPB
                        if i == 0:
                            pe.wait_ge(landed[u], 1 + it * 128 + 128 * (n // TILES + 1))
                        if n >= 2:
                            pe.wait_ge(s.exp_done, 1 + it * TILES + n - 1)
                        for half in range(2):
                            mm = pe.matmul(sps[n % 2][:, half * 512:(half + 1) * 512], qs[:, u, i * P:(i + 1) * P],
                                           ks[:, u, half * 512:(half + 1) * 512], start=True, stop=True)
                        mm.then_inc(s.scores, 1)

                    def turn(it, k):
                        n, t0, cnt, who = groups[k]
                        pe.wait_ge(s.masked, 1 + it * TILES + n + 1)
                        pe.wait_ge(s.evac_act, 1 + it * ALL_ACT + evacuated("act", max(k - 1, 0)))
                        pe.wait_ge(s.evac_dve, 1 + it * ALL_DVE + evacuated("dve", max(k - 1, 0)))
                        for w in range(cnt):
                            mm = pe.transpose(tps[k % 2][:, w * P:(w + 1) * P],
                                              prob[:, n % 4, (t0 + w) * P:(t0 + w + 1) * P], ident[:])
                        mm.then_inc(s.turned, 1)

                    def weigh(it, k):
                        n, t0, cnt, who = groups[k]
                        u, i = n // TPB, n % TPB
                        pe.wait_ge(s.evac_act, 1 + it * ALL_ACT + evacuated("act", k + 1))
                        pe.wait_ge(s.evac_dve, 1 + it * ALL_DVE + evacuated("dve", k + 1))
                        if i == 0 and t0 == 0:
                            pe.wait_ge(s.out_done, 1 + it * 2)
                        for w in range(cnt):
                            mm = pe.matmul(opsum[u][:, i * D1:(i + 1) * D1], probT[:, k % 3, w * P:(w + 1) * P],
                                           vres[:, it * 2 + u, t0 + w, :],
                                           start=(t0 == i and w == 0), stop=(t0 + w == TPB - 1))
                        mm.then_inc(s.used, 1)

                    def pair(it, last):
                        for k in range(NG):
                            n = groups[k][0]
                            if (k == 0 or groups[k - 1][0] != n) and not (last and n + LEAD >= TILES):
                                tile_scores(it, n + LEAD)
                            turn(it, k)
                            if k > 1:
                                weigh(it, k - 2)
                        weigh(it, NG - 2)
                        weigh(it, NG - 1)

                    for n in range(LEAD):
                        tile_scores(0, n)
                    with pe.Fori(0, PAIRS - 1, 1) as it:
                        pair(it, False)
                    pair(PAIRS - 1, True)

                @block.vector
                def _(dve):
                    def row_max(it, n):
                        u, i = (n // TPB) % 2, n % TPB
                        dve.wait_ge(s.scores, 1 + it * TILES + n + 1)
                        dve.tensor_reduce(negmax[:, u, i:i + 1], sps[n % 2][:], X, ALU.max, negate=True).then_inc(s.max_done, 1)

                    def pair(it, last):
                        k = 0
                        for n in range(TILES):
                            u = n // TPB
                            while k < NG and groups[k][0] == n:
                                if groups[k][3] == "dve":
                                    w = groups[k][2] * P
                                    dve.wait_ge(s.turned, 1 + it * NG + k + 1)
                                    dve.wait_ge(s.used, 1 + it * NG + max(k - 2, 0))
                                    dve.tensor_copy(probT[:, k % 3, 0:w], tps[k % 2][:, 0:w]).then_inc(s.evac_dve, 1)
                                k += 1
                            if not (last and n + LEAD >= TILES):
                                row_max(it, n + LEAD)
                            if n % TPB == TPB - 1:
                                dve.wait_ge(s.exp_done, 1 + it * TILES + n + 1)
                                dve.reciprocal(rinv[:, u, :], rowsum[:, u, :]).then_inc(s.rinv_done, 1)
                            if n in (TPB, TILES - 1):
                                u = n // TPB - 1 if n == TPB else 1
                                dve.wait_ge(s.rinv_done, 1 + it * 2 + u + 1)
                                dve.wait_ge(s.used, 1 + it * NG + NG // 2 * (u + 1))
                                dve.tensor_tensor(ores[:, it * 2 + u, :, :],
                                                  opsum[u][:, 0:TPB * D1].rearrange("p (i d) -> p i d", i=TPB),
                                                  rinv[:, u, :].unsqueeze(2).to_broadcast([P, TPB, D1]),
                                                  ALU.mult).then_inc(s.out_done, 1)

                    for n in range(LEAD):
                        row_max(0, n)
                    with dve.Fori(0, PAIRS - 1, 1) as it:
                        pair(it, False)
                    pair(PAIRS - 1, True)

                @block.scalar
                def _(act):
                    def exponent(it, n):
                        u, i = (n // TPB) % 2, n % TPB
                        act.wait_ge(s.max_done, 1 + it * TILES + n + 1)
                        if n >= LEAD:
                            act.wait_ge(s.turned, 1 + it * NG + turned_before(n - 3))
                        if i == 0 and n > 0:
                            act.wait_ge(s.rinv_done, 1 + it * 2 + n // TILES)
                        act.activation(prob[:, n % 4, :], sps[n % 2][:], ACT.Exp, bias=negmax[:, u, i:i + 1],
                                       accum_out=rowsum[:, u, i:i + 1]).then_inc(s.exp_done, 1)

                    def pair(it, last):
                        k = 0
                        for n in range(TILES):
                            while k < NG and groups[k][0] == n:
                                if groups[k][3] == "act":
                                    w = groups[k][2] * P
                                    act.wait_ge(s.turned, 1 + it * NG + k + 1)
                                    act.wait_ge(s.used, 1 + it * NG + max(k - 2, 0))
                                    act.copy(probT[:, k % 3, 0:w], tps[k % 2][:, 0:w]).then_inc(s.evac_act, 1)
                                k += 1
                            if not (last and n + LEAD >= TILES):
                                exponent(it, n + LEAD)

                    for n in range(LEAD):
                        exponent(0, n)
                    with act.Fori(0, PAIRS - 1, 1) as it:
                        pair(it, False)
                    pair(PAIRS - 1, True)

                @block.gpsimd
                def _(pool):
                    pool.memset(after[:], 0.0).then_inc(s.cleared, 1)
                    pool.wait_ge(s.cleared, 1 + 1)
                    pool.affine_select(out=after[:], in_=after[:], compare_op=ALU.is_ge, fill=1.0,
                                       base=0, pattern=[[-1, P]], channel_multiplier=1).then_inc(s.after_ready, 1)
                    wait_apart(pool, s.after_ready, 1 + 1)
                    with pool.Fori(0, PAIRS, 1) as it:
                        for n in range(TILES):
                            i = n % TPB
                            wait_apart(pool, s.exp_done, 1 + it * TILES + n + 1)
                            blk = prob[:, n % 4, i * P:(i + 1) * P]
                            pool.tensor_tensor(blk, blk, after[:], ALU.mult).then_inc(s.masked, 1)
            release(s)
        vctx.close()

        def attention_tail(phase, weights, out_tile, finish):
            w1, w2, w3, b1, b3, ng, nb, b2, aff = weights
            FC = w3.shape[1]
            OC = HD // P
            with ExitStack() as c:
                ost = sb(phase + "ost", [P, J, HD], F32, c)
                oT = sb(phase + "oT", [P, OC, GW], F32, c)
                xb = sb(phase + "xb", [P, J, D], F32, c)
                x1 = sb(phase + "x1", [P, J, D], F32, c)
                x1c = sb(phase + "x1c", [P, J, D], F32, c)
                z = sb(phase + "z", [P, J, D], F32, c)
                zT = sb(phase + "zT", [P, KD, GW], F32, c)
                hT = sb(phase + "hT", [P, FC, GW], F32, c)
                y = sb(phase + "y", [P, J, D], F32, c)
                tps = [ps(f"{phase}tps{i}", [P, GW], c) for i in range(4)]
                p1 = [ps(f"{phase}p1{i}", [P, 2, D], c) for i in range(2)]
                p3 = [ps(f"{phase}p3{i}", [P, 2, D], c) for i in range(2)]
                NLN = 2 if finish == "norm" else 1

                s = signals(phase, LN + " staged base_done oT_dve oT_act oT_turned p1_done x1_done "
                            "z_done zT_turned zT_done h_done gelu_done sum1 sum2 p3_done y_done scaled x_out")
                with nc.Block() as block:
                    def steps(e, first, step):
                        first(0)
                        with e.Fori(0, G - 1, 1) as g:
                            step(g, True)
                        step(G - 1, False)

                    @block.gpsimd
                    def _(pool):
                        def first(g):
                            wait_apart(pool, s.oT_turned, 1 + g * OC)
                            for j in range(J):
                                src = out_tile(g * J + j)
                                dst = ost[:, j, :]
                                if len(src.shape) == 3:
                                    dst = dst.rearrange("p (h d) -> p h d", h=src.shape[1])
                                pool.tensor_copy(dst, src).then_inc(s.staged, 1)
                            wait_apart(pool, s.x1_done, 1 + g * 2)
                            for j in range(J):
                                pool.tensor_tensor(xb[:, j, :], x0res[:, g * J + j, :], b1[:], ALU.add).then_inc(s.base_done, 1)

                        def step(g, more):
                            wait_apart(pool, s.x1_done, 1 + g * 2 + 2)
                            wait_apart(pool, s.y_done, 1 + g * 2)
                            for j in range(J):
                                pool.tensor_tensor(x1c[:, j, :], x1[:, j, :], x0res[:, g * J + j, :], ALU.add).then_inc(s.sum1, 1)
                            for j in range(J):
                                wait_apart(pool, s.sum1, 1 + g * J + j + 1)
                                pool.tensor_tensor(x1c[:, j, :], x1c[:, j, :], b3[:], ALU.add).then_inc(s.sum2, 1)
                            if more:
                                first(g + 1)
                            if finish == "norm":
                                for j in range(J):
                                    wait_apart(pool, s.ln_out, 1 + g * J + j + 1)
                                    pool.tensor_tensor(y[:, j, :], y[:, j, :], ng[:], ALU.mult).then_inc(s.scaled, 1)
                                    wait_apart(pool, s.scaled, 1 + g * J + j + 1)
                                    pool.tensor_tensor(x0res[:, g * J + j, :], y[:, j, :], nb[:], ALU.add).then_inc(s.x_out, 1)

                        if phase == "t1":
                            first(0)
                            for g in range(G):
                                step(g, g + 1 < G)
                        else:
                            steps(pool, first, step)

                    @block.vector
                    def _(dve):
                        def first(g):
                            dve.wait_ge(s.p1_done, 1 + g * J)
                            for m in range(2):
                                dve.wait_ge(s.oT_turned, 1 + g * OC + m + 1)
                                dve.tensor_copy(oT[:, m, :], tps[m][:]).then_inc(s.oT_dve, 1)
                            dve.wait_ge(s.base_done, 1 + g * J + J)
                            dve.wait_ge(s.sum1, 1 + g * J)
                            for q in range(2):
                                dve.wait_ge(s.p1_done, 1 + g * J + 2 * q + 2)
                                dve.tensor_tensor(x1[:, 2 * q:2 * q + 2, :], p1[q][:], xb[:, 2 * q:2 * q + 2, :],
                                                  ALU.add).then_inc(s.x1_done, 1)
                            dve.wait_ge(s.x1_done, 1 + g * 2 + 2)
                            dve.wait_ge(s.zT_turned, 1 + g * KD)
                            n = g * NLN if isinstance(g, int) else (g * NLN - (NLN - 1))
                            ln_vector(dve, s, n, lambda j: x1[:, j, :], lambda j: z[:, j, :], s.z_done)

                        def step(g, more):
                            if more:
                                first(g + 1)
                            dve.wait_ge(s.sum2, 1 + g * J + J)
                            dve.wait_ge(s.x_out, 1 + g * J)
                            for q in range(2):
                                dve.wait_ge(s.p3_done, 1 + g * J + 2 * q + 2)
                                dve.tensor_tensor(y[:, 2 * q:2 * q + 2, :], p3[q][:], x1c[:, 2 * q:2 * q + 2, :],
                                                  ALU.add).then_inc(s.y_done, 1)
                            dve.wait_ge(s.y_done, 1 + g * 2 + 2)
                            if finish == "norm":
                                ln_vector(dve, s, g * 2 + (2 if more else 1), lambda j: y[:, j, :], lambda j: y[:, j, :])
                            else:
                                for j in range(J):
                                    dve.scalar_tensor_tensor(out=xres[:, g * J + j, :], in0=y[:, j, :], scalar=gate[:, 0:1],
                                                             in1=xres[:, g * J + j, :], op0=ALU.mult,
                                                             op1=ALU.add).then_inc(s.x_out, 1)

                        steps(dve, first, step)

                    @block.scalar
                    def _(act):
                        def first(g):
                            act.wait_ge(s.p1_done, 1 + g * J)
                            for m in range(2, 4):
                                act.wait_ge(s.oT_turned, 1 + g * OC + m + 1)
                                act.copy(oT[:, m, :], tps[m][:]).then_inc(s.oT_act, 1)
                            n = g * NLN if isinstance(g, int) else (g * NLN - (NLN - 1))
                            ln_scalar(act, s, n)

                        def step(g, more):
                            act.wait_ge(s.h_done, 1 + g * FC)
                            for k in range(KD):
                                act.wait_ge(s.zT_turned, 1 + g * KD + k + 1)
                                act.activation(zT[:, k, :], tps[k][:], ACT.Identity, bias=aff[:, 1, k:k + 1],
                                               scale=aff[:, 0, k:k + 1]).then_inc(s.zT_done, 1)
                            act.wait_ge(s.p3_done, 1 + g * J)
                            for f in range(FC):
                                act.wait_ge(s.h_done, 1 + g * FC + f + 1)
                                act.activation(hT[:, f, :], tps[2 + f % 2][:], ACT.Gelu,
                                               bias=b2[:, f:f + 1]).then_inc(s.gelu_done, 1)
                            if more:
                                first(g + 1)
                            if finish == "norm":
                                ln_scalar(act, s, g * 2 + (2 if more else 1))

                        steps(act, first, step)

                    @block.tensor
                    def _(pe):
                        def first(g):
                            pe.wait_ge(s.staged, 1 + g * J + J)
                            pe.wait_ge(s.zT_done, 1 + g * KD)
                            pe.wait_ge(s.gelu_done, 1 + g * FC)
                            for m in range(OC):
                                for j in range(J):
                                    mm = pe.transpose(tps[m][:, j * P:(j + 1) * P], ost[:, j, m * P:(m + 1) * P], ident[:])
                                mm.then_inc(s.oT_turned, 1)
                            pe.wait_ge(s.oT_dve, 1 + g * 2 + 2)
                            pe.wait_ge(s.oT_act, 1 + g * 2 + 2)
                            pe.wait_ge(s.x1_done, 1 + g * 2)
                            for j in range(J):
                                for m in range(OC):
                                    mm = pe.matmul(p1[j // 2][:, j % 2, :], oT[:, m, j * P:(j + 1) * P], w1[:, m, :],
                                                   start=(m == 0), stop=(m == OC - 1))
                                mm.then_inc(s.p1_done, 1)

                        def step(g, more):
                            pe.wait_ge(s.z_done, 1 + g * J + J)
                            for k in range(KD):
                                for j in range(J):
                                    mm = pe.transpose(tps[k][:, j * P:(j + 1) * P], z[:, j, k * P:(k + 1) * P], ident[:])
                                mm.then_inc(s.zT_turned, 1)
                            pe.wait_ge(s.zT_done, 1 + g * KD + KD)
                            for f in range(FC):
                                if f >= 2:
                                    pe.wait_ge(s.gelu_done, 1 + g * FC + f - 1)
                                for k in range(KD):
                                    mm = pe.matmul(tps[2 + f % 2][:], w2[:, k, f * P:(f + 1) * P], zT[:, k, :],
                                                   start=(k == 0), stop=(k == KD - 1))
                                mm.then_inc(s.h_done, 1)
                            pe.wait_ge(s.gelu_done, 1 + g * FC + FC)
                            if more:
                                first(g + 1)
                            pe.wait_ge(s.y_done, 1 + g * 2)
                            for j in range(J):
                                for f in range(FC):
                                    mm = pe.matmul(p3[j // 2][:, j % 2, :], hT[:, f, j * P:(j + 1) * P], w3[:, f, :],
                                                   start=(f == 0), stop=(f == FC - 1))
                                mm.then_inc(s.p3_done, 1)

                        steps(pe, first, step)
                release(s)

        attention_tail("t1", t1_weights, lambda t: ores[:, t // TPB * H1:(t // TPB + 1) * H1, t % TPB, :], "norm")
        t1ctx.close()


        CT, CD = io["ctx_512"].shape[1:]
        ores_flat = ores[:].rearrange("p h i d -> p (h i d)")

        def cross_attention(phase, H, DK, src, x_affine, y_affine, wq_ap, wk_ap, wv_ap, biases, scale, ahead):
            W = H * DK
            MC = W // P
            HQ = P // DK
            NW = HQ * CT
            NP2 = H // 2
            with ExitStack() as c:
                wq = sb(phase + "wq", [P, KD, W], F32, c)
                wk = sb(phase + "wk", [P, W], F32, c)
                wv = sb(phase + "wv", [P, W], F32, c)
                aff = sb(phase + "aff", [P, 2, KD], F32, c)
                yaff = sb(phase + "yaff", [P, 2], F32, c)
                bq = sb(phase + "bq", [P, MC], F32, c)
                bk = sb(phase + "bk", [P, MC], F32, c)
                bv = sb(phase + "bv", [P, W], F32, c)
                y = sb(phase + "y", [P, CD], F32, c)
                yn = sb(phase + "yn", [P, CD], F32, c)
                yT = sb(phase + "yT", [P, P], F32, c)
                ydup = sb(phase + "ydup", [P, B, 2, CT], F32, c)
                hmask = sb(phase + "hmask", [P, HQ], F32, c)
                vmask = sb(phase + "vmask", [P, 2], F32, c)
                kT = sb(phase + "kT", [P, MC, P], F32, c)
                kblk = sb(phase + "kblk", [P, B, MC, HQ, CT], F32, c)
                v = sb(phase + "v", [P, B, W], F32, c)
                vblk = sb(phase + "vblk", [P, B, NP2, 2, DK], F32, c)
                z = sb(phase + "z", [P, J, D], F32, c)
                xT = sb(phase + "xT", [P, KD, GW], F32, c)
                qT = sb(phase + "qT", [P, MC, GW], F32, c)
                nmax = sb(phase + "nmax", [P, 2, H], F32, c)
                rsum = sb(phase + "rsum", [P, 2, H], F32, c)
                rinv = sb(phase + "rinv", [P, 2, H], F32, c)
                prob = sb(phase + "prob", [P, 2, H * CT], F32, c)
                pT = sb(phase + "pT", [P, 2, NP2 * P // 2], F32, c)
                sps = [ps(f"{phase}s{i}", [P, 1024], c) for i in range(2)]
                tps = [ps(f"{phase}t{i}", [P, GW], c) for i in range(2)]
                ops = [ps(f"{phase}o{i}", [P, GW], c) for i in range(2)]

                s = signals(phase + "c", "y_in w_in zeroed hmask_one hmask_done step")
                with nc.Block() as block:
                    @block.sync
                    def _(sp):
                        sp.dma_start(y[:], io["ctx_512"].rearrange("b t c -> (b t) c")).then_inc(s.y_in, 16)
                        sp.dma_start(wk[:], wk_ap).then_inc(s.w_in, 16)
                        sp.dma_start(wv[:], wv_ap).then_inc(s.w_in, 16)
                        sp.dma_start(wq[:], wq_ap.rearrange("(k p) n -> p k n", p=P)).then_inc(s.w_in, 16)
                        with nc.allow_non_contiguous_dma(reason="small vectors by channel"):
                            if x_affine:
                                sp.dma_start(aff[:, 0, :], chan(x_affine[0])).then_inc(s.w_in, 16)
                                sp.dma_start(aff[:, 1, :], chan(x_affine[1])).then_inc(s.w_in, 16)
                                sp.dma_start(yaff[:, 0:1], chan(y_affine[0])).then_inc(s.w_in, 16)
                                sp.dma_start(yaff[:, 1:2], chan(y_affine[1])).then_inc(s.w_in, 16)
                            if biases:
                                sp.dma_start(bq[:], chan(biases[0])).then_inc(s.w_in, 16)
                                sp.dma_start(bk[:], chan(biases[1])).then_inc(s.w_in, 16)
                        if biases:
                            sp.dma_start(bv[:], rows(biases[2])).then_inc(s.w_in, 16)
                    NW_IN = 48 + (64 if x_affine else 0) + (48 if biases else 0)

                    @block.gpsimd
                    def _(pool):
                        pool.memset(hmask[:], 1.0).then_inc(s.zeroed, 1)
                        pool.memset(vmask[:], 1.0).then_inc(s.zeroed, 1)
                        pool.wait_ge(s.zeroed, 1 + 2)
                        for mask, width, n in ((hmask, DK, HQ), (vmask, CT, 2)):
                            pool.affine_select(out=mask[:], in_=mask[:], compare_op=ALU.is_ge, fill=0.0, base=0,
                                               pattern=[[-width, n]], channel_multiplier=1).then_inc(s.hmask_one, 1)
                        pool.wait_ge(s.hmask_one, 1 + 2)
                        for mask, width, n in ((hmask, DK, HQ), (vmask, CT, 2)):
                            pool.affine_select(out=mask[:], in_=mask[:], compare_op=ALU.is_ge, fill=0.0, base=width - 1,
                                               pattern=[[width, n]], channel_multiplier=-1).then_inc(s.hmask_done, 1)

                    @block.vector
                    def _(dve):
                        dve.wait_ge(s.y_in, 1 + 16)
                        if y_affine:
                            dve.bn_stats(stats[:, 0, :], y[:]).then_inc(s.step, 1)
                            dve.wait_ge(s.step, 1 + 1)
                            dve.bn_aggr(moments[:, 0, :], stats[:, 0, :]).then_inc(s.step, 1)
                            dve.wait_ge(s.step, 1 + 3)
                            dve.reciprocal(rstd[:, 0:1], std[:, 0:1]).then_inc(s.step, 1)
                            dve.wait_ge(s.step, 1 + 4)
                            dve.tensor_scalar(yn[:], y[:], moments[:, 0, 0:1], rstd[:, 0:1],
                                              ALU.subtract, ALU.mult).then_inc(s.step, 1)
                        else:
                            dve.tensor_copy(yn[:], y[:]).then_inc(s.step, 5)
                        dve.wait_ge(s.step, 1 + 7)
                        dve.tensor_copy(ydup[:], yT[:].rearrange("p (b t) -> p b t", b=B).unsqueeze(2)
                                        .to_broadcast([P, B, 2, CT])).then_inc(s.step, 1)
                        dve.wait_ge(s.step, 1 + 9)
                        dve.wait_ge(s.w_in, 1 + NW_IN)
                        for b in range(B):
                            if biases:
                                ins = dve.tensor_tensor(v[:, b, :], ops[b][:, 0:W], bv[:], ALU.add)
                            else:
                                ins = dve.tensor_copy(v[:, b, :], ops[b][:, 0:W])
                        ins.then_inc(s.step, 1)
                        dve.wait_ge(s.step, 1 + 11)
                        dve.wait_ge(s.hmask_done, 1 + 2)
                        for b in range(B):
                            for m in range(MC):
                                dve.tensor_tensor(kblk[:, b, m, :, :],
                                                  kT[:, m, b * CT:(b + 1) * CT].unsqueeze(1).to_broadcast([P, HQ, CT]),
                                                  hmask[:].unsqueeze(2).to_broadcast([P, HQ, CT]), ALU.mult)
                            ins = dve.tensor_tensor(vblk[:, b, :, :, :],
                                                    v[:, b, :].rearrange("p (r q d) -> p r q d", r=NP2, q=2),
                                                    vmask[:].unsqueeze(1).unsqueeze(3).to_broadcast([P, NP2, 2, DK]),
                                                    ALU.mult)
                        ins.then_inc(s.step, 1)

                    @block.scalar
                    def _(act):
                        if y_affine:
                            act.wait_ge(s.step, 1 + 2)
                            act.activation(std[:, 0:1], moments[:, 0, 1:2], ACT.Sqrt, bias=eps[:, 0:1]).then_inc(s.step, 1)
                        act.wait_ge(s.step, 1 + 6)
                        act.wait_ge(s.w_in, 1 + NW_IN)
                        if y_affine:
                            act.activation(yT[:], tps[0][:, 0:P], ACT.Identity, bias=yaff[:, 1:2],
                                           scale=yaff[:, 0:1]).then_inc(s.step, 1)
                        else:
                            act.copy(yT[:], tps[0][:, 0:P]).then_inc(s.step, 1)
                        act.wait_ge(s.step, 1 + 10)
                        for m in range(MC):
                            if biases:
                                ins = act.activation(kT[:, m, :], tps[1][:, m * P:(m + 1) * P], ACT.Identity, bias=bk[:, m:m + 1])
                            else:
                                ins = act.copy(kT[:, m, :], tps[1][:, m * P:(m + 1) * P])
                        ins.then_inc(s.step, 1)

                    @block.tensor
                    def _(pe):
                        pe.wait_ge(s.step, 1 + 5)
                        pe.transpose(tps[0][:, 0:P], yn[:], ident[:]).then_inc(s.step, 1)
                        pe.wait_ge(s.step, 1 + 8)
                        pe.wait_ge(s.w_in, 1 + NW_IN)
                        for m in range(MC):
                            pe.matmul(tps[1][:, m * P:(m + 1) * P], wk[:, m * P:(m + 1) * P], yT[:], start=True, stop=True)
                        for b in range(B):
                            mm = pe.matmul(ops[b][:, 0:W], ydup[:, b, :, :].rearrange("p r t -> p (r t)"), wv[:],
                                           start=True, stop=True)
                        mm.then_inc(s.step, 1)
                release(s)

                s = signals(phase, LN + " zT_turned xT_done q_done qT_done scores max_done prob_ready exp_done "
                            "sum_done rinv_done p_turned pT_done pv_done out_done next_in")

                def steps(e, first, step):
                    first(0)
                    with e.Fori(0, G - 1, 1) as g:
                        step(g, True)
                    step(G - 1, False)

                with nc.Block() as block:
                    @block.sync
                    def _(sp):
                        sp.wait_ge(s.next_in, 1 + ahead(sp, s.next_in))

                    @block.vector
                    def _(dve):
                        def top(t, j):
                            dve.wait_ge(s.scores, 1 + t + 1)
                            dve.tensor_reduce(nmax[:, j % 2, :], sps[j % 2][:].rearrange("p (h t) -> p h t", h=H),
                                              X, ALU.max, negate=True).then_inc(s.max_done, 1)
                            dve.wait_ge(s.max_done, 1 + t + 1)
                            dve.wait_ge(s.p_turned, 1 + t - (1 if j >= 2 else j))
                            dve.tensor_tensor(prob[:, j % 2, :].rearrange("p (h t) -> p h t", h=H),
                                              sps[j % 2][:].rearrange("p (h t) -> p h t", h=H),
                                              nmax[:, j % 2, :].unsqueeze(2).to_broadcast([P, H, CT]),
                                              ALU.add).then_inc(s.prob_ready, 1)

                        def sums(t, j):
                            dve.wait_ge(s.exp_done, 1 + t + 1)
                            dve.tensor_reduce(rsum[:, j % 2, :], prob[:, j % 2, :].rearrange("p (h t) -> p h t", h=H),
                                              X, ALU.add).then_inc(s.sum_done, 1)
                            dve.wait_ge(s.sum_done, 1 + t + 1)
                            dve.reciprocal(rinv[:, j % 2, :], rsum[:, j % 2, :]).then_inc(s.rinv_done, 1)

                        def outputs(t, j):
                            dve.wait_ge(s.rinv_done, 1 + t + 1)
                            dve.wait_ge(s.pv_done, 1 + t + 1)
                            dve.tensor_tensor(ores_flat[:, bass.ts(t, W)].rearrange("p (h d) -> p h d", h=H),
                                              ops[j % 2][:, 0:W].rearrange("p (h d) -> p h d", h=H),
                                              rinv[:, j % 2, :].unsqueeze(2).to_broadcast([P, H, DK]),
                                              ALU.mult).then_inc(s.out_done, 1)

                        def norm(g):
                            dve.wait_ge(s.zT_turned, 1 + g * KD)
                            ln_vector(dve, s, g, lambda j: src(g * J + j), lambda j: z[:, j, :])

                        def step(g, more):
                            top(g * J, 0)
                            top(g * J + 1, 1)
                            for j in range(J):
                                sums(g * J + j, j)
                                if j + 2 < J:
                                    top(g * J + j + 2, j + 2)
                                if j == J - 1 and more:
                                    norm(g + 1)
                                outputs(g * J + j, j)

                        steps(dve, norm, step)

                    @block.scalar
                    def _(act):
                        def step(g, more):
                            act.wait_ge(s.q_done, 1 + g * MC)
                            for k in range(KD):
                                act.wait_ge(s.zT_turned, 1 + g * KD + k + 1)
                                if x_affine:
                                    act.activation(xT[:, k, :], tps[k][:], ACT.Identity, bias=aff[:, 1, k:k + 1],
                                                   scale=aff[:, 0, k:k + 1]).then_inc(s.xT_done, 1)
                                else:
                                    act.copy(xT[:, k, :], tps[k][:]).then_inc(s.xT_done, 1)
                            act.wait_ge(s.scores, 1 + g * J)
                            for m in range(MC):
                                act.wait_ge(s.q_done, 1 + g * MC + m + 1)
                                if biases:
                                    act.activation(qT[:, m, :], sps[m // 2][:, (m % 2) * 512:(m % 2) * 512 + 512], ACT.Identity,
                                                   bias=bq[:, m:m + 1]).then_inc(s.qT_done, 1)
                                else:
                                    act.copy(qT[:, m, :], sps[m // 2][:, (m % 2) * 512:(m % 2) * 512 + 512]).then_inc(s.qT_done, 1)

                            def evacuate(j):
                                act.wait_ge(s.pv_done, 1 + g * J + j)
                                for q in range(2):
                                    act.wait_ge(s.p_turned, 1 + g * J + j + 1)
                                    act.copy(pT[:, q, :], tps[q][:]).then_inc(s.pT_done, 1)

                            for j in range(J):
                                act.wait_ge(s.prob_ready, 1 + g * J + j + 1)
                                act.activation(prob[:, j % 2, :], prob[:, j % 2, :], ACT.Exp, scale=scale).then_inc(s.exp_done, 1)
                                if j > 0:
                                    evacuate(j - 1)
                            evacuate(J - 1)
                            if more:
                                ln_scalar(act, s, g + 1)

                        steps(act, lambda g: ln_scalar(act, s, g), step)

                    @block.tensor
                    def _(pe):
                        with pe.Fori(0, B, 1) as b:
                            for gg in range(G // B):
                                g = b * (G // B) + gg
                                pe.wait_ge(s.ln_out, 1 + g * J + J)
                                pe.wait_ge(s.pT_done, 1 + g * J * 2)
                                for k in range(KD):
                                    for j in range(J):
                                        mm = pe.transpose(tps[k][:, j * P:(j + 1) * P], z[:, j, k * P:(k + 1) * P], ident[:])
                                    mm.then_inc(s.zT_turned, 1)
                                pe.wait_ge(s.xT_done, 1 + g * KD + KD)
                                pe.wait_ge(s.prob_ready, 1 + g * J)
                                for m in range(MC):
                                    for k in range(KD):
                                        mm = pe.matmul(sps[m // 2][:, (m % 2) * 512:(m % 2) * 512 + 512],
                                                       wq[:, k, m * P:(m + 1) * P], xT[:, k, :], start=(k == 0), stop=(k == KD - 1))
                                    mm.then_inc(s.q_done, 1)
                                pe.wait_ge(s.qT_done, 1 + g * MC + MC)

                                def score(j):
                                    if j >= 2:
                                        pe.wait_ge(s.prob_ready, 1 + g * J + j - 1)
                                    for m in range(MC):
                                        mm = pe.matmul(sps[j % 2][:, m * NW:(m + 1) * NW], qT[:, m, j * P:(j + 1) * P],
                                                       kblk[:, b, m, :, :].rearrange("p q t -> p (q t)"), start=True, stop=True)
                                    mm.then_inc(s.scores, 1)

                                def turn(j):
                                    pe.wait_ge(s.exp_done, 1 + g * J + j + 1)
                                    pe.wait_ge(s.pT_done, 1 + (g * J + j) * 2)
                                    for r in range(NP2):
                                        mm = pe.transpose(tps[r // 4][:, (r % 4) * P:(r % 4 + 1) * P],
                                                          prob[:, j % 2, r * P:(r + 1) * P], ident[:])
                                    mm.then_inc(s.p_turned, 1)

                                def weigh(j):
                                    pe.wait_ge(s.pT_done, 1 + (g * J + j) * 2 + 2)
                                    pe.wait_ge(s.out_done, 1 + g * J + j - (1 if j >= 2 else j))
                                    for r in range(NP2):
                                        mm = pe.matmul(ops[j % 2][:, r * 2 * DK:(r + 1) * 2 * DK],
                                                       pT[:, r // 4, (r % 4) * P:(r % 4 + 1) * P],
                                                       vblk[:, b, r, :, :].rearrange("p q d -> p (q d)"), start=True, stop=True)
                                    mm.then_inc(s.pv_done, 1)

                                score(0)
                                score(1)
                                for j in range(J):
                                    turn(j)
                                    if j + 2 < J:
                                        score(j + 2)
                                    weigh(j)
                release(s)

        t2ctx = ExitStack()
        t2_weights, t2_ahead = tail_weights("t2", "L0_xattn_a2_", t2ctx)
        cross_attention("x2", H1, D1, lambda t: x0res[:, t, :], (io["L0_xattn_a2_lnx_g"], io["L0_xattn_a2_lnx_b"]),
                        (io["L0_xattn_a2_lny_g"], io["L0_xattn_a2_lny_b"]), io["a2_wq_flat"], io["a2_wk_flat"],
                        io["a2_wv_flat"], None, SCALE1, t2_ahead)
        attention_tail("t2", t2_weights, lambda t: ores_flat[:, bass.ts(t, HD)], "gate")
        t2ctx.close()

        attn.close()

        DEPTH, _, INNER3 = io["L0_ffn_wqkv"].shape
        HL, DL = INNER3 // 3 // io["L0_ffn_q_scale"].shape[1], io["L0_ffn_q_scale"].shape[1]
        INNER = HL * DL
        HID = io["L0_ffn_w2"].shape[1]
        FCH = [(f * P, min(P, HID - f * P)) for f in range(-(-HID // P))]
        NEG = -1e30

        s = signals("l0", LN)
        with nc.Block() as block:
            @block.vector
            def _(dve):
                with dve.Fori(0, G, 1) as g:
                    ln_vector(dve, s, g, lambda j: xres[:, g * J + j, :], lambda j: x0res[:, g * J + j, :])
                    dve.wait_ge(s.ln_out, 1 + g * J + J)

            @block.scalar
            def _(act):
                with act.Fori(0, G, 1) as g:
                    ln_scalar(act, s, g)
        release(s)

        def local_attention(l, ahead):
            U = 4
            ph = f"la{l}"
            with ExitStack() as c:
                wqkv = sb(ph + "w", [P, KD, 3, INNER], F32, c)
                wo = sb(ph + "wo", [P, INNER // P, D], F32, c)
                scl = sb(ph + "scl", [P, 2, DL], F32, c)
                cosr = sb(ph + "cos", [P, NT, 2, DL], F32, c)
                sinr = sb(ph + "sin", [P, NT, 2, DL], F32, c)
                maskf = sb(ph + "mf", [P, 2, 2, P], F32, c)
                masks = sb(ph + "mb", [P, U, 2, 2 * P], BF16, c)
                masko = sb(ph + "mo", [P, 2, 2 * P], BF16, c)
                identb = sb(ph + "ib", [P, P], BF16, c)
                goes_on = sb(ph + "go", [P, U], F32, c)
                xst = sb(ph + "xst", [P, 2, D], F32, c)
                hx = sb(ph + "hx", [P, 2, 2 * P + 1], F32, c)
                sq = sb(ph + "sq", [P, 2 * INNER], F32, c)
                ssum = sb(ph + "ss", [P, 2 * HL], F32, c)
                norm = sb(ph + "nm", [P, 2 * HL], F32, c)
                rnorm = sb(ph + "rn", [P, 2 * HL], F32, c)
                qn = sb(ph + "qn", [P, 2 * HL, DL], F32, c)
                qc = sb(ph + "qc", [P, 2 * HL, DL], F32, c)
                qs = sb(ph + "qs", [P, 2 * HL, DL], F32, c)
                qr = sb(ph + "qr", [P, 2 * HL, DL], F32, c)
                qT = sb(ph + "qT", [P, 2, HL // 2, P], F32, c)
                kT = sb(ph + "kT", [P, U, HL // 2, P], F32, c)
                v = sb(ph + "v", [P, U, INNER], F32, c)
                nmax = sb(ph + "nx", [P, HL], F32, c)
                rsum = sb(ph + "rs", [P, HL], F32, c)
                rinv = sb(ph + "ri", [P, HL], F32, c)
                prob = sb(ph + "pr", [P, HL, 2 * P], F32, c)
                pT = sb(ph + "pT", [P, HL, 2 * P], F32, c)
                o = sb(ph + "o", [P, INNER], F32, c)
                oT = sb(ph + "oT", [P, INNER], F32, c)
                bz = ps(ph + "bz", [P, 512], c)
                bqk = ps(ph + "bqk", [P, 2 * INNER], c)
                bv = ps(ph + "bv", [P, INNER], c)
                bs = ps(ph + "bs", [P, 2048], c)
                order = [4 * (r // 2) + 2 * x + r % 2 for r in range(4) for x in range(2)]

                s = signals(ph, "next_in wo_in w_in tab_in built1 built2 built3 tab1 staged x_turned h_copied carried qk_done "
                            "v_ready squared v_done ssum_done norm_done clipped rnorm_done normed cos_done sin_done "
                            "rotated qk_turned qT_done kT_done scores max_done exp_done rinv_done p_turned pT_act pT_dve "
                            "pv_done o_done o_turned oT_done wo_done x_done")

                def steps(e, begin, step):
                    begin()
                    with e.Fori(0, NT // U - 1, 1) as it:
                        for u in range(U):
                            step(it * U + u, u, 3, it)
                    for u in range(U):
                        step(NT - U + u, u, U - 1 - u, NT // U - 1)

                with nc.Block() as block:
                    @block.sync
                    def _(sp):
                        sp.dma_start(wqkv[:], io["L0_ffn_wqkv"][l].rearrange("(k p) (t n) -> p k t n", p=P, t=3)).then_inc(s.w_in, 16)
                        for n, name in enumerate(["L0_ffn_q_scale", "L0_ffn_k_scale"]):
                            sp.dma_start(scl[:, n, :], rows(io[name][l])).then_inc(s.tab_in, 16)
                        for b in range(B):
                            for tab, name in ((cosr, "rotary_cos"), (sinr, "rotary_sin")):
                                sp.dma_start(tab[:, b * TPB:(b + 1) * TPB, :, :],
                                             io[name].rearrange("(t p) q d -> p t q d", p=P)).then_inc(s.tab_in, 16)
                        for slot, head in enumerate(order):
                            sp.dma_start(wo[DL * (slot % 2):DL * (slot % 2) + DL, slot // 2, :],
                                         io["L0_ffn_wo"][l, head * DL:(head + 1) * DL, :]).then_inc(s.wo_in, 16)
                        sp.wait_ge(s.next_in, 1 + ahead(sp, s.next_in))

                    @block.gpsimd
                    def _(pool):
                        pool.memset(maskf[:], 0.0).then_inc(s.built1, 1)
                        pool.memset(goes_on[:], 1.0).then_inc(s.built1, 1)
                        pool.memset(kT[:, U - 1, :, :], 0.0).then_inc(s.built1, 1)
                        pool.memset(v[:, U - 1, :], 0.0).then_inc(s.built1, 1)
                        pool.memset(hx[:, 1, :], 0.0).then_inc(s.built1, 1)
                        pool.wait_ge(s.built1, 1 + 5)
                        pool.memset(maskf[:, 0, 0, :], NEG).then_inc(s.built2, 1)
                        for q in range(0, U, 2):
                            pool.memset(goes_on[:, q:q + 1], 0.0).then_inc(s.built2, 1)
                        pool.affine_select(out=maskf[:, 1, 0, :], in_=maskf[:, 1, 0, :], compare_op=ALU.is_ge, fill=NEG,
                                           base=0, pattern=[[1, P]], channel_multiplier=-1).then_inc(s.built2, 1)
                        for w in range(2):
                            pool.affine_select(out=maskf[:, w, 1, :], in_=maskf[:, w, 1, :], compare_op=ALU.is_ge, fill=NEG,
                                               base=0, pattern=[[-1, P]], channel_multiplier=1).then_inc(s.built2, 1)
                        pool.wait_ge(s.built2, 1 + 6)
                        pool.tensor_copy(identb[:], ident[:]).then_inc(s.built3, 1)
                        for x in range(2):
                            for q in range(U):
                                pool.tensor_copy(masks[:, q, x, :], maskf[:, q % 2, :, :].rearrange("p a t -> p (a t)")).then_inc(s.built3, 1)
                            pool.tensor_copy(masko[:, x, :], maskf[:, 1, :, :].rearrange("p a t -> p (a t)")).then_inc(s.built3, 1)

                        def stage(t, u):
                            if not (isinstance(t, int) and t == 0):
                                wait_apart(pool, s.x_turned, 1 + t - 1)
                            pool.tensor_copy(xst[:, u % 2, :], x0res[:, t, :]).then_inc(s.staged, 1)

                        def sines(t, u):
                            wait_apart(pool, s.normed, 1 + t + 1)
                            wait_apart(pool, s.rotated, 1 + t)
                            for q in range(2):
                                for a in range(2):
                                    pool.tensor_tensor(qs[:, q * HL:(q + 1) * HL, a * 32:(a + 1) * 32],
                                                       qn[:, q * HL:(q + 1) * HL, (1 - a) * 32:(2 - a) * 32],
                                                       sinr[:, t, q, a * 32:(a + 1) * 32].unsqueeze(1).to_broadcast([P, HL, 32]),
                                                       ALU.mult).then_inc(s.sin_done, 1)

                        def begin():
                            stage(0, 0)
                            stage(1, 1)
                            stage(2, 2)
                            wait_apart(pool, s.tab1, 1 + 6)
                            sines(0, 0)

                        def step(t, u, more, it):
                            if more == 3:
                                stage(t + 3, (u + 3) % U)
                            if more:
                                sines(t + 1, (u + 1) % U)

                        steps(pool, begin, step)

                    @block.vector
                    def _(dve):
                        dve.wait_ge(s.built1, 1 + 5)
                        dve.wait_ge(s.built2, 1 + 6)

                        def shifted(t, u, it):
                            dve.wait_ge(s.x_turned, 1 + t + 1)
                            dve.wait_ge(s.carried, 1 + t)
                            dve.tensor_copy(hx[:, u % 2, 0:P], bz[:, 0:P]).then_inc(s.h_copied, 1)
                            dve.tensor_copy(hx[:, u % 2, P + 1:2 * P + 1], bz[:, P:2 * P]).then_inc(s.h_copied, 1)
                            if u == 0:
                                dve.tensor_scalar(hx[:, 0, P:P + 1], hx[:, 1, 2 * P:2 * P + 1], goes_on[:, bass.ds(it, 1)],
                                                  None, ALU.mult).then_inc(s.carried, 1)
                            else:
                                dve.tensor_copy(hx[:, u % 2, P:P + 1], hx[:, 1 - u % 2, 2 * P:2 * P + 1]).then_inc(s.carried, 1)

                        def squares_sum(t):
                            dve.wait_ge(s.squared, 1 + t + 1)
                            dve.tensor_reduce(ssum[:], sq[:].rearrange("p (h d) -> p h d", d=DL), X, ALU.add).then_inc(s.ssum_done, 1)

                        def normalise(t):
                            dve.wait_ge(s.norm_done, 1 + t + 1)
                            dve.tensor_scalar(rnorm[:], norm[:], 1e-12, None, ALU.max).then_inc(s.clipped, 1)
                            dve.wait_ge(s.clipped, 1 + t + 1)
                            dve.reciprocal(rnorm[:], rnorm[:]).then_inc(s.rnorm_done, 1)
                            dve.wait_ge(s.rnorm_done, 1 + t + 1)
                            dve.wait_ge(s.sin_done, 1 + t * 4)
                            dve.tensor_tensor(qn[:], bqk[:].rearrange("p (h d) -> p h d", d=DL),
                                              rnorm[:].unsqueeze(2).to_broadcast([P, 2 * HL, DL]), ALU.mult).then_inc(s.normed, 1)

                        def rotary(t):
                            dve.wait_ge(s.normed, 1 + t + 1)
                            dve.tensor_tensor(qc[:].rearrange("p (q h) d -> p q h d", q=2),
                                              qn[:].rearrange("p (q h) d -> p q h d", q=2),
                                              cosr[:, t, :, :].unsqueeze(2).to_broadcast([P, 2, HL, DL]),
                                              ALU.mult).then_inc(s.cos_done, 1)
                            dve.wait_ge(s.cos_done, 1 + t + 1)
                            dve.wait_ge(s.sin_done, 1 + t * 4 + 4)
                            dve.wait_ge(s.qk_turned, 1 + t)
                            dve.tensor_tensor(qr[:], qc[:], qs[:], ALU.add).then_inc(s.rotated, 1)

                        def keys(t, u):
                            dve.wait_ge(s.qk_turned, 1 + t + 1)
                            dve.tensor_copy(kT[:, u, :, :].rearrange("p m t -> p (m t)"), bqk[:, INNER:2 * INNER]).then_inc(s.kT_done, 1)

                        def row_max(t):
                            dve.wait_ge(s.scores, 1 + t + 1)
                            dve.wait_ge(s.exp_done, 1 + t * 2)
                            dve.tensor_reduce(nmax[:], bs[:].rearrange("p (s t) -> p s t", s=HL), X, ALU.max,
                                              negate=True).then_inc(s.max_done, 1)

                        def begin():
                            shifted(0, 0, 0)
                            shifted(1, 1, 0)
                            dve.wait_ge(s.tab_in, 1 + 96)
                            for n in range(2):
                                dve.tensor_tensor(cosr[:, :, n, :], cosr[:, :, n, :],
                                                   scl[:, n, :].unsqueeze(1).to_broadcast([P, NT, DL]), ALU.mult).then_inc(s.tab1, 1)
                                for a in range(2):
                                    dve.tensor_tensor(sinr[:, :, n, a * 32:(a + 1) * 32], sinr[:, :, n, a * 32:(a + 1) * 32],
                                                       scl[:, n, (1 - a) * 32:(2 - a) * 32].unsqueeze(1).to_broadcast([P, NT, 32]),
                                                       ALU.mult).then_inc(s.tab1, 1)
                            dve.wait_ge(s.tab1, 1 + 6)
                            squares_sum(0)
                            normalise(0)
                            rotary(0)
                            keys(0, 0)
                            squares_sum(1)
                            row_max(0)

                        def step(t, u, more, it):
                            if more:
                                normalise(t + 1)
                            if more >= 2:
                                shifted(t + 2, (u + 2) % U, it + 1)
                            if more:
                                rotary(t + 1)
                            dve.wait_ge(s.p_turned, 1 + t * 2 + 2)
                            dve.tensor_copy(pT[:, HL // 2:HL, :].rearrange("p s t -> p (s t)"), bs[:, 1024:2048]).then_inc(s.pT_dve, 1)
                            if more:
                                keys(t + 1, (u + 1) % U)
                            dve.wait_ge(s.exp_done, 1 + t * 2 + 2)
                            dve.wait_ge(s.o_done, 1 + t)
                            dve.reciprocal(rinv[:], rsum[:]).then_inc(s.rinv_done, 1)
                            dve.wait_ge(s.rinv_done, 1 + t + 1)
                            dve.wait_ge(s.pv_done, 1 + t + 1)
                            dve.tensor_tensor(o[:].rearrange("p (s d) -> p s d", s=HL), bv[:].rearrange("p (s d) -> p s d", s=HL),
                                              rinv[:].unsqueeze(2).to_broadcast([P, HL, DL]), ALU.mult).then_inc(s.o_done, 1)
                            if more >= 2:
                                squares_sum(t + 2)
                            if more:
                                row_max(t + 1)
                            dve.wait_ge(s.wo_done, 1 + t + 1)
                            dve.tensor_tensor(x0res[:, t, :], bz[:, 0:D], x0res[:, t, :], ALU.add).then_inc(s.x_done, 1)

                        steps(dve, begin, step)

                    @block.scalar
                    def _(act):
                        def norms(t):
                            act.wait_ge(s.qk_done, 1 + t + 1)
                            act.wait_ge(s.ssum_done, 1 + t)
                            act.activation(sq[:], bqk[:], ACT.Square).then_inc(s.squared, 1)
                            act.wait_ge(s.ssum_done, 1 + t + 1)
                            act.activation(norm[:], ssum[:], ACT.Sqrt).then_inc(s.norm_done, 1)

                        def values(t, u):
                            act.wait_ge(s.v_ready, 1 + t + 1)
                            act.copy(v[:, u, :], bv[:]).then_inc(s.v_done, 1)

                        def queries(t, u):
                            act.wait_ge(s.qk_turned, 1 + t + 1)
                            act.copy(qT[:, u % 2, :, :].rearrange("p m t -> p (m t)"), bqk[:, 0:INNER]).then_inc(s.qT_done, 1)

                        def begin():
                            norms(0)
                            values(0, 0)
                            queries(0, 0)
                            norms(1)

                        def step(t, u, more, it):
                            act.wait_ge(s.max_done, 1 + t + 1)
                            act.wait_ge(s.p_turned, 1 + t * 2)
                            act.wait_ge(s.rinv_done, 1 + t)
                            for half in range(2):
                                for h in range(half * HL // 2, (half + 1) * HL // 2):
                                    ins = act.activation(prob[:, h, :], bs[:, h * 256:(h + 1) * 256], ACT.Exp,
                                                         bias=nmax[:, h:h + 1], accum_out=rsum[:, h:h + 1])
                                ins.then_inc(s.exp_done, 1)
                            if more:
                                values(t + 1, (u + 1) % U)
                            act.wait_ge(s.p_turned, 1 + t * 2 + 1)
                            act.copy(pT[:, 0:HL // 2, :].rearrange("p s t -> p (s t)"), bs[:, 0:1024]).then_inc(s.pT_act, 1)
                            if more:
                                queries(t + 1, (u + 1) % U)
                            act.wait_ge(s.o_turned, 1 + t + 1)
                            act.copy(oT[:], bz[:]).then_inc(s.oT_done, 1)
                            if more >= 2:
                                norms(t + 2)

                        steps(act, begin, step)

                    @block.tensor
                    def _(pe):
                        pe.wait_ge(s.w_in, 1 + 16)

                        def turn_x(t, u):
                            pe.wait_ge(s.staged, 1 + t + 1)
                            pe.wait_ge(s.h_copied, 1 + t * 2)
                            if not (isinstance(t, int) and t < 3):
                                pe.wait_ge(s.x_done, 1 + t - 2)
                            for k in range(KD):
                                mm = pe.transpose(bz[:, k * P:(k + 1) * P], xst[:, u % 2, k * P:(k + 1) * P], ident[:])
                            mm.then_inc(s.x_turned, 1)

                        def project(t, u, parts):
                            pe.wait_ge(s.carried, 1 + t + 1)
                            if 0 in parts:
                                pe.wait_ge(s.qT_done, 1 + t)
                                pe.wait_ge(s.kT_done, 1 + t)
                            else:
                                pe.wait_ge(s.v_done, 1 + t)
                            for n in parts:
                                dst = bqk[:, n * INNER:(n + 1) * INNER] if n < 2 else bv[:]
                                for k in range(KD):
                                    mm = pe.matmul(dst, hx[:, u % 2, k * P:(k + 1) * P], wqkv[:, k, n, :],
                                                   start=(k == 0), stop=(k == KD - 1))
                            mm.then_inc(s.qk_done if 0 in parts else s.v_ready, 1)

                        def turn_qk(t, u):
                            pe.wait_ge(s.rotated, 1 + t + 1)
                            for m in range(HL):
                                mm = pe.transpose(bqk[:, m * P:(m + 1) * P],
                                                  qr[:, 2 * m:2 * m + 2, :].rearrange("p h d -> p (h d)"), ident[:])
                            mm.then_inc(s.qk_turned, 1)

                        def score(t, u, it):
                            pe.wait_ge(s.qT_done, 1 + t + 1)
                            pe.wait_ge(s.kT_done, 1 + t + 1)
                            pe.wait_ge(s.pT_act, 1 + t)
                            pe.wait_ge(s.pT_dve, 1 + t)
                            for r in range(4):
                                mask = masks[:, it, :, :] if u == 0 else masko[:]
                                pe.matmul(bs[:, r * 512:(r + 1) * 512], identb[:], mask.rearrange("p x t -> p (x t)"),
                                          start=True, stop=False, skip_group_check=True)
                                for x in range(2):
                                    e, m = r % 2, 2 * (r // 2) + x
                                    for w, ring in enumerate(((u - 1) % U, u)):
                                        mm = pe.matmul(bs[:, r * 512 + x * 256 + w * P:r * 512 + x * 256 + (w + 1) * P],
                                                       qT[DL * e:DL * e + DL, u % 2, m, :], kT[DL * e:DL * e + DL, ring, m, :],
                                                       start=False, stop=True, skip_group_check=True)
                            mm.then_inc(s.scores, 1)

                        def begin():
                            turn_x(0, 0)
                            turn_x(1, 1)
                            project(0, 0, (0, 1))
                            project(0, 0, (2,))
                            turn_qk(0, 0)
                            project(1, 1, (0, 1))
                            pe.wait_ge(s.built3, 1 + 11)
                            score(0, 0, 0)
                            pe.wait_ge(s.wo_in, 1 + 16 * HL)
                            project(1, 1, (2,))
                            turn_x(2, 2)

                        def step(t, u, more, it):
                            for half in range(2):
                                pe.wait_ge(s.exp_done, 1 + t * 2 + half + 1)
                                for h in range(half * HL // 2, (half + 1) * HL // 2):
                                    for w in range(2):
                                        mm = pe.transpose(bs[:, h * 256 + w * P:h * 256 + (w + 1) * P],
                                                          prob[:, h, w * P:(w + 1) * P], ident[:])
                                mm.then_inc(s.p_turned, 1)
                            pe.wait_ge(s.v_done, 1 + t + (2 if more else 1))
                            for slot, head in enumerate(order):
                                if slot == 0:
                                    pe.wait_ge(s.pT_act, 1 + t + 1)
                                if slot == HL // 2:
                                    if more:
                                        turn_qk(t + 1, (u + 1) % U)
                                    pe.wait_ge(s.pT_dve, 1 + t + 1)
                                for w, ring in enumerate(((u - 1) % U, u)):
                                    mm = pe.matmul(bv[:, slot * DL:(slot + 1) * DL], pT[:, slot, w * P:(w + 1) * P],
                                                   v[:, ring, head * DL:(head + 1) * DL], start=(w == 0), stop=(w == 1))
                            mm.then_inc(s.pv_done, 1)
                            pe.wait_ge(s.o_done, 1 + t + 1)
                            pe.wait_ge(s.h_copied, 1 + 2 * (t + 3 if more >= 2 else NT))
                            for m in range(INNER // P):
                                mm = pe.transpose(bz[:, m * P:(m + 1) * P], o[:, m * P:(m + 1) * P], ident[:])
                            mm.then_inc(s.o_turned, 1)
                            if more >= 2:
                                project(t + 2, (u + 2) % U, (0, 1))
                            if more:
                                score(t + 1, (u + 1) % U, it + 1)
                            pe.wait_ge(s.oT_done, 1 + t + 1)
                            for m in range(INNER // P):
                                mm = pe.matmul(bz[:, 0:D], oT[:, m * P:(m + 1) * P], wo[:, m, :],
                                               start=(m == 0), stop=(m == INNER // P - 1))
                            mm.then_inc(s.wo_done, 1)
                            if more >= 2:
                                project(t + 2, (u + 2) % U, (2,))
                            if more == 3:
                                turn_x(t + 3, (u + 3) % U)

                        steps(pe, begin, step)
                release(s)

        def ffn_weights(l, c):
            ph = f"lf{l}"
            NF = len(FCH)
            w1 = sb(ph + "w1", [P, KD, 2 * HID], F32, c)
            w2 = sb(ph + "w2", [P, NF, D], F32, c)
            b1 = sb(ph + "b1", [P, 2, NF], F32, c)
            b2 = sb(ph + "b2", [P, D], F32, c)
            aff = sb(ph + "aff", [P, 2, KD], F32, c)

            def ahead(sp, sem):
                sp.dma_start(w1[:], io["L0_ffn_w1"][l].rearrange("(k p) n -> p k n", p=P)).then_inc(sem, 16)
                full = (NF - 1) * P
                sp.dma_start(w2[:, 0:NF - 1, :], io["L0_ffn_w2"][l, 0:full, :].rearrange("(k p) n -> p k n", p=P)).then_inc(sem, 16)
                sp.dma_start(w2[0:HID - full, NF - 1, :], io["L0_ffn_w2"][l, full:HID, :]).then_inc(sem, 16)
                sp.dma_start(b2[:], rows(io["L0_ffn_b2"][l])).then_inc(sem, 16)
                with nc.allow_non_contiguous_dma(reason="small vectors by channel"):
                    for n in range(2):
                        sp.dma_start(b1[:, n, 0:NF - 1], chan(io["L0_ffn_b1"][l, n * HID:n * HID + full])).then_inc(sem, 16)
                        sp.dma_start(b1[0:HID - full, n, NF - 1:NF],
                                     io["L0_ffn_b1"][l, n * HID + full:(n + 1) * HID].unsqueeze(1)).then_inc(sem, 16)
                    sp.dma_start(aff[:, 0, :], chan(io["L0_ffn_ln_g"][l])).then_inc(sem, 16)
                    sp.dma_start(aff[:, 1, :], chan(io["L0_ffn_ln_b"][l])).then_inc(sem, 16)
                return 160

            return (w1, w2, b1, b2, aff), ahead

        def gated_ffn(l, weights):
            ph = f"lf{l}"
            NF = len(FCH)
            HALF = D // 2
            w1, w2, b1, b2, aff = weights
            with ExitStack() as c:
                late = sb(ph + "late", [P, NT, HALF], F32, c)
                pair = sb(ph + "pair", [P, J, 2, 6], F32, c)
                z = sb(ph + "z", [P, J, D], F32, c)
                zT = sb(ph + "zT", [P, KD, GW], F32, c)
                gl = sb(ph + "gl", [P, 2, GW], F32, c)
                hT = sb(ph + "hT", [P, NF, GW], F32, c)
                xb = sb(ph + "xb", [P, J, D], F32, c)
                tps = [ps(f"{ph}t{i}", [P, GW], c) for i in range(2)]
                pa = [ps(f"{ph}a{i}", [P, GW], c) for i in range(2)]
                pg = [ps(f"{ph}g{i}", [P, GW], c) for i in range(2)]
                p3 = [ps(f"{ph}p{i}", [P, 2, D], c) for i in range(2)]
                s = signals(ph, LN + " row_zero late_in zT_turned zT_done ag_done gelu_done h_done "
                            "base_done p3_done x_done gated")

                def steps(e, first, step):
                    first(0)
                    with e.Fori(0, G - 1, 1) as g:
                        step(g, True)
                    step(G - 1, False)

                with nc.Block() as block:
                    @block.sync
                    def _(sp):
                        for lo, hi in ((0, 112), (112, 127)):
                            sp.dma_start(late[lo + 1:hi + 1, :, :], x0res[lo:hi, :, HALF:D]).then_inc(s.late_in, 16)
                        sp.wait_ge(s.row_zero, 1 + 1)
                        for b in range(B):
                            sp.dma_start(late[0:1, b * TPB + 1:(b + 1) * TPB, :],
                                         x0res[P - 1:P, b * TPB:(b + 1) * TPB - 1, HALF:D]).then_inc(s.late_in, 16)

                    @block.gpsimd
                    def _(pool):
                        pool.memset(late[0:1, :, :], 0.0).then_inc(s.row_zero, 1)
                        with pool.Fori(0, G, 1) as g:
                            wait_apart(pool, s.x_done, 1 + g * 2)
                            for j in range(J):
                                pool.tensor_tensor(xb[:, j, :], x0res[:, g * J + j, :], b2[:], ALU.add).then_inc(s.base_done, 1)

                    @block.vector
                    def _(dve):
                        def norm(g):
                            for j in range(J):
                                dve.bn_stats(pair[:, j, 0, :], x0res[:, g * J + j, 0:HALF]).then_inc(s.ln_stats, 1)
                                dve.bn_stats(pair[:, j, 1, :], late[:, g * J + j, :]).then_inc(s.ln_stats, 1)
                            wait_apart(dve, s.ln_stats, 1 + g * 2 * J + 2 * J)
                            for j in range(J):
                                dve.bn_aggr(moments[:, j, :], pair[:, j, :, :].rearrange("p a s -> p (a s)")).then_inc(s.ln_moments, 1)
                            dve.wait_ge(s.ln_std, 1 + g + 1)
                            dve.reciprocal(rstd[:, :], std[:, :]).then_inc(s.ln_rstd, 1)
                            dve.wait_ge(s.ln_rstd, 1 + g + 1)
                            dve.wait_ge(s.zT_turned, 1 + g * KD)
                            for j in range(J):
                                for a, src in ((0, x0res[:, g * J + j, 0:HALF]), (1, late[:, g * J + j, :])):
                                    ins = dve.tensor_scalar(z[:, j, a * HALF:(a + 1) * HALF], src, moments[:, j, 0:1],
                                                            rstd[:, j:j + 1], ALU.subtract, ALU.mult)
                                ins.then_inc(s.ln_out, 1)

                        def step(g, more):
                            dve.wait_ge(s.p3_done, 1 + g * J)
                            for f, (f0, n) in enumerate(FCH):
                                dve.wait_ge(s.gelu_done, 1 + g * NF + f + 1)
                                dve.scalar_tensor_tensor(out=hT[0:n, f, :], in0=pa[f % 2][0:n, :], scalar=b1[0:n, 0, f:f + 1],
                                                         in1=gl[0:n, f % 2, :], op0=ALU.add, op1=ALU.mult).then_inc(s.h_done, 1)
                            if more:
                                norm(g + 1)
                            dve.wait_ge(s.base_done, 1 + g * J + J)
                            for q in range(2):
                                dve.wait_ge(s.p3_done, 1 + g * J + 2 * q + 2)
                                dve.tensor_tensor(x0res[:, bass.ds(g * J + 2 * q, 2), :], p3[q][:], xb[:, 2 * q:2 * q + 2, :],
                                                  ALU.add).then_inc(s.x_done, 1)
                            if l == DEPTH - 1:
                                dve.wait_ge(s.x_done, 1 + g * 2 + 2)
                                for j in range(J):
                                    dve.scalar_tensor_tensor(out=xres[:, g * J + j, :], in0=x0res[:, g * J + j, :],
                                                             scalar=gate[:, 2:3], in1=xres[:, g * J + j, :],
                                                             op0=ALU.mult, op1=ALU.add).then_inc(s.gated, 1)

                        dve.wait_ge(s.late_in, 1 + 64)
                        steps(dve, norm, step)

                    @block.scalar
                    def _(act):
                        def step(g, more):
                            act.wait_ge(s.ag_done, 1 + g * NF)
                            for k in range(KD):
                                act.wait_ge(s.zT_turned, 1 + g * KD + k + 1)
                                act.activation(zT[:, k, :], tps[k][:], ACT.Identity, bias=aff[:, 1, k:k + 1],
                                               scale=aff[:, 0, k:k + 1]).then_inc(s.zT_done, 1)
                            for f, (f0, n) in enumerate(FCH):
                                act.wait_ge(s.ag_done, 1 + g * NF + f + 1)
                                act.wait_ge(s.h_done, 1 + g * NF + max(f - 1, 0))
                                act.activation(gl[0:n, f % 2, :], pg[f % 2][0:n, :], ACT.Gelu, bias=b1[0:n, 1, f:f + 1]).then_inc(s.gelu_done, 1)
                            if more:
                                ln_scalar(act, s, g + 1)

                        steps(act, lambda g: ln_scalar(act, s, g), step)

                    @block.tensor
                    def _(pe):
                        def turn(g):
                            pe.wait_ge(s.ln_out, 1 + g * J + J)
                            pe.wait_ge(s.zT_done, 1 + g * KD)
                            for k in range(KD):
                                for j in range(J):
                                    mm = pe.transpose(tps[k][:, j * P:(j + 1) * P], z[:, j, k * P:(k + 1) * P], ident[:])
                                mm.then_inc(s.zT_turned, 1)

                        def step(g, more):
                            pe.wait_ge(s.zT_done, 1 + g * KD + KD)
                            for f, (f0, n) in enumerate(FCH):
                                pe.wait_ge(s.h_done, 1 + g * NF + max(f - 1, 0))
                                for dst, off in ((pg[f % 2], HID), (pa[f % 2], 0)):
                                    for k in range(KD):
                                        mm = pe.matmul(dst[0:n, :], w1[:, k, off + f0:off + f0 + n], zT[:, k, :],
                                                       start=(k == 0), stop=(k == KD - 1))
                                mm.then_inc(s.ag_done, 1)
                            pe.wait_ge(s.h_done, 1 + g * NF + NF)
                            pe.wait_ge(s.x_done, 1 + g * 2)
                            for j in range(J):
                                if more and j == J - 1:
                                    turn(g + 1)
                                for f, (f0, n) in enumerate(FCH):
                                    mm = pe.matmul(p3[j // 2][:, j % 2, :], hT[0:n, f, j * P:(j + 1) * P], w2[0:n, f, :],
                                                   start=(f == 0), stop=(f == NF - 1))
                                mm.then_inc(s.p3_done, 1)

                        steps(pe, turn, step)
                release(s)

        for l in range(DEPTH):
            with ExitStack() as weights_stack:
                ffn, ffn_ahead = ffn_weights(l, weights_stack)
                local_attention(l, ffn_ahead)
                gated_ffn(l, ffn)


        H3 = 16
        D3 = D // H3
        attn = ExitStack()
        ores = sb("ores3", [P, NT * D], F32, attn)
        ores_flat = ores[:]
        E = io["L1_ffn_router_bias"].shape[0]
        wo = sb("r_wo", [P, KD, D], F32, attn)
        bo = sb("r_bo", [P, D], F32, attn)
        nw = sb("r_nw", [P, D], F32, attn)
        rw = sb("r_rw", [P, KD, E], F32, attn)
        rb = sb("r_rb", [P, E], F32, attn)

        def router_ahead(sp, sem):
            sp.dma_start(wo[:], io["L1_xattn_Wo"].rearrange("(k p) n -> p k n", p=P)).then_inc(sem, 16)
            sp.dma_start(bo[:], rows(io["L1_xattn_bo"])).then_inc(sem, 16)
            sp.dma_start(nw[:], rows(io["L1_ffn_norm_weight"])).then_inc(sem, 16)
            sp.dma_start(rw[:], io["router_wT"].rearrange("(k p) n -> p k n", p=P)).then_inc(sem, 16)
            sp.dma_start(rb[:], rows(io["L1_ffn_router_bias"])).then_inc(sem, 16)
            return 80

        cross_attention("x3", H3, D3, lambda t: xres[:, t, :], None, None, io["L1_xattn_Wq"], io["L1_xattn_Wk"],
                        io["L1_xattn_Wv"], (io["L1_xattn_bq"], io["L1_xattn_bk"], io["L1_xattn_bv"]), D3 ** -0.5, router_ahead)

        FE = io["L1_ffn_fc1_bias"].shape[1]
        CAP = max(1, -(-TOK // E))
        ROW = D + E
        AROW = D + 1
        assert CAP == P
        token_rows = nc.dram_tensor("token_rows", (TOK, ROW), F32).ap()
        mixed = nc.dram_tensor("mixed", (TOK, AROW), F32).ap()
        moe = ExitStack()
        logitsT = sb("logitsT", [E, TOK], F32, moe)
        idxT = sb("idxT", [P, E], U32, moe)
        RING = 4
        w1e = sb("w1e", [P, RING, KD, FE], F32, moe)
        w2e = sb("w2e", [P, RING, FE // P, D], F32, moe)
        b1e = sb("b1e", [P, E, FE // P], F32, moe)
        b2e = sb("b2e", [P, E, D], F32, moe)

        with ExitStack() as c:
            ost = sb("r_ost", [P, J, D], F32, c)
            oT = sb("r_oT", [P, KD, GW], F32, c)
            y = sb("r_y", [P, J, D], F32, c)
            h = sb("r_h", [P, J, D], F32, c)
            junk = sb("r_junk", [P, D], F32, c)
            ms = sb("r_ms", [P, J], F32, c)
            rms = sb("r_rms", [P, J], F32, c)
            rrms = sb("r_rr", [P, J], F32, c)
            row = sb("r_row", [P, J, ROW], F32, c)
            xT = sb("r_xT", [P, KD, GW], F32, c)
            lg = sb("r_lg", [P, J, E], F32, c)
            top = sb("r_top", [P, J], F32, c)
            ex = sb("r_ex", [P, J, E], F32, c)
            den = sb("r_den", [P, J], F32, c)
            rden = sb("r_rden", [P, J], F32, c)
            zero = sb("r_zero", [P, AROW], F32, c)
            tps = [ps(f"r_t{i}", [P, GW], c) for i in range(2)]
            p1 = [ps(f"r_p{i}", [P, 2, D], c) for i in range(2)]
            plg = ps("r_lgps", [P, J, E], c)
            plt = ps("r_ltps", [E, GW], c)
            s = signals("r", LN + " zeroed mixed_zero staged oT_turned oT_done p1_done y_done x_done squared "
                        "rms_done rrms_done xn_done xn_turned xT_done lg_done lg_ready top_done shifted exp_done den_done "
                        "rden_done probs_done lgT_done lgT_out rows_out")
            with nc.Block() as block:
                @block.sync
                def _(sp):
                    sp.wait_ge(s.zeroed, 1 + 1)
                    sp.dma_start(mixed.rearrange("(t p) c -> p t c", p=P),
                                 zero[:].unsqueeze(1).to_broadcast([P, NT, AROW])).then_inc(s.mixed_zero, 16)
                    with sp.Fori(0, G, 1) as g:
                        sp.wait_ge(s.probs_done, 1 + g + 1)
                        sp.dma_start(token_rows.rearrange("(t p) c -> p t c", p=P)[:, bass.ts(g, J), :], row[:]).then_inc(s.rows_out, 16)
                    sp.wait_ge(s.rows_out, 1 + 16 * G)
                    sp.wait_ge(s.mixed_zero, 1 + 16)

                @block.gpsimd
                def _(pool):
                    pool.memset(zero[:], 0.0).then_inc(s.zeroed, 1)
                    with pool.Fori(0, G, 1) as g:
                        wait_apart(pool, s.oT_turned, 1 + g * KD)
                        for j in range(J):
                            pool.tensor_copy(ost[:, j, :], ores_flat[:, bass.ts(g * J + j, D)]).then_inc(s.staged, 1)

                @block.vector
                def _(dve):
                    with dve.Fori(0, G, 1) as g:
                        for q in range(2):
                            dve.wait_ge(s.p1_done, 1 + g * J + 2 * q + 2)
                            dve.tensor_tensor(y[:, 2 * q:2 * q + 2, :], p1[q][:], bo[:].unsqueeze(1).to_broadcast([P, 2, D]),
                                              ALU.add).then_inc(s.y_done, 1)
                        dve.wait_ge(s.y_done, 1 + g * 2 + 2)
                        for j in range(J):
                            dve.scalar_tensor_tensor(out=xres[:, g * J + j, :], in0=y[:, j, :], scalar=gate[:, 1:2],
                                                     in1=xres[:, g * J + j, :], op0=ALU.mult, op1=ALU.add).then_inc(s.x_done, 1)
                        wait_apart(dve, s.x_done, 1 + g * J + J)
                        ln_vector(dve, s, g, lambda j: xres[:, g * J + j, :], lambda j: h[:, j, :])
                        dve.wait_ge(s.rms_done, 1 + g + 1)
                        dve.reciprocal(rrms[:], rms[:]).then_inc(s.rrms_done, 1)
                        dve.wait_ge(s.rrms_done, 1 + g + 1)
                        dve.wait_ge(s.rows_out, 1 + g * 16)
                        for j in range(J):
                            dve.scalar_tensor_tensor(out=row[:, j, 0:D], in0=h[:, j, :], scalar=rrms[:, j:j + 1],
                                                     in1=nw[:], op0=ALU.mult, op1=ALU.mult).then_inc(s.xn_done, 1)
                        dve.wait_ge(s.lg_done, 1 + g + 1)
                        dve.wait_ge(s.lgT_done, 1 + g)
                        dve.tensor_tensor(lg[:], plg[:], rb[:].unsqueeze(1).to_broadcast([P, J, E]), ALU.add).then_inc(s.lg_ready, 1)
                        dve.wait_ge(s.lg_ready, 1 + g + 1)
                        dve.tensor_reduce(top[:], lg[:], X, ALU.max, negate=True).then_inc(s.top_done, 1)
                        dve.wait_ge(s.top_done, 1 + g + 1)
                        dve.tensor_tensor(ex[:], lg[:], top[:].unsqueeze(2).to_broadcast([P, J, E]), ALU.add).then_inc(s.shifted, 1)
                        dve.wait_ge(s.exp_done, 1 + g + 1)
                        dve.tensor_reduce(den[:], ex[:], X, ALU.add).then_inc(s.den_done, 1)
                        dve.wait_ge(s.den_done, 1 + g + 1)
                        dve.reciprocal(rden[:], den[:]).then_inc(s.rden_done, 1)
                        dve.wait_ge(s.rden_done, 1 + g + 1)
                        dve.tensor_tensor(row[:, :, D:ROW], ex[:], rden[:].unsqueeze(2).to_broadcast([P, J, E]), ALU.mult).then_inc(s.probs_done, 1)

                @block.scalar
                def _(act):
                    with act.Fori(0, G, 1) as g:
                        act.wait_ge(s.p1_done, 1 + g * J)
                        for k in range(KD):
                            act.wait_ge(s.oT_turned, 1 + g * KD + k + 1)
                            act.copy(oT[:, k, :], tps[k][:]).then_inc(s.oT_done, 1)
                        ln_scalar(act, s, g)
                        for j in range(J):
                            act.wait_ge(s.ln_out, 1 + g * J + j + 1)
                            if j > 0:
                                act.wait_ge(s.squared, 1 + g * J + j)
                            act.activation(junk[:], h[:, j, :], ACT.Square, accum_out=ms[:, j:j + 1]).then_inc(s.squared, 1)
                        act.wait_ge(s.squared, 1 + g * J + J)
                        act.activation(rms[:], ms[:], ACT.Sqrt, bias=eps[:, 0:1], scale=1.0 / D).then_inc(s.rms_done, 1)
                        act.wait_ge(s.lg_done, 1 + g)
                        for k in range(KD):
                            act.wait_ge(s.xn_turned, 1 + g * KD + k + 1)
                            act.copy(xT[:, k, :], tps[k][:]).then_inc(s.xT_done, 1)
                        act.wait_ge(s.shifted, 1 + g + 1)
                        act.activation(ex[:], ex[:], ACT.Exp).then_inc(s.exp_done, 1)
                        act.wait_ge(s.lgT_done, 1 + g + 1)
                        act.copy(logitsT[:, bass.ts(g, GW)], plt[:]).then_inc(s.lgT_out, 1)

                @block.tensor
                def _(pe):
                    with pe.Fori(0, G, 1) as g:
                        pe.wait_ge(s.staged, 1 + g * J + J)
                        pe.wait_ge(s.xT_done, 1 + g * KD)
                        for k in range(KD):
                            for j in range(J):
                                mm = pe.transpose(tps[k][:, j * P:(j + 1) * P], ost[:, j, k * P:(k + 1) * P], ident[:])
                            mm.then_inc(s.oT_turned, 1)
                        pe.wait_ge(s.oT_done, 1 + g * KD + KD)
                        pe.wait_ge(s.y_done, 1 + g * 2)
                        for j in range(J):
                            for k in range(KD):
                                mm = pe.matmul(p1[j // 2][:, j % 2, :], oT[:, k, j * P:(j + 1) * P], wo[:, k, :],
                                               start=(k == 0), stop=(k == KD - 1))
                            mm.then_inc(s.p1_done, 1)
                        pe.wait_ge(s.xn_done, 1 + g * J + J)
                        for k in range(KD):
                            for j in range(J):
                                mm = pe.transpose(tps[k][:, j * P:(j + 1) * P], row[:, j, k * P:(k + 1) * P], ident[:])
                            mm.then_inc(s.xn_turned, 1)
                        pe.wait_ge(s.xT_done, 1 + g * KD + KD)
                        pe.wait_ge(s.lg_ready, 1 + g)
                        for j in range(J):
                            for k in range(KD):
                                mm = pe.matmul(plg[:, j, :], xT[:, k, j * P:(j + 1) * P], rw[:, k, :],
                                               start=(k == 0), stop=(k == KD - 1))
                        mm.then_inc(s.lg_done, 1)
                        pe.wait_ge(s.lg_ready, 1 + g + 1)
                        pe.wait_ge(s.lgT_out, 1 + g)
                        for j in range(J):
                            mm = pe.transpose(plt[:, j * P:(j + 1) * P], lg[:, j, :], ident[:])
                        mm.then_inc(s.lgT_done, 1)
            release(s)

        with ExitStack() as c:
            best = sb("best", [E, 8], F32, c)
            where8 = sb("where8", [E, 8], U32, c)
            chosen = sb("chosen", [E, CAP], F32, c)
            pidx = ps("pidx", [P, E], c)
            s = signals("top", "next_in best_done found kept removed turned idx_done")
            with nc.Block() as block:
                @block.sync
                def _(sp):
                    with nc.allow_non_contiguous_dma(reason="biases by channel"):
                        sp.dma_start(b1e[:], io["L1_ffn_fc1_bias"].rearrange("e (k p) -> p e k", p=P)).then_inc(s.next_in, 16)
                    sp.dma_start(b2e[:].rearrange("p e c -> p (e c)"),
                                 io["L1_ffn_fc2_bias"].rearrange("e c -> (e c)").unsqueeze(0).to_broadcast([P, E * D])).then_inc(s.next_in, 16)
                    for r in range(RING):
                        sp.dma_start(w1e[:, r, :, :], io["fc1_T"][r].rearrange("(k p) f -> p k f", p=P)).then_inc(s.next_in, 16)
                        sp.dma_start(w2e[:, r, :, :], io["fc2_T"][r].rearrange("(k p) c -> p k c", p=P)).then_inc(s.next_in, 16)
                    sp.wait_ge(s.next_in, 1 + 32 + 32 * RING)

                @block.vector
                def _(dve):
                    with dve.Fori(0, CAP // 8, 1) as r:
                        wait_apart(dve, s.removed, 1 + r)
                        dve.max(best[:], logitsT[:]).then_inc(s.best_done, 1)
                        wait_apart(dve, s.best_done, 1 + r + 1)
                        wait_apart(dve, s.kept, 1 + r)
                        dve.max_index(where8[:], best[:], logitsT[:]).then_inc(s.found, 1)
                        wait_apart(dve, s.found, 1 + r + 1)
                        dve.match_replace(logitsT[:], best[:], logitsT[:], -3.4028235e38).then_inc(s.removed, 1)
                        dve.tensor_copy(chosen[:, bass.ts(r, 8)], where8[:]).then_inc(s.kept, 1)
                    dve.wait_ge(s.turned, 1 + 1)
                    dve.tensor_copy(idxT[:], pidx[:]).then_inc(s.idx_done, 1)

                @block.tensor
                def _(pe):
                    pe.wait_ge(s.kept, 1 + CAP // 8)
                    pe.transpose(pidx[:], chosen[:], ident[0:E, 0:E]).then_inc(s.turned, 1)
            release(s)

        with ExitStack() as c:
            FC = FE // P
            idx = sb("idx", [P, RING, 1], U32, c)
            xe = sb("xe", [P, RING, ROW], F32, c)
            xeT = sb("xeT", [P, 2, D], F32, c)
            hT = sb("hTe", [P, 2, FC, P], F32, c)
            gated = sb("gated", [P, 2, AROW], F32, c)
            bx = [ps(f"bx{i}", [P, D], c) for i in range(2)]
            bh = [ps(f"bh{i}", [P, FC, P], c) for i in range(2)]
            by = [ps(f"by{i}", [P, D], c) for i in range(2)]
            s = signals("e", "w_in0 w_in1 w_in2 w_in3 idx_ready @x_in0 @x_in1 @x_in2 @x_in3 turned xT_done fc1_done gelu_done "
                        "fc2_done gate_done biased weighted @added")
            w_in = (s.w_in0, s.w_in1, s.w_in2, s.w_in3)
            x_in = (s.x_in0, s.x_in1, s.x_in2, s.x_in3)
            with nc.Block() as block:
                @block.sync
                def _(sp):
                    def load(e, r):
                        sp.dma_start(w1e[:, r, :, :], io["fc1_T"].rearrange("e (k p) f -> e p k f", p=P)[e]).then_inc(w_in[r], 16)
                        sp.dma_start(w2e[:, r, :, :], io["fc2_T"].rearrange("e (k p) c -> e p k c", p=P)[e]).then_inc(w_in[r], 16)

                    with sp.Fori(1, E // RING, 1) as it:
                        for r in range(RING):
                            sp.wait_ge(s.fc2_done, 1 + it * RING - RING + r + 1)
                            load(it * RING + r, r)

                def steps(eng, step):
                    for r in range(RING):
                        step(r, r, RING)
                    with eng.Fori(1, E // RING - 1, 1) as it:
                        for r in range(RING):
                            step(it * RING + r, r, RING)
                    for r in range(RING):
                        step(E - RING + r, r, RING - 1 - r)

                @block.gpsimd
                def _(pool):
                    def fetch(e, r):
                        if not (isinstance(e, int) and e < RING):
                            wait_apart(pool, s.weighted, 1 + e - RING + 1)
                        wait_apart(pool, s.idx_ready, 1 + e + 1)
                        pool.indirect_dma_start(out=xe[:, r, :], out_offset=None, in_=token_rows,
                                                in_offset=bass.IndirectOffsetOnAxis(ap=idx[:, r, :], axis=0)).then_inc(x_in[r], 16)

                    def step(e, r, more):
                        if more >= 2:
                            fetch(e + 2, (r + 2) % RING)
                        wait_apart(pool, s.weighted, 1 + e + 1)
                        if not (isinstance(e, int) and e == 0):
                            wait_apart(pool, s.added, e * 16)
                        pool.indirect_dma_start(out=mixed, out_offset=bass.IndirectOffsetOnAxis(ap=idx[:, r, :], axis=0),
                                                in_=gated[:, r % 2, :], in_offset=None, compute_op=ALU.add).then_inc(s.added, 16)

                    fetch(0, 0)
                    fetch(1, 1)
                    steps(pool, step)
                    pool.wait_ge(s.added, 16 * E)

                @block.vector
                def _(dve):
                    def index(e, r):
                        if not (isinstance(e, int) and e < RING):
                            dve.wait_ge(s.added, (e - RING + 1) * 16)
                        dve.tensor_copy(idx[:, r, :], idxT[:, bass.ds(e, 1)]).then_inc(s.idx_ready, 1)

                    def tokens(e, r):
                        dve.wait_ge(s.turned, 1 + e + 1)
                        if not (isinstance(e, int) and e < 2):
                            dve.wait_ge(s.fc1_done, 1 + e - 1)
                        dve.tensor_copy(xeT[:, r % 2, :], bx[r % 2][:]).then_inc(s.xT_done, 1)

                    def step(e, r, more):
                        if more >= 3:
                            index(e + 3, (r + 3) % RING)
                        if more >= 2:
                            tokens(e + 2, (r + 2) % RING)
                        if not (isinstance(e, int) and e < 2):
                            dve.wait_ge(s.added, e * 16 - 16)
                        dve.wait_ge(s.fc2_done, 1 + e + 1)
                        dve.tensor_copy(gated[:, r % 2, D:AROW], xe[:, r, bass.ds(e + D, 1)]).then_inc(s.gate_done, 1)
                        dve.tensor_tensor(gated[:, r % 2, 0:D], by[r % 2][:], b2e[:, e, :], ALU.add).then_inc(s.biased, 1)
                        dve.wait_ge(s.biased, 1 + e + 1)
                        dve.tensor_scalar(gated[:, r % 2, 0:D], gated[:, r % 2, 0:D], gated[:, r % 2, D:AROW], None,
                                          ALU.mult).then_inc(s.weighted, 1)

                    for e in range(3):
                        index(e, e)
                    tokens(0, 0)
                    tokens(1, 1)
                    steps(dve, step)

                @block.scalar
                def _(act):
                    def gelus(e, r):
                        act.wait_ge(s.fc1_done, 1 + e + 1)
                        if not (isinstance(e, int) and e < 2):
                            act.wait_ge(s.fc2_done, 1 + e - 1)
                        for f in range(FC):
                            ins = act.activation(hT[:, r % 2, f, :], bh[r % 2][:, f, :], ACT.Gelu, bias=b1e[:, e, f:f + 1])
                        ins.then_inc(s.gelu_done, 1)

                    def step(e, r, more):
                        if more >= 1:
                            gelus(e + 1, (r + 1) % RING)

                    gelus(0, 0)
                    steps(act, step)

                @block.tensor
                def _(pe):
                    def turn(e, r, it):
                        pe.wait_ge(x_in[r], it * 16 + 16)
                        if not (isinstance(e, int) and e < 2):
                            pe.wait_ge(s.xT_done, 1 + e - 1)
                        for k in range(KD):
                            mm = pe.transpose(bx[r % 2][:, k * P:(k + 1) * P], xe[:, r, k * P:(k + 1) * P], ident[:])
                        mm.then_inc(s.turned, 1)

                    def fc1(e, r, it):
                        pe.wait_ge(w_in[r], 1 + it * 32)
                        pe.wait_ge(s.xT_done, 1 + e + 1)
                        if not (isinstance(e, int) and e < 2):
                            pe.wait_ge(s.gelu_done, 1 + e - 1)
                        for f in range(FC):
                            for k in range(KD):
                                mm = pe.matmul(bh[r % 2][:, f, :], w1e[:, r, k, f * P:(f + 1) * P], xeT[:, r % 2, k * P:(k + 1) * P],
                                               start=(k == 0), stop=(k == KD - 1))
                        mm.then_inc(s.fc1_done, 1)

                    def fc2(e, r):
                        pe.wait_ge(s.gelu_done, 1 + e + 1)
                        if not (isinstance(e, int) and e < 2):
                            pe.wait_ge(s.weighted, 1 + e - 1)
                        for f in range(FC):
                            mm = pe.matmul(by[r % 2][:], hT[:, r % 2, f, :], w2e[:, r, f, :], start=(f == 0), stop=(f == FC - 1))
                        mm.then_inc(s.fc2_done, 1)

                    def step(it, r, more):
                        e = it * RING + r
                        if more >= 1:
                            fc1(e + 1, (r + 1) % RING, it + (r + 1) // RING)
                        if more >= 2:
                            turn(e + 2, (r + 2) % RING, it + (r + 2) // RING)
                        fc2(e, r)

                    turn(0, 0, 0)
                    fc1(0, 0, 0)
                    turn(1, 1, 0)
                    for r in range(RING):
                        step(0, r, RING)
                    with pe.Fori(1, E // RING - 1, 1) as it:
                        for r in range(RING):
                            step(it, r, RING)
                    for r in range(RING):
                        step(E // RING - 1, r, RING - 1 - r)
            release(s)

        with ExitStack() as c:
            acc = sb("acc", [P, NT, AROW], F32, c)
            none = sb("none", [P, NT], F32, c)
            coef = sb("coef", [P, NT], F32, c)
            fin = sb("fin", [P, NT, D], F32, c)
            s = signals("f", "in0 in1 in2 in3 none_done total_done inverse_done coef_done x_done x_out")
            got = (s.in0, s.in1, s.in2, s.in3)
            with nc.Block() as block:
                @block.sync
                def _(sp):
                    for g in range(G):
                        sp.dma_start(acc[:, g * J:(g + 1) * J, :],
                                     mixed.rearrange("(t p) c -> p t c", p=P)[:, g * J:(g + 1) * J, :]).then_inc(got[g], 16)
                    for g in range(G):
                        sp.wait_ge(s.x_done, 1 + g * J + J)
                        sp.dma_start(out.rearrange("b (t p) c -> p (b t) c", p=P)[:, g * J:(g + 1) * J, :],
                                     fin[:, g * J:(g + 1) * J, :]).then_inc(s.x_out, 16)
                    sp.wait_ge(s.x_out, 1 + 16 * G)

                @block.vector
                def _(dve):
                    for g in range(G):
                        t = slice(g * J, (g + 1) * J)
                        total = acc[:, t, D]
                        dve.wait_ge(got[g], 1 + 16)
                        dve.tensor_scalar(none[:, t], total, 0.0, None, ALU.is_le).then_inc(s.none_done, 1)
                        dve.wait_ge(s.none_done, 1 + g + 1)
                        dve.tensor_tensor(none[:, t], none[:, t], total, ALU.add).then_inc(s.total_done, 1)
                        dve.wait_ge(s.total_done, 1 + g + 1)
                        dve.reciprocal(coef[:, t], none[:, t]).then_inc(s.inverse_done, 1)
                        dve.wait_ge(s.inverse_done, 1 + g + 1)
                        dve.tensor_scalar(coef[:, t], coef[:, t], gate[:, 3:4], None, ALU.mult).then_inc(s.coef_done, 1)
                        dve.wait_ge(s.coef_done, 1 + g + 1)
                        for j in range(J):
                            dve.scalar_tensor_tensor(out=fin[:, g * J + j, :], in0=acc[:, g * J + j, 0:D],
                                                     scalar=coef[:, g * J + j:g * J + j + 1], in1=xres[:, g * J + j, :],
                                                     op0=ALU.mult, op1=ALU.add).then_inc(s.x_done, 1)
            release(s)
        moe.close()
        attn.close()


def shape_constants(tokens=1024, dim=64, window=128):
    import numpy as np

    half = np.arange(0, dim, 2, dtype=np.float32)
    inv_freq = (1.0 / np.float32(10000.0) ** (half / np.float32(dim))).astype(np.float32)
    t = np.arange(tokens, dtype=np.float32)
    freqs = t[:, None] * inv_freq[None, :]
    base = ((half + np.float32(0.4 * dim)) / np.float32(1.4 * dim)).astype(np.float32)
    power = (t - tokens // 2) / np.float32(window // 2)
    scale = (base[None, :] ** power[:, None]).astype(np.float32)
    cos, sin = np.cos(freqs), np.sin(freqs)
    qk_scale = np.float32(8.0)
    two = lambda a, b: np.concatenate([a, b], axis=-1)
    c = np.stack([two(cos * scale, cos * scale) * qk_scale, two(cos / scale, cos / scale)], axis=1)
    s = np.stack([two(-sin * scale, sin * scale) * qk_scale, two(-sin / scale, sin / scale)], axis=1)
    return {"rotary_cos": c.astype(np.float32), "rotary_sin": s.astype(np.float32)}


def kernel(**inputs):
    import numpy as np
    import concourse.bacc as bacc
    from concourse import mybir
    from concourse.bass_utils import run_bass_kernel_spmd as run

    given = {name: np.ascontiguousarray(value) for name, value in inputs.items()}
    for block in ("a1", "a2"):
        for w in ("wq", "wk", "wv"):
            a = given[f"L0_xattn_{block}_{w}"]
            given[f"{block}_{w}_flat"] = np.ascontiguousarray(a.transpose(1, 0, 2).reshape(a.shape[1], -1))
    given["router_wT"] = np.ascontiguousarray(given["L1_ffn_router_weight"].T)
    given["fc1_T"] = np.ascontiguousarray(given.pop("L1_ffn_fc1_weight").transpose(0, 2, 1))
    given["fc2_T"] = np.ascontiguousarray(given.pop("L1_ffn_fc2_weight").transpose(0, 2, 1))
    given.update(shape_constants())
    nc = bacc.Bacc("TRN2", target_bir_lowering=False, num_devices=1)
    arrays, io = {}, {}
    for name, a in given.items():
        arrays["in_" + name] = a
        io[name] = nc.dram_tensor("in_" + name, a.shape, mybir.dt.from_np(a.dtype), kind="ExternalInput").ap()
    out = nc.dram_tensor("x_out", inputs["x"].shape, mybir.dt.float32, kind="ExternalOutput").ap()
    build(nc, io, out)
    return run(nc, [arrays], core_ids=[0]).results[0]["x_out"]
```
